# Optimizing a Trainium2 kernel written in Bass

```python
import numpy as np
import jax
import jax.numpy as jnp

def _softmax(x, axis=-1):
    return jax.nn.softmax(x, axis=axis)

def _gelu(x):
    return jax.nn.gelu(x, approximate=True)

def _silu(x):
    return jax.nn.silu(x)

def _sigmoid(x):
    return jax.nn.sigmoid(x)

def _layernorm(x, axis=-1, eps=1e-05):
    m = jnp.mean(x, axis=axis, keepdims=True)
    v = jnp.var(x, axis=axis, keepdims=True)
    return (x - m) / jnp.sqrt(v + eps)

def _scatter_add(tgt, idx, src, axis=0):
    return tgt.at[idx].add(src)

def _segment_sum(src, seg, n):
    return jax.ops.segment_sum(src, seg, n)
kernel_name = 'mk_decoder_postln_d1_seqx_r4_731212'

def setup_inputs(seed: int=0):
    np.random.seed(seed)
    _w = jnp.asarray

    def _rec_inputs():
        import jax
        import jax.numpy as jnp
        _rk = jax.random.key(seed)
        x = -0.0002928 + 1 * jax.random.normal(jax.random.fold_in(_rk, 1), (32, 112, 256), jnp.float32)
        _lenS = 112 - jax.random.randint(jax.random.fold_in(_rk, 7), (32,), 0, max(1, 112 // 4) + 1, jnp.int32)
        _lenS2 = 375 - jax.random.randint(jax.random.fold_in(_rk, 8), (32,), 0, max(1, 375 // 4) + 1, jnp.int32)
        _ctx_1024P = jax.random.normal(jax.random.fold_in(_rk, 11), (32, 16, 256), jnp.float32)
        _ctx_1024c = jax.random.dirichlet(jax.random.fold_in(_rk, 511), 0.3 * jnp.ones((16,), jnp.float32), (32, 375))
        _ctx_1024t = jnp.einsum('bsk,bkd->bsd', _ctx_1024c, _ctx_1024P)
        _ctx_1024t = _ctx_1024t * jax.lax.rsqrt(jnp.mean(jnp.square(_ctx_1024t)) + 1e-12) * 0.953939
        ctx_1024 = -1.39393e-06 + 0.999914 * (_ctx_1024t + 0.3 * jax.random.normal(jax.random.fold_in(_rk, 611), (32, 375, 256), jnp.float32))
        _validS = jnp.arange(112)[None, :] < _lenS[:, None]
        _validS2 = jnp.arange(375)[None, :] < _lenS2[:, None]
        _causal = jnp.tril(jnp.ones((112, 112), dtype=bool))
        mask_BxS2_bf1 = jnp.ones((32, 375), dtype=bool)
        return (x, ctx_1024, mask_BxS2_bf1)
    x, ctx_1024, mask_BxS2_bf1 = _rec_inputs()

    def _L0_attn_setup():
        import jax, jax.numpy as jnp
        import numpy as np
        B, S, D, H, DH, FF = (2, 1024, 256, 16, 64, 1024)

        def _ln(x, g, b):
            m = x.mean(-1, keepdims=True)
            v = ((x - m) ** 2).mean(-1, keepdims=True)
            return (x - m) * jax.lax.rsqrt(v + 1e-05) * g + b

        def _phi(x, proj):
            return jax.nn.elu(x @ proj) + 1.0
        key = jax.random.key(seed)
        ks = jax.random.split(key, 10)
        s = 0.02
        return {'x': jax.random.normal(ks[0], (B, S, D), jnp.float32), 'wq': jax.random.normal(ks[1], (D, H * DH), jnp.float32) * s, 'wk': jax.random.normal(ks[2], (D, H * DH), jnp.float32) * s, 'wv': jax.random.normal(ks[3], (D, H * DH), jnp.float32) * s, 'wo': jax.random.normal(ks[4], (H * DH, D), jnp.float32) * s, 'proj': jax.random.normal(ks[5], (DH, DH), jnp.float32) / np.sqrt(DH).astype(np.float32), 'w1': jax.random.normal(ks[6], (D, FF), jnp.float32) * s, 'b1': jnp.zeros((FF,), jnp.float32), 'w2': jax.random.normal(ks[7], (FF, D), jnp.float32) * s, 'b2': jnp.zeros((D,), jnp.float32), 'g1': jnp.ones((D,), jnp.float32), 'beta1': jnp.zeros((D,), jnp.float32), 'g2': jnp.ones((D,), jnp.float32), 'beta2': jnp.zeros((D,), jnp.float32)}
    _L0_attn_all = _L0_attn_setup()
    _L0_attn_in = {k: v for k, v in _L0_attn_all.items() if k in ('wq', 'wk', 'wv', 'wo', 'proj', 'w1', 'b1', 'w2', 'b2', 'g1', 'beta1', 'g2', 'beta2')}
    del _L0_attn_all

    def _L0_xattn_setup():
        import jax, jax.numpy as jnp
        import numpy as np
        DIM = 256
        HEADS = 16
        DIM_HEAD = 64
        INNER = HEADS * DIM_HEAD
        EPS = 1e-05

        def layer_norm(x, w, b):
            mu = jnp.mean(x, axis=-1, keepdims=True)
            var = jnp.mean(jnp.square(x - mu), axis=-1, keepdims=True)
            return (x - mu) * jax.lax.rsqrt(var + EPS) * w + b
        key = jax.random.key(seed)
        ks = jax.random.split(key, 6)
        b, n, m = (2, 512, 512)
        x = jax.random.normal(ks[0], (b, n, DIM), dtype=jnp.float32)
        context = jax.random.normal(ks[1], (b, m, DIM), dtype=jnp.float32)
        context_mask = jnp.ones((b, m), dtype=bool)
        s = 0.02
        Wq = jax.random.normal(ks[2], (DIM, INNER), dtype=jnp.float32) * s
        Wkv = jax.random.normal(ks[3], (DIM, 2 * INNER), dtype=jnp.float32) * s
        Wo = jax.random.normal(ks[4], (INNER, DIM), dtype=jnp.float32) * s
        norm_w = jnp.ones((DIM,), dtype=jnp.float32)
        norm_b = jnp.zeros((DIM,), dtype=jnp.float32)
        ctx_norm_w = jnp.ones((DIM,), dtype=jnp.float32)
        ctx_norm_b = jnp.zeros((DIM,), dtype=jnp.float32)
        return {'x': x, 'context': context, 'norm_w': norm_w, 'norm_b': norm_b, 'ctx_norm_w': ctx_norm_w, 'ctx_norm_b': ctx_norm_b, 'Wq': Wq, 'Wkv': Wkv, 'Wo': Wo, 'context_mask': context_mask}
    _L0_xattn_all = _L0_xattn_setup()
    _L0_xattn_in = {k: v for k, v in _L0_xattn_all.items() if k in ('norm_w', 'norm_b', 'ctx_norm_w', 'ctx_norm_b', 'Wq', 'Wkv', 'Wo')}
    del _L0_xattn_all

    def _L0_ffn_setup():
        import jax, jax.numpy as jnp
        import numpy as np
        E = 8
        K = 2
        CAPACITY_FACTOR = 1.25
        key = jax.random.key(seed)
        ks = jax.random.split(key, 4)
        B, T, C, H = (8, 512, 256, 1024)
        x = jax.random.normal(ks[0], (B, T, C), jnp.float32)
        Wr = jax.random.normal(ks[1], (C, E), jnp.float32) * 0.02
        br = jnp.zeros((E,), jnp.float32)
        W1 = jax.random.normal(ks[2], (E, C, H), jnp.float32) * 0.02
        b1 = jnp.zeros((E, H), jnp.float32)
        W2 = jax.random.normal(ks[3], (E, H, C), jnp.float32) * 0.02
        b2 = jnp.zeros((E, C), jnp.float32)
        return {'x': x, 'Wr': Wr, 'br': br, 'W1': W1, 'b1': b1, 'W2': W2, 'b2': b2}
    _L0_ffn_all = _L0_ffn_setup()
    _L0_ffn_in = {k: v for k, v in _L0_ffn_all.items() if k in ('Wr', 'br', 'W1', 'b1', 'W2', 'b2')}
    del _L0_ffn_all
    return {'x': x, 'ctx_1024': ctx_1024, 'mask_BxS2_bf1': mask_BxS2_bf1, 'L0_attn_wq': _L0_attn_in['wq'], 'L0_attn_wk': _L0_attn_in['wk'], 'L0_attn_wv': _L0_attn_in['wv'], 'L0_attn_wo': _L0_attn_in['wo'], 'L0_attn_proj': _L0_attn_in['proj'], 'L0_attn_w1': _L0_attn_in['w1'], 'L0_attn_b1': _L0_attn_in['b1'], 'L0_attn_w2': _L0_attn_in['w2'], 'L0_attn_b2': _L0_attn_in['b2'], 'L0_attn_g1': _L0_attn_in['g1'], 'L0_attn_beta1': _L0_attn_in['beta1'], 'L0_attn_g2': _L0_attn_in['g2'], 'L0_attn_beta2': _L0_attn_in['beta2'], 'L0_xattn_norm_w': _L0_xattn_in['norm_w'], 'L0_xattn_norm_b': _L0_xattn_in['norm_b'], 'L0_xattn_ctx_norm_w': _L0_xattn_in['ctx_norm_w'], 'L0_xattn_ctx_norm_b': _L0_xattn_in['ctx_norm_b'], 'L0_xattn_Wq': _L0_xattn_in['Wq'], 'L0_xattn_Wkv': _L0_xattn_in['Wkv'], 'L0_xattn_Wo': _L0_xattn_in['Wo'], 'L0_ffn_Wr': _L0_ffn_in['Wr'], 'L0_ffn_br': _L0_ffn_in['br'], 'L0_ffn_W1': _L0_ffn_in['W1'], 'L0_ffn_b1': _L0_ffn_in['b1'], 'L0_ffn_W2': _L0_ffn_in['W2'], 'L0_ffn_b2': _L0_ffn_in['b2']}

def reference(x, ctx_1024, mask_BxS2_bf1, L0_attn_wq, L0_attn_wk, L0_attn_wv, L0_attn_wo, L0_attn_proj, L0_attn_w1, L0_attn_b1, L0_attn_w2, L0_attn_b2, L0_attn_g1, L0_attn_beta1, L0_attn_g2, L0_attn_beta2, L0_xattn_norm_w, L0_xattn_norm_b, L0_xattn_ctx_norm_w, L0_xattn_ctx_norm_b, L0_xattn_Wq, L0_xattn_Wkv, L0_xattn_Wo, L0_ffn_Wr, L0_ffn_br, L0_ffn_W1, L0_ffn_b1, L0_ffn_W2, L0_ffn_b2):
    import jax
    import jax.numpy as jnp

    def _L0_attn_ref(x, wq, wk, wv, wo, proj, w1, b1, w2, b2, g1, beta1, g2, beta2):
        import jax, jax.numpy as jnp
        import numpy as np
        B, S, D, H, DH, FF = (2, 1024, 256, 16, 64, 1024)

        def _ln(x, g, b):
            m = x.mean(-1, keepdims=True)
            v = ((x - m) ** 2).mean(-1, keepdims=True)
            return (x - m) * jax.lax.rsqrt(v + 1e-05) * g + b

        def _phi(x, proj):
            return jax.nn.elu(x @ proj) + 1.0
        b, s, d = x.shape
        h = _ln(x, g1, beta1)
        q = _phi((h @ wq).reshape(b, s, H, DH), proj)
        k = _phi((h @ wk).reshape(b, s, H, DH), proj)
        v = (h @ wv).reshape(b, s, H, DH)
        qs = jnp.moveaxis(q, 1, 0)
        ks_ = jnp.moveaxis(k, 1, 0)
        vs = jnp.moveaxis(v, 1, 0)

        def step(carry, qkv_t):
            kv, ksum = carry
            q_t, k_t, v_t = qkv_t
            kv = kv + k_t[..., :, None] * v_t[..., None, :]
            ksum = ksum + k_t
            num = jnp.einsum('bhd,bhde->bhe', q_t, kv)
            den = jnp.einsum('bhd,bhd->bh', q_t, ksum) + 1e-06
            return ((kv, ksum), num / den[..., None])
        kv0 = jnp.zeros((b, H, DH, DH), x.dtype)
        ks0 = jnp.zeros((b, H, DH), x.dtype)
        _, outs = jax.lax.scan(step, (kv0, ks0), (qs, ks_, vs))
        attn = jnp.moveaxis(outs, 0, 1).reshape(b, s, H * DH) @ wo
        x = x + attn
        h2 = _ln(x, g2, beta2)
        x = x + (jax.nn.gelu(h2 @ w1 + b1, approximate=False) @ w2 + b2)
        return x

    def _L0_xattn_ref(x, context, norm_w, norm_b, ctx_norm_w, ctx_norm_b, Wq, Wkv, Wo, context_mask):
        import jax, jax.numpy as jnp
        import numpy as np
        DIM = 256
        HEADS = 16
        DIM_HEAD = 64
        INNER = HEADS * DIM_HEAD
        EPS = 1e-05

        def layer_norm(x, w, b):
            mu = jnp.mean(x, axis=-1, keepdims=True)
            var = jnp.mean(jnp.square(x - mu), axis=-1, keepdims=True)
            return (x - mu) * jax.lax.rsqrt(var + EPS) * w + b
        scale = DIM_HEAD ** (-0.5)
        xn = layer_norm(x, norm_w, norm_b)
        cn = layer_norm(context, ctx_norm_w, ctx_norm_b)
        b, n, _ = xn.shape
        m = cn.shape[1]
        q = (xn @ Wq).reshape(b, n, HEADS, DIM_HEAD).transpose(0, 2, 1, 3)
        kv = cn @ Wkv
        k = kv[..., :INNER].reshape(b, m, HEADS, DIM_HEAD).transpose(0, 2, 1, 3)
        v = kv[..., INNER:].reshape(b, m, HEADS, DIM_HEAD).transpose(0, 2, 1, 3)
        sim = jnp.einsum('bhid,bhjd->bhij', q * scale, k)
        neg = -jnp.finfo(sim.dtype).max
        sim = jnp.where(context_mask[:, None, None, :], sim, neg)
        attn = jax.nn.softmax(sim, axis=-1)
        out = jnp.einsum('bhij,bhjd->bhid', attn, v)
        out = out.transpose(0, 2, 1, 3).reshape(b, n, INNER)
        return out @ Wo

    def _L0_ffn_ref(x, Wr, br, W1, b1, W2, b2):
        import jax, jax.numpy as jnp
        import numpy as np
        E = 8
        K = 2
        CAPACITY_FACTOR = 1.25
        B, T, C = x.shape
        cap = max(1, int(T / E * CAPACITY_FACTOR))
        probs = jax.nn.softmax(x @ Wr + br, axis=-1)
        topk_p, topk_e = jax.lax.top_k(probs, K)
        e_flat = topk_e.reshape(B, T * K)
        p_flat = topk_p.reshape(B, T * K)
        oh = jax.nn.one_hot(e_flat, E, dtype=jnp.int32)
        pos_all = jnp.cumsum(oh, axis=1) - oh
        pos = jnp.take_along_axis(pos_all, e_flat[:, :, None], axis=2)[:, :, 0]
        keep = pos < cap
        b_idx = jnp.arange(B)[:, None]
        flat_idx = (e_flat * B + b_idx) * cap + jnp.minimum(pos, cap - 1)
        x_rep = jnp.broadcast_to(x[:, :, None, :], (B, T, K, C)).reshape(B, T * K, C)
        buf = jnp.zeros((E * B * cap, C), x.dtype).at[flat_idx.reshape(-1)].add((x_rep * keep[:, :, None].astype(x.dtype)).reshape(-1, C))
        buf = buf.reshape(E, B * cap, C)
        h = jax.nn.relu(jnp.einsum('enc,ech->enh', buf, W1) + b1[:, None, :])
        y = jnp.einsum('enh,ehc->enc', h, W2) + b2[:, None, :]
        y_tok = y.reshape(E * B * cap, C)[flat_idx.reshape(-1)].reshape(B, T * K, C)
        y_tok = y_tok * (p_flat * keep.astype(x.dtype))[:, :, None]
        return y_tok.reshape(B, T, K, C).sum(axis=2)
    x = _layernorm(x + _L0_attn_ref(x, L0_attn_wq, L0_attn_wk, L0_attn_wv, L0_attn_wo, L0_attn_proj, L0_attn_w1, L0_attn_b1, L0_attn_w2, L0_attn_b2, L0_attn_g1, L0_attn_beta1, L0_attn_g2, L0_attn_beta2), axis=-1)
    x = _layernorm(x + _L0_xattn_ref(x, ctx_1024, L0_xattn_norm_w, L0_xattn_norm_b, L0_xattn_ctx_norm_w, L0_xattn_ctx_norm_b, L0_xattn_Wq, L0_xattn_Wkv, L0_xattn_Wo, mask_BxS2_bf1), axis=-1)
    x = _layernorm(x + _L0_ffn_ref(x, L0_ffn_Wr, L0_ffn_br, L0_ffn_W1, L0_ffn_b1, L0_ffn_W2, L0_ffn_b2), axis=-1)
    return x

_drawn_inputs = setup_inputs


def setup_inputs(seed=0):
    import zlib

    import numpy as np

    out = dict(_drawn_inputs(seed))
    spreads = {'L0_attn_b1': (0.0, 0.428),
     'L0_attn_b2': (0.0, 0.1),
     'L0_attn_g1': (1.0, 0.6),
     'L0_attn_beta1': (0.0, 0.8),
     'L0_attn_g2': (1.0, 0.6),
     'L0_attn_beta2': (0.0, 0.8),
     'L0_xattn_norm_w': (1.0, 0.6),
     'L0_xattn_norm_b': (0.0, 0.8),
     'L0_xattn_ctx_norm_w': (1.0, 0.6),
     'L0_xattn_ctx_norm_b': (0.0, 0.41),
     'L0_ffn_br': (0.0, 0.273),
     'L0_ffn_b1': (0.0, 0.8),
     'L0_ffn_b2': (0.0, 0.426)}
    factors = {'L0_attn_wq': 8.0, 'L0_attn_wk': 8.0, 'L0_attn_proj': 8.0, 'L0_xattn_Wq': 8.0}
    for name, (base, spread) in spreads.items():
        noise = np.random.default_rng([zlib.crc32(name.encode()), seed]).standard_normal(out[name].shape)
        drawn = base * np.exp(spread * noise) if base else spread * noise
        out[name] = jnp.asarray(drawn.astype(out[name].dtype))
    for name, factor in factors.items():
        out[name] = (out[name] * factor).astype(out[name].dtype)
    return out
```

```python
from contextlib import ExitStack

import concourse.bass as bass
from concourse import mybir

F32 = mybir.dt.float32
F16 = mybir.dt.float16
BF16 = mybir.dt.bfloat16
U8 = mybir.dt.uint8
ALU = mybir.AluOpType
ACT = mybir.ActivationFunctionType
AXX = mybir.AxisListType.X

P = 128
B, T, D = 32, 112, 256
S2 = 375
H, DH = 16, 64
INNER = H * DH
FF = 1024
KD = D // P
KI = INNER // P
E = 8
CAP = max(1, int(T / E * 1.25))
SLOTS = E * CAP
ES = B * CAP
G4 = 4
NG = B // G4
GT = G4 * T
JT, JP = 3, S2 // 3
WSCALE = 64.0
UNSCALE = 1.0 / WSCALE
EPS = 1e-5
MASKED = 3.0e38
WCOLS = KD * INNER


def at_least(eng, sem, n):
    if isinstance(n, int) and n <= 0:
        return
    eng.wait_ge(sem, n)


def settle(eng, passed, *waits):
    for sem, n in waits:
        at_least(eng, sem, n)
    eng.sem_inc(passed, 1)


def split_product(pe, out, lhs, rhs, first, last):
    (lh, ll), (rh, rl) = lhs, rhs
    pe.matmul(out, lh, rh, start=first, stop=False)
    pe.matmul(out, lh, rl, start=False, stop=False)
    return pe.matmul(out, ll, rh, start=False, stop=last)


def decoder_kernel(nc, a, out):
    root = ExitStack()
    with root:
        def sem(name):
            return root.enter_context(nc.semaphore(name))

        def sb_in(stack):
            return lambda name, shape, dt: stack.enter_context(nc.sbuf_tensor(name, shape, dt))

        def psum_in(stack):
            return lambda name, shape, dt=F32: stack.enter_context(nc.psum_tensor(name, shape, dt))

        sb = sb_in(root)
        x_sb = sb("x_sb", [T, B, D], F32)
        ident = sb("ident", [P, P], F32)
        half_neg = sb("half_neg", [P, 4], F32)
        consts_done = sem("consts_done")
        passed = sem("passed")

        layer1(nc, a, x_sb, ident, half_neg, consts_done, passed, sb_in, psum_in, sem)
        layer2(nc, a, x_sb, ident, half_neg, passed, sb_in, psum_in, sem)
        layer3(nc, a, out, x_sb, ident, half_neg, passed, sb_in, psum_in, sem)


def layer1(nc, a, x_sb, ident, half_neg, consts_done, passed, sb_in, psum_in, sem):
    stack = ExitStack()
    with stack:
        sb, psum = sb_in(stack), psum_in(stack)
        names = ["wq", "wk", "wv", "wo", "w1", "w2"]
        hi = {n: sb(f"a_{n}_hi", [P, WCOLS], F16) for n in names}
        lo = {n: sb(f"a_{n}_lo", [P, WCOLS], F16) for n in names}
        g1, be1, g2, be2 = (sb(f"a_{n}", [P, KD], F32) for n in ("g1", "be1", "g2", "be2"))
        b1 = sb("a_b1", [P, FF // P], F32)
        b2 = sb("a_b2", [T, D], F32)
        causal = sb("causal", [T, T], F32)
        load_layer1(nc, a, x_sb, ident, half_neg, consts_done, causal, hi, lo, (g1, be1, g2, be2, b1, b2), sb_in, psum_in, sem)

        def pair(name, k, c0, n, width):
            c = k * width + c0
            return hi[name][:, c:c + n], lo[name][:, c:c + n]

        xh = sb("xh", [T, G4, D], F32)
        h32 = sb("h32", [P, KD, GT], F32)
        h_hi, h_lo = sb("h_hi", [P, KD, GT], F16), sb("h_lo", [P, KD, GT], F16)
        neg_relu = sb("neg_relu", [P, 4, GT], F32)
        phi_exp = sb("phi_exp", [P, 2, GT], F32)
        qz = sb("qz", [P, H, GT], F32)
        kt = sb("kt", [P, KI, GT], F32)
        v_hi, v_lo = sb("v_hi", [T, G4, INNER], F16), sb("v_lo", [T, G4, INNER], F16)
        sm = sb("sm", [T, 2, 4, T], F32)
        den = sb("den", [T, 2, 4], F32)
        den_eps = sb("den_eps", [T, 2, 4], F32)
        rec = sb("rec", [T, 2, 4], F32)
        pn = sb("pn", [T, 4, 4, T], F32)
        p_hi, p_lo = sb("p_hi", [T, 2, 4 * T], F16), sb("p_lo", [T, 2, 4 * T], F16)
        o_hi, o_lo = sb("o_hi", [P, KI, T], F16), sb("o_lo", [P, KI, T], F16)
        x1 = sb("x1", [T, G4, D], F32)
        xsum = sb("xsum", [T, G4, D], F32)
        gelu32 = sb("gelu32", [P, 2, GT], F32)
        ff_hi = kt[:, 0:KI // 2, :].rearrange("p k t -> p (k t)").bitcast(F16).rearrange("p (f t) -> p f t", t=GT)
        ff_lo = kt[:, KI // 2:KI, :].rearrange("p k t -> p (k t)").bitcast(F16).rearrange("p (f t) -> p f t", t=GT)
        stats = sb("a_stats", [T, G4, 6], F32)
        mom = sb("a_mom", [T, G4, 2], F32)
        rstd = sb("a_rstd", [T, G4], F32)

        NPB = 4
        pb = [psum(f"a_pb{i}", [P, 512]) for i in range(NPB)]
        s_ps = [psum(f"a_s{i}", [P, 512]) for i in range(2)]
        t_ps, o_ps = psum("a_t", [P, 512]), psum("a_o", [P, 512])

        FT = FF // P
        LN1, Q0, K0 = 0, KD, KD + KI
        V0 = K0 + KI
        WO0 = V0 + 2 * G4
        LN2 = WO0 + G4
        F0 = LN2 + KD
        Y0 = F0 + FT
        USES = Y0 + G4
        assert USES % NPB == 0
        UNITS = G4 * H // 4

        stats_done, mom_done, eps_done, rstd_done, xh_done = (
            sem(f"a_{n}") for n in ("stats_done", "mom_done", "eps_done", "rstd_done", "xh_done"))
        pb_ready = sem("a_pb_ready")
        pb_free = [sem(f"a_pb_free{i}") for i in range(NPB)]
        h_hi_done = sem("a_h_hi_done")
        qz_zeroed = sem("a_qz_zeroed")
        relu_done, exp_done, v_hi_done = sem("a_relu_done"), sem("a_exp_done"), sem("a_v_hi_done")
        s_ready, s_masked, den_done, rec_done, pn_done = (
            sem(f"a_{n}") for n in ("s_ready", "s_masked", "den_done", "rec_done", "pn_done"))
        t_ready, p_hi_done, p_lo_done, av_done = (sem(f"a_{n}") for n in ("t_ready", "p_hi_done", "p_lo_done", "av_done"))
        o_hi_done, o_lo_done = sem("a_o_hi_done"), sem("a_o_lo_done")
        xs1_done, xs_done = sem("a_xs1_done"), sem("a_xs_done")
        gelu_done, ff_hi_done = sem("a_gelu_done"), sem("a_ff_hi_done")

        def ready(g, use):
            return USES * g + use + 1

        def freed(g, use):
            return (USES // NPB) * g + use // NPB + 1

        def groups(eng, body):
            body(0)
            with eng.Fori(1, NG) as g:
                body(g)

        block = stack.enter_context(nc.Block())

        @block.tensor
        def _(pe):
            def claim(g, use):
                at_least(pe, pb_free[use % NPB], freed(g, use) - 1)
                return pb[use % NPB]

            def written(g, u0, u1):
                for use in range(u0, u1):
                    pe.wait_ge(pb_free[use % NPB], freed(g, use))

            def turn(g, ln, use):
                pe.wait_ge(xh_done, 3 * g + ln + 1)
                for k in range(KD):
                    bank = claim(g, use + k)
                    for b in range(G4):
                        mm = pe.transpose(bank[:, b * T:(b + 1) * T], xh[:, b, k * P:(k + 1) * P], ident[0:T, 0:T])
                    mm.then_inc(pb_ready, 1)

            def from_h(g, name, use, m, width):
                bank = claim(g, use)
                for k in range(KD):
                    mm = split_product(pe, bank[:, 0:GT], pair(name, k, m * P, P, width),
                                       (h_hi[:, k, :], h_lo[:, k, :]), k == 0, k == KD - 1)
                mm.then_inc(pb_ready, 1)

            def scores(g, u):
                b, quad = divmod(u, 4)
                at_least(pe, s_masked, UNITS * g + u - 1)
                for i in range(4):
                    h = 4 * quad + i
                    mm = pe.matmul(s_ps[u % 2][0:T, i * T:(i + 1) * T], qz[:, h, b * T:(b + 1) * T],
                                   kt[:, h // 2, b * T:(b + 1) * T], start=True, stop=True)
                mm.then_inc(s_ready, 1)

            def turn_scores(g, u):
                pe.wait_ge(pn_done, UNITS * g + u + 1)
                at_least(pe, p_lo_done, UNITS * g + u)
                for i in range(4):
                    mm = pe.transpose(t_ps[0:T, i * T:(i + 1) * T], pn[:, u % 4, i, :], ident[0:T, 0:T])
                mm.then_inc(t_ready, 1)

            def values(g, u):
                b, quad = divmod(u, 4)
                pe.wait_ge(p_lo_done, UNITS * g + u + 1)
                if u % 2 == 0:
                    at_least(pe, o_lo_done, (UNITS // 2) * g + u // 2)
                for i in range(4):
                    h = 4 * quad + i
                    r, c = DH * (h % 2), (u % 2) * 2 * T + (i // 2) * T
                    cols = slice(h * DH, (h + 1) * DH)
                    mm = split_product(pe, o_ps[r:r + DH, c:c + T], (v_hi[:, b, cols], v_lo[:, b, cols]),
                                       (p_hi[:, u % 2, i * T:(i + 1) * T], p_lo[:, u % 2, i * T:(i + 1) * T]), True, True)
                mm.then_inc(av_done, 1)

            def rows_out(g, use, name, lhs):
                bank = claim(g, use)
                for k in range(KI):
                    mm = split_product(pe, bank[0:T, 0:D], lhs(k), pair(name, k, 0, D, D), k == 0, k == KI - 1)
                mm.then_inc(pb_ready, 1)

            def body(g):
                turn(g, 0, LN1)
                written(g, LN1, Q0)
                for m in range(KI):
                    from_h(g, "wq", Q0 + m, m, INNER)
                for m in range(KI):
                    from_h(g, "wk", K0 + m, m, INNER)
                for b in range(G4):
                    for n in range(2):
                        bank = claim(g, V0 + 2 * b + n)
                        for k in range(KD):
                            lhs = (h_hi[:, k, b * T:(b + 1) * T], h_lo[:, k, b * T:(b + 1) * T])
                            mm = split_product(pe, bank[0:T, :], lhs, pair("wv", k, n * 512, 512, INNER), k == 0, k == KD - 1)
                        mm.then_inc(pb_ready, 1)
                written(g, V0 - NPB, V0)
                for t in range(UNITS + 5):
                    if t < UNITS:
                        scores(g, t)
                    if 2 <= t < UNITS + 2:
                        turn_scores(g, t - 2)
                    if 3 <= t < UNITS + 3:
                        if t == 3:
                            written(g, WO0 - NPB, WO0)
                        values(g, t - 3)
                    if t >= 7 and (t - 7) % 4 == 0:
                        b = (t - 7) // 4
                        pe.wait_ge(o_lo_done, (UNITS // 2) * g + 2 * b + 2)
                        rows_out(g, WO0 + b, "wo", lambda k: (o_hi[:, k, :], o_lo[:, k, :]))
                turn(g, 1, LN2)
                written(g, LN2, F0)
                for f in range(FT):
                    from_h(g, "w1", F0 + f, f, FF)
                written(g, Y0 - NPB, Y0)
                for b in range(G4):
                    rows_out(g, Y0 + b, "w2", lambda k: (ff_hi[:, k, b * T:(b + 1) * T], ff_lo[:, k, b * T:(b + 1) * T]))

            groups(pe, body)

        @block.scalar
        def _(act):
            def ln_out(g, ln, use, gain, shift):
                for k in range(KD):
                    act.wait_ge(pb_ready, ready(g, use + k))
                    bank = pb[(use + k) % NPB][:, 0:GT]
                    act.activation(h32[:, k, :], bank, ACT.Identity, bias=shift[:, k:k + 1], scale=gain[:, k:k + 1])
                    act.activation(h_hi[:, k, :], bank, ACT.Identity, bias=shift[:, k:k + 1],
                                   scale=gain[:, k:k + 1]).then_inc(h_hi_done, 1)

            def body(g):
                ln_out(g, 0, LN1, g1, be1)
                for i in range(2 * KI + 1):
                    if i < 2 * KI:
                        act.wait_ge(pb_ready, ready(g, Q0 + i))
                        at_least(act, exp_done, 2 * KI * g + i - 3)
                        act.activation(neg_relu[:, i % 4, :], pb[(Q0 + i) % NPB][:, 0:GT], ACT.Relu,
                                       scale=-1.0).then_inc(relu_done, 1)
                    if i >= 1:
                        j = i - 1
                        act.wait_ge(relu_done, 2 * KI * g + j + 1)
                        use = Q0 + j - 2
                        if j >= 2:
                            act.wait_ge(pb_free[use % NPB], freed(g, use))
                        act.activation(phi_exp[:, j % 2, :], neg_relu[:, j % 4, :], ACT.Exp, scale=-1.0).then_inc(exp_done, 1)
                for i in range(2 * G4):
                    act.wait_ge(pb_ready, ready(g, V0 + i))
                    b, n = divmod(i, 2)
                    act.activation(v_hi[:, b, n * 512:(n + 1) * 512], pb[(V0 + i) % NPB][0:T, :], ACT.Identity,
                                   scale=UNSCALE).then_inc(v_hi_done, 1)
                for t in range(UNITS + 3):
                    if 2 <= t < UNITS + 2:
                        u = t - 2
                        act.wait_ge(t_ready, UNITS * g + u + 1)
                        at_least(act, av_done, UNITS * g + u - 1)
                        act.activation(p_hi[:, u % 2, :], t_ps[0:T, 0:4 * T], ACT.Identity).then_inc(p_hi_done, 1)
                    if t >= 3 and (t - 3) % 2 == 1:
                        u = t - 3
                        act.wait_ge(av_done, UNITS * g + u + 1)
                        if u % 4 == 1 and u >= 5:
                            act.wait_ge(pb_ready, ready(g, WO0 + u // 4 - 1))
                        p0 = 4 * ((u // 2) % 2)
                        act.activation(o_hi[:, p0:p0 + 4, :], o_ps[:, 0:4 * T].rearrange("p (m t) -> p m t", t=T),
                                       ACT.Identity).then_inc(o_hi_done, 1)
                ln_out(g, 1, LN2, g2, be2)
                for f in range(FT):
                    act.wait_ge(pb_ready, ready(g, F0 + f))
                    if f >= 2:
                        act.wait_ge(pb_free[(F0 + f - 2) % NPB], freed(g, F0 + f - 2))
                    act.activation(gelu32[:, f % 2, :], pb[(F0 + f) % NPB][:, 0:GT], ACT.Gelu, bias=b1[:, f:f + 1],
                                   scale=UNSCALE).then_inc(gelu_done, 1)

            groups(act, body)

        @block.vector
        def _(dve):
            def ln_rows(g, ln, rows, dst, done):
                for b in range(G4):
                    ins = dve.bn_stats(stats[:, b, :], rows(b))
                ins.then_inc(stats_done, 1)
                settle(dve, passed, (stats_done, 3 * g + ln + 1))
                for b in range(G4):
                    ins = dve.bn_aggr(mom[:, b, :], stats[:, b, :])
                ins.then_inc(mom_done, 1)
                dve.wait_ge(rstd_done, 3 * g + ln + 1)
                for b in range(G4):
                    ins = dve.tensor_scalar(dst(b), rows(b), mom[:, b, 0:1], rstd[:, b:b + 1], ALU.subtract, ALU.mult)
                ins.then_inc(done, 1)

            def ln_low(g, ln, use):
                for k in range(KD):
                    dve.wait_ge(h_hi_done, 4 * g + 2 * ln + k + 1)
                    dve.tensor_tensor(h_lo[:, k, :], h32[:, k, :], h_hi[:, k, :],
                                      ALU.subtract).then_inc(pb_free[(use + k) % NPB], 1)

            def body(g):
                x_rows = lambda b: x_sb[:, bass.ds(G4 * g + b, 1), :].rearrange("p a d -> p (a d)")
                ln_rows(g, 0, x_rows, lambda b: xh[:, b, :], xh_done)
                ln_low(g, 0, LN1)
                if isinstance(g, int):
                    dve.wait_ge(qz_zeroed, 1)
                for i in range(2 * KI):
                    bank = pb[(Q0 + i) % NPB]
                    dve.wait_ge(exp_done, 2 * KI * g + i + 1)
                    if i < KI:
                        for r in range(2):
                            rows = slice(DH * r, DH * (r + 1))
                            ins = dve.scalar_tensor_tensor(qz[rows, 2 * i + r, :], bank[rows, 0:GT], 0.0,
                                                           phi_exp[rows, i % 2, :], ALU.max, ALU.add)
                    else:
                        ins = dve.scalar_tensor_tensor(kt[:, i - KI, :], bank[:, 0:GT], 0.0, phi_exp[:, i % 2, :],
                                                       ALU.max, ALU.add)
                    ins.then_inc(pb_free[(Q0 + i) % NPB], 1)
                for i in range(2 * G4):
                    b, n = divmod(i, 2)
                    cols = slice(n * 512, (n + 1) * 512)
                    dve.wait_ge(v_hi_done, 2 * G4 * g + i + 1)
                    dve.scalar_tensor_tensor(v_lo[:, b, cols], pb[(V0 + i) % NPB][0:T, :], UNSCALE, v_hi[:, b, cols],
                                             ALU.mult, ALU.subtract).then_inc(pb_free[(V0 + i) % NPB], 1)
                for t in range(UNITS + 5):
                    if t >= 4 and t - 4 < UNITS and (t - 4) % 2 == 1:
                        u = t - 4
                        dve.wait_ge(o_hi_done, (UNITS // 2) * g + u // 2 + 1)
                        p0 = 4 * ((u // 2) % 2)
                        dve.tensor_tensor(o_lo[:, p0:p0 + 4, :], o_ps[:, 0:4 * T].rearrange("p (m t) -> p m t", t=T),
                                          o_hi[:, p0:p0 + 4, :], ALU.subtract).then_inc(o_lo_done, 1)
                    if t < UNITS:
                        u = t
                        dve.wait_ge(s_ready, UNITS * g + u + 1)
                        at_least(dve, pn_done, UNITS * g + u - 1)
                        for i in range(4):
                            ins = dve.tensor_tensor_reduce(sm[:, u % 2, i, :], s_ps[u % 2][0:T, i * T:(i + 1) * T], causal[:, :],
                                                           1.0, 0.0, ALU.mult, ALU.add, den[:, u % 2, i:i + 1])
                        ins.then_inc(s_masked, 1)
                        dve.wait_ge(s_masked, UNITS * g + u + 1)
                        dve.tensor_scalar(den_eps[:, u % 2, :], den[:, u % 2, :], 1e-6, None, ALU.add).then_inc(den_done, 1)
                        dve.wait_ge(den_done, UNITS * g + u + 1)
                        dve.reciprocal(rec[:, u % 2, :], den_eps[:, u % 2, :]).then_inc(rec_done, 1)
                    if 2 <= t < UNITS + 2:
                        u = t - 2
                        dve.wait_ge(p_hi_done, UNITS * g + u + 1)
                        dve.tensor_tensor(p_lo[:, u % 2, :], t_ps[0:T, 0:4 * T], p_hi[:, u % 2, :],
                                          ALU.subtract).then_inc(p_lo_done, 1)
                    if t >= 8 and (t - 8) % 4 == 0:
                        b = (t - 8) // 4
                        use = WO0 + b
                        dve.wait_ge(pb_ready, ready(g, use))
                        dve.scalar_tensor_tensor(x1[:, b, :], pb[use % NPB][0:T, 0:D], UNSCALE, x_rows(b),
                                                 ALU.mult, ALU.add).then_inc(pb_free[use % NPB], 1)
                dve.wait_ge(pb_free[(LN2 - 1) % NPB], freed(g, LN2 - 1))
                ln_rows(g, 1, lambda b: x1[:, b, :], lambda b: xh[:, b, :], xh_done)
                ln_low(g, 1, LN2)
                for f in range(FT):
                    dve.wait_ge(ff_hi_done, FT * g + f + 1)
                    dve.tensor_tensor(ff_lo[:, f, :], gelu32[:, f % 2, :], ff_hi[:, f, :],
                                      ALU.subtract).then_inc(pb_free[(F0 + f) % NPB], 1)
                dve.wait_ge(xs_done, g + 1)
                for b in range(G4):
                    use = Y0 + b
                    dve.wait_ge(pb_ready, ready(g, use))
                    dve.scalar_tensor_tensor(xsum[:, b, :], pb[use % NPB][0:T, 0:D], UNSCALE, xsum[:, b, :],
                                             ALU.mult, ALU.add).then_inc(pb_free[use % NPB], 1)
                dve.wait_ge(pb_free[(USES - 1) % NPB], freed(g, USES - 1))
                ln_rows(g, 2, lambda b: xsum[:, b, :], x_rows, xh_done)

            groups(dve, body)

        @block.gpsimd
        def _(pool):
            def ln_rstd(g, ln):
                settle(pool, passed, (mom_done, 3 * g + ln + 1))
                pool.tensor_scalar(rstd[:, :], mom[:, :, 1], EPS, None, ALU.add).then_inc(eps_done, 1)
                pool.wait_ge(eps_done, 3 * g + ln + 1)
                pool.tensor_tensor(rstd[:, :], rstd[:, :], half_neg[0:T, :], ALU.pow).then_inc(rstd_done, 1)

            def body(g):
                ln_rstd(g, 0)
                for u in range(UNITS):
                    pool.wait_ge(rec_done, UNITS * g + u + 1)
                    at_least(pool, t_ready, UNITS * g + u - 3)
                    pool.tensor_tensor(pn[:, u % 4, :, :], sm[:, u % 2, :, :],
                                       rec[:, u % 2, :].unsqueeze(2).to_broadcast([T, 4, T]), ALU.mult).then_inc(pn_done, 1)
                ln_rstd(g, 1)
                pool.tensor_tensor(xsum[:, :, :], x1[:, :, :], x_sb[:, bass.ds(G4 * g, G4), :], ALU.add).then_inc(xs1_done, 1)
                pool.wait_ge(xs1_done, g + 1)
                pool.tensor_tensor(xsum[:, :, :], xsum[:, :, :], b2[:, :].unsqueeze(1).to_broadcast([T, G4, D]),
                                   ALU.add).then_inc(xs_done, 1)
                for f in range(FT):
                    settle(pool, passed, (gelu_done, FT * g + f + 1))
                    pool.tensor_copy(ff_hi[:, f, :], gelu32[:, f % 2, :]).then_inc(ff_hi_done, 1)
                ln_rstd(g, 2)

            pool.memset(qz[:, :, :], 0.0).then_inc(qz_zeroed, 1)
            groups(pool, body)




def load_layer1(nc, a, x_sb, ident, half_neg, consts_done, causal, hi, lo, vectors, sb_in, psum_in, sem):
    stack = ExitStack()
    with stack:
        sb, psum = sb_in(stack), psum_in(stack)
        g1, be1, g2, be2, b1, b2 = vectors
        NST = 3
        stage = [sb(f"a_stage{i}", [P, WCOLS], F32) for i in range(NST)]
        raw = [sb(f"a_raw{i}", [P, KD, INNER], F32) for i in range(2)]
        turned = sb("a_turned", [P, 2 * KI // 2, 4, P], F32)
        proj2 = sb("a_proj2", [P, P], F32)
        turn_ps = [psum(f"a_turn{i}", [P, 4 * P]) for i in range(4)]
        fold_ps = [psum(f"a_fold{i}", [P, 4 * P]) for i in range(4)]
        loaded = [sem(f"a_loaded{i}") for i in range(NST)]
        hi_done, lo_done = sem("a_whi_done"), sem("a_wlo_done")
        raw_loaded, vec_loaded, x_loaded = sem("a_raw_loaded"), sem("a_vec_loaded"), sem("a_x_loaded")
        p2_zero, p2_loaded = sem("a_p2_zero"), sem("a_p2_loaded")
        turn_ready, turn_done, fold_ready, fold_hi, fold_lo = (
            sem(f"a_{n}") for n in ("turn_ready", "turn_done", "fold_ready", "fold_hi", "fold_lo"))
        rows = lambda w: w.rearrange("(k p) n -> p k n", p=P)
        jobs = [(rows(a[f"L0_attn_{n}"]), hi[n][:, :], lo[n][:, :]) for n in ("wv", "wo", "w1", "w2")]
        NT = 2 * KI * KD // 4
        block = stack.enter_context(nc.Block())

        @block.sync
        def _(sp):
            for i, n in enumerate(("L0_attn_wq", "L0_attn_wk")):
                sp.dma_start(raw[i][:, :, :], rows(a[n])).then_inc(raw_loaded, 16)
            sp.wait_ge(p2_zero, 1)
            for r in range(2):
                sp.dma_start(proj2[DH * r:DH * (r + 1), DH * r:DH * (r + 1)], a["L0_attn_proj"]).then_inc(p2_loaded, 16)
            for i, (src, _, _) in enumerate(jobs):
                at_least(sp, lo_done, i - NST + 1)
                sp.dma_start(stage[i % NST][:, :].rearrange("p (k n) -> p k n", n=src.shape[2]), src).then_inc(loaded[i % NST], 16)
            for t, n in ((g1, "g1"), (be1, "beta1"), (g2, "g2"), (be2, "beta2"), (b1, "b1")):
                sp.dma_start(t[:, :], a[f"L0_attn_{n}"].rearrange("(k p) -> p k", p=P),
                             allow_slow_non_contiguous=True).then_inc(vec_loaded, 16)
            sp.dma_start(b2[:, :], a["L0_attn_b2"].partition_broadcast(T)).then_inc(vec_loaded, 16)
            sp.dma_start(x_sb[:, :, :], a["x"].rearrange("b t d -> t b d")).then_inc(x_loaded, 16)
            sp.wait_ge(vec_loaded, 6 * 16)
            sp.wait_ge(x_loaded, 16)

        @block.gpsimd
        def _(pool):
            pool.memset(proj2[:, :], 0.0).then_inc(p2_zero, 1)
            pool.memset(ident[:, :], 1.0).then_inc(consts_done, 1)
            pool.memset(causal[:, :], 1.0).then_inc(consts_done, 1)
            pool.memset(half_neg[:, :], -0.5).then_inc(consts_done, 1)
            pool.wait_ge(consts_done, 3)
            pool.affine_select(out=ident[:, :], in_=ident[:, :], compare_op=ALU.is_equal, fill=0.0, base=0,
                               pattern=[[-1, P]], channel_multiplier=1).then_inc(consts_done, 1)
            pool.affine_select(out=causal[:, :], in_=causal[:, :], compare_op=ALU.is_ge, fill=0.0, base=0,
                               pattern=[[-1, T]], channel_multiplier=1).then_inc(consts_done, 1)

        @block.tensor
        def _(pe):
            pe.wait_ge(consts_done, 5)
            pe.wait_ge(raw_loaded, 32)
            for n in range(NT):
                w, m2 = divmod(n, KI // 2)
                at_least(pe, turn_done, n - 3)
                for i in range(4):
                    m, k = 2 * m2 + i // 2, i % 2
                    mm = pe.transpose(turn_ps[n % 4][:, i * P:(i + 1) * P], raw[w][:, k, m * P:(m + 1) * P], ident[:, :])
                mm.then_inc(turn_ready, 1)
            pe.wait_ge(p2_loaded, 32)
            for n in range(NT):
                pe.wait_ge(turn_done, n + 1)
                at_least(pe, fold_lo, n - 3)
                for i in range(4):
                    mm = pe.matmul(fold_ps[n % 4][:, i * P:(i + 1) * P], turned[:, n, i, :], proj2[:, :], start=True, stop=True)
                mm.then_inc(fold_ready, 1)

        def folded(t, n):
            w, m2 = divmod(n, KI // 2)
            return t[("wq", "wk")[w]][:, :].rearrange("p (k m c) -> p m k c", k=KD, c=P)[:, 2 * m2:2 * m2 + 2, :, :]

        def fold_bank(n):
            return fold_ps[n % 4][:, :].rearrange("p (m k c) -> p m k c", m=2, k=KD)

        @block.scalar
        def _(act):
            for n in range(NT):
                act.wait_ge(turn_ready, n + 1)
                act.activation(turned[:, n, :, :], turn_ps[n % 4][:, :].rearrange("p (i c) -> p i c", c=P),
                               ACT.Identity).then_inc(turn_done, 1)
            for n in range(NT):
                act.wait_ge(fold_ready, n + 1)
                act.activation(folded(hi, n), fold_bank(n), ACT.Identity).then_inc(fold_hi, 1)
            for i, (_, h, _) in enumerate(jobs):
                act.wait_ge(loaded[i % NST], 16 * (i // NST + 1))
                act.activation(h, stage[i % NST][:, :], ACT.Identity, scale=WSCALE).then_inc(hi_done, 1)

        @block.vector
        def _(dve):
            for n in range(NT):
                dve.wait_ge(fold_hi, n + 1)
                dve.tensor_tensor(folded(lo, n), fold_bank(n), folded(hi, n), ALU.subtract).then_inc(fold_lo, 1)
            for i, (_, h, l) in enumerate(jobs):
                dve.wait_ge(hi_done, i + 1)
                dve.scalar_tensor_tensor(l, stage[i % NST][:, :], WSCALE, h, ALU.mult, ALU.subtract).then_inc(lo_done, 1)


def layer2(nc, a, x_sb, ident, half_neg, passed, sb_in, psum_in, sem):
    stack = ExitStack()
    with stack:
        sb, psum = sb_in(stack), psum_in(stack)
        names = ["q", "k", "v", "o"]
        hi = {n: sb(f"b_w{n}_hi", [P, WCOLS], F16) for n in names}
        lo = {n: sb(f"b_w{n}_lo", [P, WCOLS], F16) for n in names}
        gx, bx, gc, bc = (sb(f"b_{n}", [P, KD], F32) for n in ("gx", "bx", "gc", "bc"))
        load_layer2(nc, a, hi, lo, (gx, bx, gc, bc), sb_in, sem)

        def pair(name, k, c0, n, width):
            c = k * width + c0
            return hi[name][:, c:c + n], lo[name][:, c:c + n]

        SP2 = S2 + 1
        NT4 = JT + 1
        ctx = sb("ctx", [JP, 2, JT, D], F32)
        mask8 = sb("mask8", [T, 2, S2], U8)
        mask_bias = sb("mask_bias", [T, 2, S2], F32)
        stats = sb("b_stats", [P, NT4, 6], F32)
        mom = sb("b_mom", [P, NT4, 2], F32)
        rstd = sb("b_rstd", [P, NT4], F32)
        shift = sb("b_shift", [P, NT4], F32)
        xc = sb("xc", [JP, JT, D], F32)
        xn = sb("xn", [T, D], F32)
        cn32 = sb("cn32", [P, KD, S2], F32)
        cn_hi, cn_lo = (sb(f"cn_{n}", [P, 2, KD, SP2], F16) for n in ("hi", "lo"))
        xt32 = sb("xt32", [P, KD, T], F32)
        xt_hi, xt_lo = (sb(f"xt_{n}", [P, 2, KD, T], F16) for n in ("hi", "lo"))
        k_hi, k_lo = (sb(f"k_{n}", [P, 2, KI, SP2], F16) for n in ("hi", "lo"))
        v2_hi, v2_lo = (sb(f"v2_{n}", [JP, 2, JT, INNER], F16) for n in ("hi", "lo"))
        qz_hi, qz_lo = (sb(f"qz_{n}", [P, 2, H, T], F16) for n in ("hi", "lo"))
        s_neg = sb("s_neg", [T, 2, S2], F32)
        neg_max = sb("neg_max", [T, 4], F32)
        p32 = sb("p32", [T, 4, S2], F32)
        p_sum = sb("p_sum", [T, 4], F32)
        p_rec = sb("p_rec", [T, 4], F32)
        p_norm = sb("p_norm", [T, 4, S2], F32)
        pt_hi, pt_lo = (sb(f"pt_{n}", [JP, 2, JT * T], F16) for n in ("hi", "lo"))
        o_hi, o_lo = (sb(f"b_o_{n}", [P, KI, T], F16) for n in ("hi", "lo"))
        z = sb("b_z", [T, D], F32)
        z_stats, z_mom, z_rstd = sb("z_stats", [T, 6], F32), sb("z_mom", [T, 2], F32), sb("z_rstd", [T, 1], F32)

        NPB = 3
        pb = [psum(f"b_pb{i}", [P, 512]) for i in range(NPB)]
        s_ps = [psum(f"b_s{i}", [P, 512]) for i in range(2)]
        t_ps, o_ps, misc_ps = psum("b_t", [P, 512]), psum("b_o", [P, 512]), psum("b_misc", [P, 512])

        NCH = 16
        Q0, K0, V0 = 0, 2, 2 + KI
        TURN_AT = (11, 12)
        PER = NCH + KD
        PRE = 2 * KD + NCH
        assert PER % NPB == 0

        def has_prep(b):
            return not isinstance(b, int) or b + 2 < B

        def use_piece(n, s):
            if isinstance(n, int) and n == 0:
                return 0, 2 * KD + s
            b = n - 1
            return b, PRE + s + (sum(s > at for at in TURN_AT) if has_prep(b) else 0)

        def use_turn(n, k):
            if isinstance(n, int) and n < 2:
                return 0, KD * n + k
            return n - 2, PRE + TURN_AT[k] + 1 + k

        def ready(use):
            return use[0] * PER + use[1] + 1

        def freed(use):
            return use[0] * (PER // NPB) + use[1] // NPB + 1

        def bank(use):
            return pb[use[1] % NPB]

        ctx_loaded = [sem(f"b_ctx_loaded{i}") for i in range(2)]
        mask_loaded = [sem(f"b_mask_loaded{i}") for i in range(2)]
        mask_m1, mask_done = sem("b_mask_m1"), sem("b_mask_done")
        zeroed, stats_zeroed = sem("b_zeroed"), sem("b_stats_zeroed")
        pb_ready = sem("b_pb_ready")
        pb_free = [sem(f"b_pb_free{i}") for i in range(NPB)]
        piece_hi = sem("b_piece_hi")
        stats_done, mom_done, eps_done, rstd_done, shift_neg, shift_done = (
            sem(f"b_{n}") for n in ("stats_done", "mom_done", "eps_done", "rstd_done", "shift_neg", "shift_done"))
        xc_done, xn_done, xt_ready, xt_turned, xt_hi_done, xt_done = (
            sem(f"b_{n}") for n in ("xc_done", "xn_done", "xt_ready", "xt_turned", "xt_hi_done", "xt_done"))
        cn_hi_done, cn_done = sem("b_cn_hi_done"), sem("b_cn_done")
        s_ready, s_masked, p_exp, p_sum_rec, p_norm_done = (
            sem(f"b_{n}") for n in ("s_ready", "s_masked", "p_exp", "p_sum_rec", "p_norm_done"))
        t_ready, pt_hi_done, pt_lo_done, av_done, o_hi_done, o_lo_done = (
            sem(f"b_{n}") for n in ("t_ready", "pt_hi_done", "pt_lo_done", "av_done", "o_hi_done", "o_lo_done"))
        wo_ready, z_done, z_stats_done, z_mom_done, z_eps, z_rstd_done, x_done = (
            sem(f"b_{n}") for n in ("wo_ready", "z_done", "z_stats_done", "z_mom_done", "z_eps", "z_rstd_done", "x_done"))

        def x_row(b):
            return x_sb[:, bass.ds(b, 1), :].rearrange("p a d -> p (a d)")

        def batches(eng, body):
            body(0, 0)
            body(1, 1)
            with eng.Fori(1, B // 2 - 1) as i:
                for par in range(2):
                    body(2 * i + par, par)
            body(B - 2, 0)
            body(B - 1, 1)

        def is_first(b):
            return isinstance(b, int) and b == 0

        def is_last(b):
            return isinstance(b, int) and b == B - 1

        block = stack.enter_context(nc.Block())

        @block.sync
        def _(sp):
            def load(n, par):
                settle(sp, passed, (xc_done, n - 1))
                sp.dma_start(ctx[:, par, :, :], a["ctx_1024"][bass.ds(n, 1), :, :].rearrange(
                    "a (p t) d -> p (a t) d", t=JT)).then_inc(ctx_loaded[par], 16)
                settle(sp, passed, (mask_done, n - 1))
                sp.dma_start(mask8[:, par, :], a["mask_BxS2_bf1"][bass.ds(n, 1), :].rearrange(
                    "a s -> (a s)").partition_broadcast(T)).then_inc(mask_loaded[par], 16)

            load(0, 0)
            load(1, 1)
            with sp.Fori(1, B // 2) as i:
                for par in range(2):
                    load(2 * i + par, par)

        @block.tensor
        def _(pe):
            def claim(use):
                at_least(pe, pb_free[use[1] % NPB], freed(use) - 1)
                return bank(use)

            def turn_x(n):
                pe.wait_ge(xn_done, n + 1)
                at_least(pe, z_done, n - 2)
                at_least(pe, xt_turned, n)
                for k in range(KD):
                    mm = pe.transpose(misc_ps[:, k * T:(k + 1) * T], xn[:, k * P:(k + 1) * P], ident[0:T, 0:T])
                mm.then_inc(xt_ready, 1)

            def turn_ctx(n, k):
                pe.wait_ge(xc_done, n + 1)
                ps = claim(use_turn(n, k))
                for t in range(JT):
                    mm = pe.transpose(ps[:, t * JP:(t + 1) * JP], xc[:, t, k * P:(k + 1) * P], ident[0:JP, 0:JP])
                mm.then_inc(pb_ready, 1)

            def piece(n, par, s):
                if s == Q0:
                    pe.wait_ge(xt_done, n + 1)
                if s == K0:
                    pe.wait_ge(cn_done, KD * (n + 1))
                ps = claim(use_piece(n, s))
                if s < K0:
                    for i in range(4):
                        for k in range(KD):
                            mm = split_product(pe, ps[:, i * T:(i + 1) * T], pair("q", k, (4 * s + i) * P, P, INNER),
                                               (xt_hi[:, par, k, :], xt_lo[:, par, k, :]), k == 0, k == KD - 1)
                elif s < V0:
                    for k in range(KD):
                        mm = split_product(pe, ps[:, 0:S2], pair("k", k, (s - K0) * P, P, INNER),
                                           (cn_hi[:, par, k, 0:S2], cn_lo[:, par, k, 0:S2]), k == 0, k == KD - 1)
                else:
                    t, half = divmod(s - V0, 2)
                    cols = slice(t * JP, (t + 1) * JP)
                    for k in range(KD):
                        mm = split_product(pe, ps[0:JP, :], (cn_hi[:, par, k, cols], cn_lo[:, par, k, cols]),
                                           pair("v", k, half * 512, 512, INNER), k == 0, k == KD - 1)
                mm.then_inc(pb_ready, 1)

            def written(n, s):
                use = use_piece(n, s)
                pe.wait_ge(pb_free[use[1] % NPB], freed(use))

            def scores(b, par, h):
                written(b, Q0 + h // 8)
                written(b, K0 + h // 2)
                at_least(pe, s_masked, H * b + h - 1)
                mm = split_product(pe, s_ps[h % 2][0:T, 0:S2], (qz_hi[:, par, h, :], qz_lo[:, par, h, :]),
                                   (k_hi[:, par, h // 2, 0:S2], k_lo[:, par, h // 2, 0:S2]), True, True)
                mm.then_inc(s_ready, 1)

            def turn_scores(b, h):
                pe.wait_ge(p_norm_done, H * b + h + 1)
                at_least(pe, pt_lo_done, H * b + h)
                for t in range(JT):
                    mm = pe.transpose(t_ps[0:JP, t * T:(t + 1) * T], p_norm[:, h % 4, t * JP:(t + 1) * JP], ident[0:T, 0:T])
                mm.then_inc(t_ready, 1)

            def values(b, par, h):
                if h == 0:
                    for s in range(NCH - NPB, NCH):
                        written(b, s)
                pe.wait_ge(pt_lo_done, H * b + h + 1)
                if h % 8 == 0:
                    at_least(pe, o_lo_done, 2 * b + h // 8)
                r, c = DH * (h % 2), (h // 2 % 4) * T
                for t in range(JT):
                    cols = slice(h * DH, (h + 1) * DH)
                    mm = split_product(pe, o_ps[r:r + DH, c:c + T], (v2_hi[:, par, t, cols], v2_lo[:, par, t, cols]),
                                       (pt_hi[:, h % 2, t * T:(t + 1) * T], pt_lo[:, h % 2, t * T:(t + 1) * T]),
                                       t == 0, t == JT - 1)
                mm.then_inc(av_done, 1)

            def out_rows(b):
                pe.wait_ge(o_lo_done, 2 * b + 2)
                at_least(pe, xt_turned, min(b + 3, B) if isinstance(b, int) else b + 3)
                at_least(pe, z_done, b)
                for m in range(KI):
                    mm = split_product(pe, misc_ps[0:T, 0:D], (o_hi[:, m, :], o_lo[:, m, :]), pair("o", m, 0, D, D),
                                       m == 0, m == KI - 1)
                mm.then_inc(wo_ready, 1)

            def body(b, par):
                for s in range(H):
                    if s + 2 < H:
                        scores(b, par, s + 2)
                    elif not is_last(b):
                        scores(b + 1, 1 - par, s + 2 - H)
                    if not is_last(b):
                        piece(b + 1, 1 - par, s)
                    turn_scores(b, s)
                    if s > 0:
                        values(b, par, s - 1)
                    elif not is_first(b):
                        values(b - 1, 1 - par, H - 1)
                    if s == 2 and not is_first(b):
                        out_rows(b - 1)
                    if has_prep(b):
                        if s == 10:
                            turn_x(b + 2)
                        if s in TURN_AT:
                            turn_ctx(b + 2, TURN_AT.index(s))

            for n in range(2):
                turn_x(n)
                for k in range(KD):
                    turn_ctx(n, k)
            for s in range(NCH):
                piece(0, 0, s)
            for h in range(2):
                scores(0, 0, h)
            batches(pe, body)
            values(B - 1, 1, H - 1)
            out_rows(B - 1)

        @block.scalar
        def _(act):
            def x_columns(n):
                act.wait_ge(xt_ready, n + 1)
                at_least(act, xt_done, n)
                for k in range(KD):
                    ins = act.activation(xt32[:, k, :], misc_ps[:, k * T:(k + 1) * T], ACT.Identity, bias=bx[:, k:k + 1],
                                         scale=gx[:, k:k + 1])
                ins.then_inc(xt_turned, 1)

            def ctx_columns(n, k):
                use = use_turn(n, k)
                act.wait_ge(pb_ready, ready(use))
                at_least(act, cn_done, KD * (n - 1) + k + 1)
                act.activation(cn32[:, k, :], bank(use)[:, 0:S2], ACT.Identity, bias=bc[:, k:k + 1],
                               scale=gc[:, k:k + 1]).then_inc(pb_free[use[1] % NPB], 1)

            def piece_high(n, par, s):
                use = use_piece(n, s)
                act.wait_ge(pb_ready, ready(use))
                ps = bank(use)
                if s < K0:
                    for r in range(2):
                        rows = slice(DH * r, DH * (r + 1))
                        ins = act.activation(qz_hi[rows, par, 8 * s + r:8 * s + 8:2, :],
                                             ps[rows, 0:4 * T].rearrange("p (m t) -> p m t", t=T), ACT.Identity,
                                             scale=UNSCALE * DH ** -0.5)
                elif s < V0:
                    ins = act.activation(k_hi[:, par, s - K0, 0:S2], ps[:, 0:S2], ACT.Identity, scale=UNSCALE)
                else:
                    t, half = divmod(s - V0, 2)
                    ins = act.activation(v2_hi[:, par, t, half * 512:(half + 1) * 512], ps[0:JP, :], ACT.Identity, scale=UNSCALE)
                ins.then_inc(piece_hi, 1)

            def softmax_exp(b, h):
                act.wait_ge(s_masked, H * b + h + 1)
                at_least(act, p_norm_done, H * b + h - 3)
                act.activation(p32[:, h % 4, :], s_neg[:, h % 2, :], ACT.Exp, bias=neg_max[:, h % 4:h % 4 + 1], scale=-1.0,
                               accum_out=p_sum[:, h % 4:h % 4 + 1]).then_inc(p_exp, 1)

            def turned_high(b, h):
                act.wait_ge(t_ready, H * b + h + 1)
                at_least(act, av_done, H * b + h - 1)
                act.activation(pt_hi[:, h % 2, :], t_ps[0:JP, 0:JT * T], ACT.Identity).then_inc(pt_hi_done, 1)

            def out_high(b, half):
                act.wait_ge(av_done, H * b + 8 * half + 8)
                if half == 0:
                    at_least(act, wo_ready, b)
                act.activation(o_hi[:, 4 * half:4 * half + 4, :], o_ps[:, 0:4 * T].rearrange("p (m t) -> p m t", t=T),
                               ACT.Identity).then_inc(o_hi_done, 1)

            def body(b, par):
                for s in range(H):
                    if s + 1 < H:
                        softmax_exp(b, s + 1)
                    elif not is_last(b):
                        softmax_exp(b + 1, 0)
                    if s == 1 and not is_first(b):
                        out_high(b - 1, 1)
                    if s == 9:
                        out_high(b, 0)
                    if not is_last(b):
                        piece_high(b + 1, 1 - par, s)
                    turned_high(b, s)
                    if has_prep(b):
                        if s == 11:
                            x_columns(b + 2)
                        if s - 1 in TURN_AT:
                            ctx_columns(b + 2, TURN_AT.index(s - 1))

            for n in range(2):
                x_columns(n)
                for k in range(KD):
                    ctx_columns(n, k)
            act.wait_ge(zeroed, 2)
            for s in range(NCH):
                piece_high(0, 0, s)
            softmax_exp(0, 0)
            batches(act, body)
            out_high(B - 1, 1)

        @block.vector
        def _(dve):
            def prep_stats(n, par, tiles):
                dve.wait_ge(ctx_loaded[par], 16 * (half_of(n) + 1))
                at_least(dve, mom_done, n)
                for t in tiles:
                    src = ctx[:, par, t, :] if t < JT else x_row(n)
                    ins = dve.bn_stats(stats[0:JP if t < JT else T, t, :], src)
                if JT in tiles:
                    ins.then_inc(stats_done, 1)

            def prep_moments(n):
                settle(dve, passed, (stats_done, n + 1), (xc_done, n))
                for t in range(NT4):
                    ins = dve.bn_aggr(mom[0:JP if t < JT else T, t, :], stats[0:JP if t < JT else T, t, :])
                ins.then_inc(mom_done, 1)

            def prep_x(n):
                dve.wait_ge(rstd_done, n + 1)
                at_least(dve, xt_ready, n)
                dve.tensor_scalar(xn[:, :], x_row(n), mom[0:T, JT, 0:1], rstd[0:T, JT:JT + 1], ALU.subtract,
                                  ALU.mult).then_inc(xn_done, 1)

            def piece_low(n, par, s):
                use = use_piece(n, s)
                dve.wait_ge(piece_hi, NCH * n + s + 1)
                ps = bank(use)
                if s < K0:
                    for r in range(2):
                        rows = slice(DH * r, DH * (r + 1))
                        heads = slice(8 * s + r, 8 * s + 8, 2)
                        ins = dve.scalar_tensor_tensor(qz_lo[rows, par, heads, :], ps[rows, 0:4 * T].rearrange("p (m t) -> p m t", t=T),
                                                       UNSCALE * DH ** -0.5, qz_hi[rows, par, heads, :], ALU.mult, ALU.subtract)
                elif s < V0:
                    ins = dve.scalar_tensor_tensor(k_lo[:, par, s - K0, 0:S2], ps[:, 0:S2], UNSCALE, k_hi[:, par, s - K0, 0:S2],
                                                   ALU.mult, ALU.subtract)
                else:
                    t, half = divmod(s - V0, 2)
                    cols = slice(half * 512, (half + 1) * 512)
                    ins = dve.scalar_tensor_tensor(v2_lo[:, par, t, cols], ps[0:JP, :], UNSCALE, v2_hi[:, par, t, cols],
                                                   ALU.mult, ALU.subtract)
                ins.then_inc(pb_free[use[1] % NPB], 1)

            def mask_max(b, par, h):
                waits = [(s_ready, H * b + h + 1), (p_exp, H * b + h - 1)]
                if h == 0:
                    waits.append((mask_done, b + 1))
                settle(dve, passed, *waits)
                dve.tensor_tensor_reduce(s_neg[:, h % 2, :], s_ps[h % 2][0:T, 0:S2], mask_bias[:, par, :], -1.0, 3.4e38,
                                         ALU.add, ALU.min, neg_max[:, h % 4:h % 4 + 1]).then_inc(s_masked, 1)

            def sum_reciprocal(b, h):
                dve.wait_ge(p_exp, H * b + h + 1)
                dve.reciprocal(p_rec[:, h % 4:h % 4 + 1], p_sum[:, h % 4:h % 4 + 1]).then_inc(p_sum_rec, 1)

            def turned_low(b, h):
                dve.wait_ge(pt_hi_done, H * b + h + 1)
                dve.tensor_tensor(pt_lo[:, h % 2, :], t_ps[0:JP, 0:JT * T], pt_hi[:, h % 2, :],
                                  ALU.subtract).then_inc(pt_lo_done, 1)

            def out_low(b, half):
                dve.wait_ge(o_hi_done, 2 * b + half + 1)
                dve.tensor_tensor(o_lo[:, 4 * half:4 * half + 4, :], o_ps[:, 0:4 * T].rearrange("p (m t) -> p m t", t=T),
                                  o_hi[:, 4 * half:4 * half + 4, :], ALU.subtract).then_inc(o_lo_done, 1)

            def residual(b):
                dve.wait_ge(wo_ready, b + 1)
                at_least(dve, x_done, b)
                dve.scalar_tensor_tensor(z[:, :], misc_ps[0:T, 0:D], UNSCALE, x_row(b), ALU.mult, ALU.add).then_inc(z_done, 1)
                dve.wait_ge(z_done, b + 1)
                dve.bn_stats(z_stats[:, :], z[:, :]).then_inc(z_stats_done, 1)

            def residual_moments(b):
                settle(dve, passed, (z_stats_done, b + 1))
                dve.bn_aggr(z_mom[:, :], z_stats[:, :]).then_inc(z_mom_done, 1)

            def norm_out(b):
                dve.wait_ge(z_rstd_done, b + 1)
                dve.tensor_scalar(x_row(b), z[:, :], z_mom[:, 0:1], z_rstd[:, :], ALU.subtract, ALU.mult).then_inc(x_done, 1)

            def body(b, par):
                for s in range(H):
                    if s + 1 < H:
                        mask_max(b, par, s + 1)
                    elif not is_last(b):
                        mask_max(b + 1, 1 - par, 0)
                    sum_reciprocal(b, s)
                    if not is_first(b):
                        if s == 1:
                            out_low(b - 1, 1)
                        if s == 3:
                            residual(b - 1)
                        if s == 4:
                            residual_moments(b - 1)
                        if s == 6:
                            norm_out(b - 1)
                    if s == 9:
                        out_low(b, 0)
                    if not is_last(b):
                        piece_low(b + 1, 1 - par, s)
                    turned_low(b, s)
                    if has_prep(b):
                        if s == 2:
                            prep_stats(b + 2, par, (0, 1))
                        if s == 4:
                            prep_stats(b + 2, par, (2, JT))
                        if s == 5:
                            prep_moments(b + 2)
                        if s == 7:
                            prep_x(b + 2)

            def half_of(n):
                return n // 2 if isinstance(n, int) else halves[0]

            halves = [None]
            dve.wait_ge(stats_zeroed, 1)
            for n in range(2):
                prep_stats(n, n, (0, 1, 2, JT))
                prep_moments(n)
                prep_x(n)
            dve.wait_ge(zeroed, 2)
            for s in range(NCH):
                piece_low(0, 0, s)
            mask_max(0, 0, 0)
            body(0, 0)
            body(1, 1)
            with dve.Fori(1, B // 2 - 1) as i:
                halves[0] = i + 1
                for par in range(2):
                    body(2 * i + par, par)
            body(B - 2, 0)
            body(B - 1, 1)
            out_low(B - 1, 1)
            residual(B - 1)
            residual_moments(B - 1)
            norm_out(B - 1)

        @block.gpsimd
        def _(pool):
            def mask(n, par):
                settle(pool, passed, (mask_loaded[par], 16 * (half_of(n) + 1)),
                       (s_masked, H * (n - 1)))
                pool.tensor_scalar(mask_bias[:, par, :].rearrange("q (t p) -> q t p", t=JT),
                                   mask8[:, par, :].rearrange("q (p t) -> q t p", t=JT), -1.0, MASKED, ALU.add,
                                   ALU.mult).then_inc(mask_done, 1)

            def prep_rstd(n):
                settle(pool, passed, (mom_done, n + 1), (xc_done, n))
                pool.tensor_scalar(rstd[:, :], mom[:, :, 1], EPS, None, ALU.add).then_inc(eps_done, 1)
                pool.wait_ge(eps_done, n + 1)
                pool.tensor_tensor(rstd[:, :], rstd[:, :], half_neg[:, :], ALU.pow).then_inc(rstd_done, 1)
                pool.wait_ge(rstd_done, n + 1)
                pool.tensor_tensor(shift[:, :], mom[:, :, 0], rstd[:, :], ALU.mult).then_inc(shift_neg, 1)
                settle(pool, passed, (shift_neg, n + 1))
                pool.tensor_scalar(shift[:, :], shift[:, :], -1.0, None, ALU.mult).then_inc(shift_done, 1)

            def prep_rows(n, par):
                waits = [(shift_done, n + 1), (xn_done, n + 1)]
                if not is_first(n):
                    waits.append((pb_ready, ready(use_turn(n - 1, KD - 1))))
                settle(pool, passed, *waits)
                for t in range(JT):
                    ins = pool.tensor_scalar(xc[:, t, :], ctx[:, par, t, :], rstd[0:JP, t:t + 1], shift[0:JP, t:t + 1],
                                             ALU.mult, ALU.add)
                ins.then_inc(xc_done, 1)

            def split_x(n, par):
                settle(pool, passed, (xt_turned, n + 1))
                pool.tensor_copy(xt_hi[:, par, :, :], xt32[:, :, :]).then_inc(xt_hi_done, 1)
                pool.wait_ge(xt_hi_done, n + 1)
                pool.tensor_tensor(xt_lo[:, par, :, :], xt32[:, :, :], xt_hi[:, par, :, :], ALU.subtract).then_inc(xt_done, 1)

            def split_ctx(n, par, k):
                use = use_turn(n, k)
                settle(pool, passed, (pb_free[use[1] % NPB], freed(use)))
                pool.tensor_copy(cn_hi[:, par, k, 0:S2], cn32[:, k, :]).then_inc(cn_hi_done, 1)
                pool.wait_ge(cn_hi_done, KD * n + k + 1)
                pool.tensor_tensor(cn_lo[:, par, k, 0:S2], cn32[:, k, :], cn_hi[:, par, k, 0:S2], ALU.subtract).then_inc(cn_done, 1)

            def residual_rstd(b):
                settle(pool, passed, (z_mom_done, b + 1))
                pool.tensor_scalar(z_rstd[:, :], z_mom[:, 1:2], EPS, None, ALU.add).then_inc(z_eps, 1)
                pool.wait_ge(z_eps, b + 1)
                pool.tensor_tensor(z_rstd[:, :], z_rstd[:, :], half_neg[0:T, 0:1], ALU.pow).then_inc(z_rstd_done, 1)

            def normalise(b, h):
                settle(pool, passed, (p_sum_rec, H * b + h + 1), (t_ready, H * b + h - 3))
                pool.tensor_scalar(p_norm[:, h % 4, :], p32[:, h % 4, :], p_rec[:, h % 4:h % 4 + 1], 0.0, ALU.mult,
                                   ALU.add).then_inc(p_norm_done, 1)

            def body(b, par):
                for s in range(H):
                    normalise(b, s)
                    if s == 0 and not is_last(b):
                        mask(b + 1, 1 - par)
                    if s == 5 and not is_first(b):
                        residual_rstd(b - 1)
                    if has_prep(b):
                        if s == 6:
                            prep_rstd(b + 2)
                        if s == 8:
                            prep_rows(b + 2, par)
                        if s == 12:
                            split_x(b + 2, par)
                        if s - 2 in TURN_AT:
                            split_ctx(b + 2, par, TURN_AT.index(s - 2))

            def half_of(n):
                return n // 2 if isinstance(n, int) else halves[par_of[0]]

            halves, par_of = [None, None], [0]
            pool.memset(mom[:, :, :], 1.0).then_inc(stats_zeroed, 1)
            pool.memset(qz_hi[:, :, :, :], 0.0).then_inc(zeroed, 1)
            pool.memset(qz_lo[:, :, :, :], 0.0).then_inc(zeroed, 1)
            mask(0, 0)
            for n in range(2):
                prep_rstd(n)
                prep_rows(n, n)
                split_x(n, n)
                for k in range(KD):
                    split_ctx(n, n, k)
            body(0, 0)
            body(1, 1)
            with pool.Fori(1, B // 2 - 1) as i:
                halves[0], halves[1] = i + 1, i
                for par in range(2):
                    par_of[0] = 1 - par
                    body(2 * i + par, par)
            body(B - 2, 0)
            body(B - 1, 1)
            residual_rstd(B - 1)


def load_layer2(nc, a, hi, lo, vectors, sb_in, sem):
    stack = ExitStack()
    with stack:
        sb = sb_in(stack)
        NST = 3
        stage = [sb(f"b_stage{i}", [P, WCOLS], F32) for i in range(NST)]
        loaded = [sem(f"b_loaded{i}") for i in range(NST)]
        hi_done, lo_done, vec_loaded = sem("b_whi_done"), sem("b_wlo_done"), sem("b_vec_loaded")
        rows = lambda w: w.rearrange("(k p) n -> p k n", p=P)
        wkv = a["L0_xattn_Wkv"]
        jobs = [(rows(a["L0_xattn_Wq"]), "q"), (rows(wkv[:, 0:INNER]), "k"), (rows(wkv[:, INNER:2 * INNER]), "v"),
                (rows(a["L0_xattn_Wo"]), "o")]
        block = stack.enter_context(nc.Block())

        @block.sync
        def _(sp):
            for i, (src, _) in enumerate(jobs):
                at_least(sp, lo_done, i - NST + 1)
                sp.dma_start(stage[i % NST][:, :].rearrange("p (k n) -> p k n", n=src.shape[2]), src).then_inc(loaded[i % NST], 16)
            for t, n in zip(vectors, ("norm_w", "norm_b", "ctx_norm_w", "ctx_norm_b")):
                sp.dma_start(t[:, :], a[f"L0_xattn_{n}"].rearrange("(k p) -> p k", p=P),
                             allow_slow_non_contiguous=True).then_inc(vec_loaded, 16)
            sp.wait_ge(vec_loaded, 4 * 16)

        @block.scalar
        def _(act):
            for i, (_, n) in enumerate(jobs):
                act.wait_ge(loaded[i % NST], 16 * (i // NST + 1))
                act.activation(hi[n][:, :], stage[i % NST][:, :], ACT.Identity, scale=WSCALE).then_inc(hi_done, 1)

        @block.vector
        def _(dve):
            for i, (_, n) in enumerate(jobs):
                dve.wait_ge(hi_done, i + 1)
                dve.scalar_tensor_tensor(lo[n][:, :], stage[i % NST][:, :], WSCALE, hi[n][:, :], ALU.mult,
                                         ALU.subtract).then_inc(lo_done, 1)


def layer3(nc, a, out, x_sb, ident, half_neg, passed, sb_in, psum_in, sem):
    stack = ExitStack()
    with stack:
        sb = sb_in(stack)
        wr = sb("wr", [P, KD, E], F32)
        br = sb("br", [T, E], F32)
        b1, b2 = sb("c_b1", [P, E, FF // P], F32), sb("c_b2", [P, E, KD], F32)
        rev = sb("rev", [T, E], F32)
        slot_id = sb("slot_id", [T, CAP], F32)
        earlier = sb("earlier", [T, T], F32)
        FAR = 1024.0
        probs = sb("probs", [T, B, E], F32)
        place = sb("place", [T, B, E], F32)
        gather = sb("gather", [T, B, SLOTS], F16)
        y_t = sb("y_t", [P, KD, E, ES], F32)
        w1_loaded = [sem(f"c_w1_loaded{i}") for i in range(2)]
        w2_loaded = [sem(f"c_w2_loaded{i}") for i in range(2)]

        mid = ExitStack()
        with mid:
            sbm = sb_in(mid)
            w1_raw, w2_raw = sbm("w1_raw", [P, 2, WCOLS], F32), sbm("w2_raw", [P, 2, WCOLS], F32)
            buf_hi, buf_lo = (sbm(f"buf_{n}", [P, KD, E, ES], F16) for n in ("hi", "lo"))

            def load_expert(sp, e, par):
                sp.dma_start(w1_raw[:, par, :].rearrange("p (k n) -> p k n", k=KD),
                             a["L0_ffn_W1"][bass.ds(e, 1), :, :].rearrange("a (k p) n -> p (a k) n", p=P)).then_inc(w1_loaded[par], 16)
                sp.dma_start(w2_raw[:, par, :].rearrange("p (k n) -> p k n", n=D),
                             a["L0_ffn_W2"][bass.ds(e, 1), :, :].rearrange("a (k p) n -> p (a k) n", p=P)).then_inc(w2_loaded[par], 16)

            route(nc, a, x_sb, ident, passed, wr, br, b1, b2, rev, slot_id, earlier, FAR, probs, place, load_expert, sb_in, psum_in, sem)
            dispatch(nc, x_sb, slot_id, place, gather, buf_hi, buf_lo, sb_in, psum_in, sem)
            experts(nc, passed, w1_raw, w2_raw, w1_loaded, w2_loaded, load_expert, b1, b2, buf_hi, buf_lo, y_t, sb_in, psum_in, sem)
        combine(nc, out, x_sb, ident, half_neg, passed, probs, gather, y_t, sb_in, psum_in, sem)


def route(nc, a, x_sb, ident, passed, wr, br, b1, b2, rev, slot_id, earlier, FAR, probs, place, load_expert, sb_in, psum_in, sem):
    stack = ExitStack()
    with stack:
        sb, psum = sb_in(stack), psum_in(stack)
        xs = sb("r_xs", [T, 2, G4, D], F32)
        xt = sb("r_xt", [P, 2, KD, GT], F32)
        logits = sb("logits", [T, B, E], F32)
        work = {n: sb(f"r_{n}", [T, B, E], F32) for n in ("exp", "eq", "one", "two", "left")}
        top = {n: sb(f"r_{n}", [T, B], F32) for n in ("max", "sum", "rec", "max1", "id1", "max2", "id2")}
        turn_ps = [psum(f"r_turn{i}", [P, 512]) for i in range(2 * KD)]
        logit_ps = [psum(f"r_logit{i}", [P, 512]) for i in range(2)]
        count_ps = psum("r_count", [P, 512])
        vec_loaded, const_done, xs_done, turn_ready, xt_done, logit_ready, logit_done = (
            sem(f"r_{n}") for n in ("vec_loaded", "const_done", "xs_done", "turn_ready", "xt_done", "logit_ready", "logit_done"))
        step, exp_done, count_ready = sem("r_step"), sem("r_exp_done"), sem("r_count_ready")
        block = stack.enter_context(nc.Block())

        def groups(eng, body):
            body(0, 0)
            body(1, 1)
            with eng.Fori(1, NG // 2) as i:
                for par in range(2):
                    body(2 * i + par, par)

        @block.sync
        def _(sp):
            sp.dma_start(wr[:, :, :], a["L0_ffn_Wr"].rearrange("(k p) e -> p k e", p=P)).then_inc(vec_loaded, 16)
            sp.dma_start(br[:, :], a["L0_ffn_br"].partition_broadcast(T)).then_inc(vec_loaded, 16)
            for e in range(E):
                sp.dma_start(b1[:, e, :], a["L0_ffn_b1"][e, :].rearrange("(f p) -> p f", p=P),
                             allow_slow_non_contiguous=True).then_inc(vec_loaded, 16)
                sp.dma_start(b2[:, e, :], a["L0_ffn_b2"][e, :].rearrange("(f p) -> p f", p=P),
                             allow_slow_non_contiguous=True).then_inc(vec_loaded, 16)
            for e in range(2):
                load_expert(sp, e, e)
            sp.wait_ge(vec_loaded, 16 * (2 + 2 * E))

        @block.gpsimd
        def _(pool):
            for e in range(E):
                ins = pool.memset(rev[:, e:e + 1], float(E - e))
            ins.then_inc(const_done, 1)
            for c in range(CAP):
                ins = pool.memset(slot_id[:, c:c + 1], c - FAR)
            ins.then_inc(const_done, 1)
            pool.memset(earlier[:, :], 1.0).then_inc(const_done, 1)
            pool.wait_ge(const_done, 3)
            pool.affine_select(out=earlier[:, :], in_=earlier[:, :], compare_op=ALU.is_gt, fill=0.0, base=0,
                               pattern=[[1, T]], channel_multiplier=-1).then_inc(const_done, 1)

            def body(g, par):
                settle(pool, passed, (turn_ready, g - 1))
                pool.tensor_copy(xs[:, par, :, :], x_sb[:, bass.ds(G4 * g, G4), :]).then_inc(xs_done, 1)

            groups(pool, body)

        @block.tensor
        def _(pe):
            pe.wait_ge(vec_loaded, 16 * (2 + 2 * E))

            def body(g, par):
                pe.wait_ge(xs_done, g + 1)
                at_least(pe, xt_done, g - 1)
                for k in range(KD):
                    for b in range(G4):
                        mm = pe.transpose(turn_ps[2 * par + k][:, b * T:(b + 1) * T], xs[:, par, b, k * P:(k + 1) * P], ident[0:T, 0:T])
                mm.then_inc(turn_ready, 1)
                pe.wait_ge(xt_done, g + 1)
                at_least(pe, logit_done, g - 1)
                for b in range(G4):
                    for k in range(KD):
                        mm = pe.matmul(logit_ps[par][0:T, b * E:(b + 1) * E], xt[:, par, k, b * T:(b + 1) * T], wr[:, k, :],
                                       start=(k == 0), stop=(k == KD - 1))
                mm.then_inc(logit_ready, 1)

            groups(pe, body)
            pe.wait_ge(step, 16)
            pe.wait_ge(const_done, 4)
            pe.matmul(count_ps[0:T, 0:B * E], earlier[:, :], work["left"][:, :, :].rearrange("p b e -> p (b e)"),
                      start=True, stop=True).then_inc(count_ready, 1)

        @block.scalar
        def _(act):
            def body(g, par):
                act.wait_ge(turn_ready, g + 1)
                at_least(act, logit_ready, g - 1)
                for k in range(KD):
                    ins = act.activation(xt[:, par, k, :], turn_ps[2 * par + k][:, 0:GT], ACT.Identity)
                ins.then_inc(xt_done, 1)

            groups(act, body)
            act.wait_ge(step, 2)
            act.activation(work["exp"][:, :, :], logits[:, :, :], ACT.Exp).then_inc(exp_done, 1)

        @block.vector
        def _(dve):
            dve.wait_ge(vec_loaded, 16 * (2 + 2 * E))

            def body(g, par):
                dve.wait_ge(logit_ready, g + 1)
                dve.tensor_tensor(logits[:, bass.ds(G4 * g, G4), :], logit_ps[par][0:T, 0:G4 * E].rearrange("p (b e) -> p b e", e=E),
                                  br[:, :].unsqueeze(1).to_broadcast([T, G4, E]), ALU.add).then_inc(logit_done, 1)

            groups(dve, body)
            dve.wait_ge(logit_done, NG)
            dve.wait_ge(const_done, 2)
            count = [0]

            def then(ins):
                count[0] += 1
                ins.then_inc(step, 1)
                dve.wait_ge(step, count[0])

            over = lambda t: t[:, :].unsqueeze(2).to_broadcast([T, B, E])
            revs = rev[:, :].unsqueeze(1).to_broadcast([T, B, E])
            w = {n: t[:, :, :] for n, t in work.items()}
            then(dve.tensor_reduce(top["max"][:, :], logits[:, :, :], AXX, ALU.max))
            then(dve.tensor_tensor(logits[:, :, :], logits[:, :, :], over(top["max"]), ALU.subtract))
            dve.wait_ge(exp_done, 1)
            then(dve.tensor_reduce(top["sum"][:, :], w["exp"], AXX, ALU.add))
            then(dve.reciprocal(top["rec"][:, :], top["sum"][:, :]))
            then(dve.tensor_tensor(probs[:, :, :], w["exp"], over(top["rec"]), ALU.mult))
            then(dve.tensor_reduce(top["max1"][:, :], probs[:, :, :], AXX, ALU.max))
            then(dve.tensor_tensor(w["eq"], probs[:, :, :], over(top["max1"]), ALU.is_equal))
            then(dve.tensor_tensor(w["eq"], w["eq"], revs, ALU.mult))
            then(dve.tensor_reduce(top["id1"][:, :], w["eq"], AXX, ALU.max))
            then(dve.tensor_tensor(w["one"], revs, over(top["id1"]), ALU.is_equal))
            then(dve.scalar_tensor_tensor(w["left"], w["one"], -4.0, probs[:, :, :], ALU.mult, ALU.add))
            then(dve.tensor_reduce(top["max2"][:, :], w["left"], AXX, ALU.max))
            then(dve.tensor_tensor(w["eq"], w["left"], over(top["max2"]), ALU.is_equal))
            then(dve.tensor_tensor(w["eq"], w["eq"], revs, ALU.mult))
            then(dve.tensor_reduce(top["id2"][:, :], w["eq"], AXX, ALU.max))
            dve.tensor_tensor(w["two"], revs, over(top["id2"]), ALU.is_equal).then_inc(exp_done, 1)
            dve.wait_ge(exp_done, 2)
            then(dve.tensor_tensor(w["left"], w["one"], w["two"], ALU.add))
            dve.wait_ge(count_ready, 1)
            dve.scalar_tensor_tensor(place[:, :, :].rearrange("p b e -> p (b e)"), w["left"].rearrange("p b e -> p (b e)"), -FAR,
                                     count_ps[0:T, 0:B * E], ALU.mult, ALU.add).then_inc(step, 1)


def dispatch(nc, x_sb, slot_id, place, gather, buf_hi, buf_lo, sb_in, psum_in, sem):
    stack = ExitStack()
    with stack:
        sb, psum = sb_in(stack), psum_in(stack)
        x_hi, x_lo = (sb(f"d_x_{n}", [T, 2, G4, D], F16) for n in ("hi", "lo"))
        hi_ps = [psum(f"d_hi{i}", [P, 512]) for i in range(G4)]
        lo_ps = [psum(f"d_lo{i}", [P, 512]) for i in range(G4)]
        gather_done, x_hi_done, x_lo_done, hi_ready, lo_ready, hi_done, lo_done = (
            sem(f"d_{n}") for n in ("gather_done", "x_hi_done", "x_lo_done", "hi_ready", "lo_ready", "hi_done", "lo_done"))
        block = stack.enter_context(nc.Block())

        def groups(eng, body):
            body(0, 0)
            body(1, 1)
            with eng.Fori(1, NG // 2) as i:
                for par in range(2):
                    body(2 * i + par, par)

        def slots_of(buf, b):
            return buf[:, :, :, bass.ds(b * CAP, CAP)]

        @block.scalar
        def _(act):
            def split(g, par):
                at_least(act, lo_ready, G4 * (g - 1))
                act.activation(x_hi[:, par, :, :], x_sb[:, bass.ds(G4 * g, G4), :], ACT.Identity).then_inc(x_hi_done, 1)

            def body(g, par):
                split(g, par)
                for b in range(G4):
                    act.wait_ge(hi_ready, G4 * g + b + 1)
                    act.activation(slots_of(buf_hi, G4 * g + b), hi_ps[b][:, 0:KD * SLOTS].rearrange("p (k e c) -> p k e c", k=KD, e=E),
                                   ACT.Identity).then_inc(hi_done, 1)

            groups(act, body)

        @block.vector
        def _(dve):
            def body(g, par):
                at_b = bass.ds(G4 * g, G4)
                dve.tensor_tensor(gather[:, at_b, :].rearrange("p b (e c) -> p (b e) c", c=CAP),
                                  place[:, at_b, :].rearrange("p b e -> p (b e)").unsqueeze(2).to_broadcast([T, G4 * E, CAP]),
                                  slot_id[:, :].unsqueeze(1).to_broadcast([T, G4 * E, CAP]), ALU.is_equal).then_inc(gather_done, 1)
                dve.wait_ge(x_hi_done, g + 1)
                at_least(dve, lo_ready, G4 * (g - 1))
                dve.tensor_tensor(x_lo[:, par, :, :], x_sb[:, at_b, :], x_hi[:, par, :, :], ALU.subtract).then_inc(x_lo_done, 1)
                for b in range(G4):
                    dve.wait_ge(lo_ready, G4 * g + b + 1)
                    dve.tensor_copy(slots_of(buf_lo, G4 * g + b),
                                    lo_ps[b][:, 0:KD * SLOTS].rearrange("p (k e c) -> p k e c", k=KD, e=E)).then_inc(lo_done, 1)

            groups(dve, body)

        @block.tensor
        def _(pe):
            def body(g, par):
                pe.wait_ge(gather_done, g + 1)
                pe.wait_ge(x_lo_done, g + 1)
                for b in range(G4):
                    at_least(pe, hi_done, G4 * (g - 1) + b + 1)
                    at_least(pe, lo_done, G4 * (g - 1) + b + 1)
                    for src, ps, done in ((x_hi, hi_ps, hi_ready), (x_lo, lo_ps, lo_ready)):
                        for k in range(KD):
                            mm = pe.matmul(ps[b][:, k * SLOTS:(k + 1) * SLOTS], src[:, par, b, k * P:(k + 1) * P],
                                           gather[:, bass.ds(G4 * g + b, 1), :].rearrange("p a s -> p (a s)"), start=True, stop=True)
                        mm.then_inc(done, 1)

            groups(pe, body)


def experts(nc, passed, w1_raw, w2_raw, w1_loaded, w2_loaded, load_expert, b1, b2, buf_hi, buf_lo, y_t, sb_in, psum_in, sem):
    stack = ExitStack()
    with stack:
        sb, psum = sb_in(stack), psum_in(stack)
        FT, HALF = FF // P, ES // 2
        w1_hi, w1_lo, w2_hi, w2_lo = (sb(f"e_{n}", [P, 2, WCOLS], F16) for n in ("w1_hi", "w1_lo", "w2_hi", "w2_lo"))
        h_hi, h_lo = (sb(f"e_h_{n}", [P, FT, ES], F16) for n in ("hi", "lo"))
        r32 = sb("r32", [P, 2, ES], F32)
        NPB = 4
        pb = [psum(f"e_pb{i}", [P, 2, 512]) for i in range(NPB)]
        USES = FT + KD
        pb_ready = sem("e_pb_ready")
        pb_free = [sem(f"e_pb_free{i}") for i in range(NPB)]
        w_hi_done, w_lo_done, relu_done, h_hi_done, h_lo_done = (
            sem(f"e_{n}") for n in ("w_hi_done", "w_lo_done", "relu_done", "h_hi_done", "h_lo_done"))
        block = stack.enter_context(nc.Block())

        def each(eng, body):
            for par in range(2):
                body(0, par)
            with eng.Fori(1, E // 2 - 1) as i:
                for par in range(2):
                    body(i, par)
            for par in range(2):
                body(E // 2 - 1, par)

        def is_last(i, par):
            return isinstance(i, int) and i == E // 2 - 1 and par == 1

        def ready(i, par, use):
            return 2 * USES * i + USES * par + use + 1

        def freed(i, par, use):
            return 2 * USES // NPB * i + (USES * par + use) // NPB + 1

        def bank(par, use):
            return (USES * par + use) % NPB

        def of_expert(t, k, e):
            return t[:, k, bass.ds(e, 1), :].rearrange("p a n -> p (a n)")

        @block.sync
        def _(sp):
            def load(i, par):
                settle(sp, passed, (w_lo_done, 2 * (2 * i + par - 2) + 2))
                load_expert(sp, 2 * i + par, par)

            for par in range(2):
                load(1, par)
            with sp.Fori(2, E // 2) as i:
                for par in range(2):
                    load(i, par)

        def next_expert(i, par):
            return (i, 1) if par == 0 else (i + 1, 0)

        @block.scalar
        def _(act):
            def split(i, par, which):
                raw, loaded, hi = ((w1_raw, w1_loaded, w1_hi), (w2_raw, w2_loaded, w2_hi))[which]
                act.wait_ge(loaded[par], 16 * (i + 1))
                if not (isinstance(i, int) and i == 0):
                    act.wait_ge(pb_ready, ready(i - 1, par, (FT, USES)[which] - 1))
                act.activation(hi[:, par, :], raw[:, par, :], ACT.Identity, scale=WSCALE).then_inc(w_hi_done, 1)

            def body(i, par):
                e = 2 * i + par
                for f in range(FT):
                    act.wait_ge(pb_ready, ready(i, par, f))
                    at_least(act, h_lo_done, FT * e + f - 1)
                    act.activation(r32[:, f % 2, :].rearrange("p (a n) -> p a n", a=2), pb[bank(par, f)][:, :, 0:HALF], ACT.Relu,
                                   bias=b1[:, bass.ds(e, 1), f], scale=UNSCALE).then_inc(pb_free[bank(par, f)], 1)
                    if f in (1, 4) and not is_last(i, par):
                        split(*next_expert(i, par), (1, 4).index(f))
                for c in range(KD):
                    use = FT + c
                    act.wait_ge(pb_ready, ready(i, par, use))
                    act.activation(of_expert(y_t, c, e).rearrange("p (a n) -> p a n", a=2), pb[bank(par, use)][:, :, 0:HALF],
                                   ACT.Identity, bias=b2[:, bass.ds(e, 1), c], scale=UNSCALE).then_inc(pb_free[bank(par, use)], 1)

            for which in range(2):
                split(0, 0, which)
            each(act, body)

        @block.vector
        def _(dve):
            def split(i, par, which):
                raw, hi, lo = ((w1_raw, w1_hi, w1_lo), (w2_raw, w2_hi, w2_lo))[which]
                dve.wait_ge(w_hi_done, 2 * (2 * i + par) + which + 1)
                dve.scalar_tensor_tensor(lo[:, par, :], raw[:, par, :], WSCALE, hi[:, par, :], ALU.mult,
                                         ALU.subtract).then_inc(w_lo_done, 1)

            def body(i, par):
                e = 2 * i + par
                for f in range(FT):
                    dve.wait_ge(h_hi_done, FT * e + f + 1)
                    dve.tensor_tensor(h_lo[:, f, :], r32[:, f % 2, :], h_hi[:, f, :], ALU.subtract).then_inc(h_lo_done, 1)
                    if f in (1, 4) and not is_last(i, par):
                        split(*next_expert(i, par), (1, 4).index(f))

            for which in range(2):
                split(0, 0, which)
            each(dve, body)

        @block.gpsimd
        def _(pool):
            def body(i, par):
                e = 2 * i + par
                if par == 1:
                    pool.wait_ge(pb_ready, ready(i, 0, USES - 1))
                elif not (isinstance(i, int) and i == 0):
                    pool.wait_ge(pb_ready, ready(i - 1, 1, USES - 1))
                for f in range(FT):
                    settle(pool, passed, (pb_free[bank(par, f)], freed(i, par, f)))
                    pool.tensor_copy(h_hi[:, f, :], r32[:, f % 2, :]).then_inc(h_hi_done, 1)

            each(pool, body)

        @block.tensor
        def _(pe):
            def claim(i, par, use):
                at_least(pe, pb_free[bank(par, use)], freed(i, par, use) - 1)
                return pb[bank(par, use)]

            def body(i, par):
                e = 2 * i + par
                pe.wait_ge(w_lo_done, 2 * e + 1)
                for f in range(FT):
                    ps = claim(i, par, f)
                    for n in range(2):
                        cols = slice(n * HALF, (n + 1) * HALF)
                        for k in range(KD):
                            c0 = k * FF + f * P
                            mm = split_product(pe, ps[:, n, 0:HALF], (w1_hi[:, par, c0:c0 + P], w1_lo[:, par, c0:c0 + P]),
                                               (of_expert(buf_hi, k, e)[:, cols], of_expert(buf_lo, k, e)[:, cols]),
                                               k == 0, k == KD - 1)
                    mm.then_inc(pb_ready, 1)
                pe.wait_ge(w_lo_done, 2 * e + 2)
                for c in range(KD):
                    ps = claim(i, par, FT + c)
                    for n in range(2):
                        cols = slice(n * HALF, (n + 1) * HALF)
                        for f in range(FT):
                            if c == 0 and n == 0:
                                pe.wait_ge(h_lo_done, FT * e + f + 1)
                            c0 = f * D + c * P
                            mm = split_product(pe, ps[:, n, 0:HALF], (w2_hi[:, par, c0:c0 + P], w2_lo[:, par, c0:c0 + P]),
                                               (h_hi[:, f, cols], h_lo[:, f, cols]), f == 0, f == FT - 1)
                    mm.then_inc(pb_ready, 1)

            each(pe, body)


def combine(nc, out, x_sb, ident, half_neg, passed, probs, gather, y_t, sb_in, psum_in, sem):
    stack = ExitStack()
    with stack:
        sb, psum = sb_in(stack), psum_in(stack)
        HS = SLOTS // 2
        yb = sb("yb", [P, 2, KD, SLOTS], F32)
        gw = sb("gw", [T, 2, SLOTS], F32)
        gw_t = sb("gw_t", [HS, 2, 2 * T], F32)
        y_n = sb("y_n", [HS, 2, 2 * D], F32)
        z = sb("c_z", [T, 2, G4, D], F32)
        zo = sb("c_zo", [T, 2, G4, D], F32)
        stats, mom, rstd = sb("c_stats", [T, G4, 6], F32), sb("c_mom", [T, G4, 2], F32), sb("c_rstd", [T, G4], F32)
        g_ps = [psum(f"c_g{i}", [P, 512]) for i in range(2)]
        y_ps = [psum(f"c_y{i}", [P, 512]) for i in range(2)]
        o_ps = [psum(f"c_o{i}", [P, 512]) for i in range(2)]
        yb_done, gw_done, g_ready, y_ready, gw_t_done, y_n_done, o_ready, z_done = (
            sem(f"c_{n}") for n in ("yb_done", "gw_done", "g_ready", "y_ready", "gw_t_done", "y_n_done", "o_ready", "z_done"))
        stats_done, mom_done, eps_done, rstd_done, zo_done = (
            sem(f"c_{n}") for n in ("stats_done", "mom_done", "eps_done", "rstd_done", "zo_done"))
        stored = [sem(f"c_stored{i}") for i in range(2)]
        block = stack.enter_context(nc.Block())

        def groups(eng, body):
            body(0, 0)
            body(1, 1)
            with eng.Fori(1, NG // 2) as i:
                for par in range(2):
                    body(2 * i + par, par)

        @block.gpsimd
        def _(pool):
            def copies(g):
                for q in range(G4):
                    b = G4 * g + q
                    settle(pool, passed, (y_ready, b - 1))
                    pool.tensor_copy(yb[:, q % 2, :, :].rearrange("p k (e c) -> p k e c", c=CAP),
                                     y_t[:, :, :, bass.ds(b * CAP, CAP)]).then_inc(yb_done, 1)

            def body(g, par):
                copies(g)
                settle(pool, passed, (mom_done, g + 1))
                pool.tensor_scalar(rstd[:, :], mom[:, :, 1], EPS, None, ALU.add).then_inc(eps_done, 1)
                pool.wait_ge(eps_done, g + 1)
                pool.tensor_tensor(rstd[:, :], rstd[:, :], half_neg[0:T, :], ALU.pow).then_inc(rstd_done, 1)

            groups(pool, body)

        @block.vector
        def _(dve):
            def weights(b, q):
                at_least(dve, g_ready, b - 1)
                dve.tensor_tensor(gw[:, q % 2, :].rearrange("p (e c) -> p e c", c=CAP),
                                  gather[:, bass.ds(b, 1), :].rearrange("p a (e c) -> p (a e) c", c=CAP),
                                  probs[:, bass.ds(b, 1), :].rearrange("p a e -> p (a e)").unsqueeze(2).to_broadcast([T, E, CAP]),
                                  ALU.mult).then_inc(gw_done, 1)

            def body(g, par):
                for q in range(G4 + 1):
                    if q < G4:
                        weights(G4 * g + q, q)
                    if q >= 1:
                        b = G4 * g + q - 1
                        dve.wait_ge(o_ready, b + 1)
                        if q == 1:
                            at_least(dve, zo_done, g - 1)
                        dve.tensor_tensor(z[:, par, q - 1, :], o_ps[(q - 1) % 2][0:T, 0:D],
                                          x_sb[:, bass.ds(b, 1), :].rearrange("p a d -> p (a d)"), ALU.add).then_inc(z_done, 1)
                dve.wait_ge(z_done, G4 * (g + 1))
                at_least(dve, mom_done, g)
                for q in range(G4):
                    ins = dve.bn_stats(stats[:, q, :], z[:, par, q, :])
                ins.then_inc(stats_done, 1)
                settle(dve, passed, (stats_done, g + 1), (zo_done, g))
                for q in range(G4):
                    ins = dve.bn_aggr(mom[:, q, :], stats[:, q, :])
                ins.then_inc(mom_done, 1)
                dve.wait_ge(rstd_done, g + 1)
                if not (isinstance(g, int) and g < 2):
                    dve.wait_ge(stored[par], stored_before(g))
                for q in range(G4):
                    ins = dve.tensor_scalar(zo[:, par, q, :], z[:, par, q, :], mom[:, q, 0:1], rstd[:, q:q + 1], ALU.subtract, ALU.mult)
                ins.then_inc(zo_done, 1)

            pairs = [None]

            def stored_before(g):
                return 16 * pairs[0]

            body(0, 0)
            body(1, 1)
            with dve.Fori(1, NG // 2) as i:
                pairs[0] = i
                for par in range(2):
                    body(2 * i + par, par)

        @block.scalar
        def _(act):
            def body(g, par):
                for q in range(G4):
                    b = G4 * g + q
                    act.wait_ge(g_ready, b + 1)
                    at_least(act, o_ready, b - 1)
                    act.activation(gw_t[:, q % 2, :], g_ps[q % 2][0:HS, 0:2 * T], ACT.Identity).then_inc(gw_t_done, 1)
                    act.wait_ge(y_ready, b + 1)
                    act.activation(y_n[:, q % 2, :], y_ps[q % 2][0:HS, :], ACT.Identity).then_inc(y_n_done, 1)

            groups(act, body)

        @block.tensor
        def _(pe):
            def turn(b, q):
                pe.wait_ge(gw_done, b + 1)
                at_least(pe, gw_t_done, b - 1)
                for s in range(2):
                    mm = pe.transpose(g_ps[q % 2][0:HS, s * T:(s + 1) * T], gw[:, q % 2, s * HS:(s + 1) * HS], ident[0:T, 0:T])
                mm.then_inc(g_ready, 1)
                pe.wait_ge(yb_done, b + 1)
                at_least(pe, y_n_done, b - 1)
                for s in range(2):
                    for k in range(KD):
                        mm = pe.transpose(y_ps[q % 2][0:HS, s * D + k * P:s * D + (k + 1) * P],
                                          yb[:, q % 2, k, s * HS:(s + 1) * HS], ident[:, :])
                mm.then_inc(y_ready, 1)

            def bring_back(b, q):
                pe.wait_ge(gw_t_done, b + 1)
                pe.wait_ge(y_n_done, b + 1)
                at_least(pe, z_done, b - 1)
                for s in range(2):
                    mm = pe.matmul(o_ps[q % 2][0:T, 0:D], gw_t[:, q % 2, s * T:(s + 1) * T], y_n[:, q % 2, s * D:(s + 1) * D],
                                   start=(s == 0), stop=(s == 1))
                mm.then_inc(o_ready, 1)

            def body(g, par):
                for q in range(G4 + 1):
                    if q < G4:
                        turn(G4 * g + q, q)
                    if q >= 1:
                        bring_back(G4 * g + q - 1, q - 1)

            groups(pe, body)

        @block.sync
        def _(sp):
            def body(g, par):
                sp.wait_ge(zo_done, g + 1)
                sp.dma_start(out[bass.ds(G4 * g, G4), :, :].rearrange("b t d -> t b d"), zo[:, par, :, :]).then_inc(stored[par], 16)

            groups(sp, body)
            for par in range(2):
                sp.wait_ge(stored[par], 16 * NG // 2)


_INS = ['x', 'ctx_1024', 'mask_BxS2_bf1', 'L0_attn_wq', 'L0_attn_wk', 'L0_attn_wv', 'L0_attn_wo', 'L0_attn_proj',
        'L0_attn_w1', 'L0_attn_b1', 'L0_attn_w2', 'L0_attn_b2', 'L0_attn_g1', 'L0_attn_beta1', 'L0_attn_g2',
        'L0_attn_beta2', 'L0_xattn_norm_w', 'L0_xattn_norm_b', 'L0_xattn_ctx_norm_w', 'L0_xattn_ctx_norm_b',
        'L0_xattn_Wq', 'L0_xattn_Wkv', 'L0_xattn_Wo', 'L0_ffn_Wr', 'L0_ffn_br', 'L0_ffn_W1', 'L0_ffn_b1',
        'L0_ffn_W2', 'L0_ffn_b2']


def kernel(**inputs):
    import numpy as _np
    import concourse.bacc as _bacc
    from concourse.bass_utils import run_bass_kernel_spmd as _run

    nc = _bacc.Bacc("TRN2", target_bir_lowering=False, num_devices=1)
    arrays, args = {}, {}
    for name in _INS:
        a = _np.ascontiguousarray(inputs[name])
        if a.dtype == _np.bool_:
            a = a.view(_np.uint8)
        arrays[f"in_{name}_dram"] = a
        args[name] = nc.dram_tensor(f"in_{name}_dram", a.shape, mybir.dt.from_np(a.dtype), kind="ExternalInput").ap()
    out = nc.dram_tensor("out_dram", (B, T, D), F32, kind="ExternalOutput").ap()
    decoder_kernel(nc, args, out)
    r = _run(nc, [arrays], core_ids=[0])
    return r.results[0]["out_dram"]
```

```python
from contextlib import ExitStack

import concourse.bass as bass
from concourse import mybir

F32 = mybir.dt.float32
F16 = mybir.dt.float16
BF16 = mybir.dt.bfloat16
U8 = mybir.dt.uint8
ALU = mybir.AluOpType
ACT = mybir.ActivationFunctionType
AXX = mybir.AxisListType.X

P = 128
B, T, D = 32, 112, 256
S2 = 375
H, DH = 16, 64
INNER = H * DH
FF = 1024
KD = D // P
KI = INNER // P
E = 8
CAP = max(1, int(T / E * 1.25))
SLOTS = E * CAP
ES = B * CAP
G4 = 4
NG = B // G4
GT = G4 * T
JT, JP = 3, S2 // 3
WSCALE = 64.0
UNSCALE = 1.0 / WSCALE
EPS = 1e-5
MASKED = 3.0e38
WCOLS = KD * INNER


def at_least(eng, sem, n):
    if isinstance(n, int) and n <= 0:
        return
    eng.wait_ge(sem, n)


def settle(eng, passed, *waits):
    for sem, n in waits:
        at_least(eng, sem, n)
    eng.sem_inc(passed, 1)


def split_product(pe, out, lhs, rhs, first, last):
    (lh, ll), (rh, rl) = lhs, rhs
    pe.matmul(out, lh, rh, start=first, stop=False)
    pe.matmul(out, lh, rl, start=False, stop=False)
    return pe.matmul(out, ll, rh, start=False, stop=last)


def decoder_kernel(nc, a, out):
    root = ExitStack()
    with root:
        def sem(name):
            return root.enter_context(nc.semaphore(name))

        def sb_in(stack):
            return lambda name, shape, dt: stack.enter_context(nc.sbuf_tensor(name, shape, dt))

        def psum_in(stack):
            return lambda name, shape, dt=F32: stack.enter_context(nc.psum_tensor(name, shape, dt))

        sb = sb_in(root)
        x_sb = sb("x_sb", [T, B, D], F32)
        ident = sb("ident", [P, P], F32)
        half_neg = sb("half_neg", [P, 4], F32)
        consts_done = sem("consts_done")
        passed = sem("passed")

        layer1(nc, a, x_sb, ident, half_neg, consts_done, passed, sb_in, psum_in, sem)
        layer2(nc, a, x_sb, ident, half_neg, passed, sb_in, psum_in, sem)
        layer3(nc, a, out, x_sb, ident, half_neg, passed, sb_in, psum_in, sem)


def layer1(nc, a, x_sb, ident, half_neg, consts_done, passed, sb_in, psum_in, sem):
    stack = ExitStack()
    with stack:
        sb, psum = sb_in(stack), psum_in(stack)
        names = ["wq", "wk", "wv", "wo", "w1", "w2"]
        hi = {n: sb(f"a_{n}_hi", [P, WCOLS], F16) for n in names}
        lo = {n: sb(f"a_{n}_lo", [P, WCOLS], F16) for n in names}
        g1, be1, g2, be2 = (sb(f"a_{n}", [P, KD], F32) for n in ("g1", "be1", "g2", "be2"))
        b1 = sb("a_b1", [P, FF // P], F32)
        b2 = sb("a_b2", [T, D], F32)
        causal = sb("causal", [T, T], F32)
        load_layer1(nc, a, x_sb, ident, half_neg, consts_done, causal, hi, lo, (g1, be1, g2, be2, b1, b2), sb_in, psum_in, sem)

        def pair(name, k, c0, n, width):
            c = k * width + c0
            return hi[name][:, c:c + n], lo[name][:, c:c + n]

        FT = FF // P
        LNS = 3
        NSM = 2
        xh = sb("xh", [T, G4, D], F32)
        h32 = sb("h32", [P, KD, GT], F32)
        h_hi, h_lo = (sb(f"h_{n}", [P, 2, KD, GT], F16) for n in ("hi", "lo"))
        neg_relu = sb("neg_relu", [P, 2, GT], F32)
        phi_exp = sb("phi_exp", [P, 2, GT], F32)
        qz = sb("qz", [P, H, GT], F32)
        kt = sb("kt", [P, KI, GT], F32)
        v1 = sb("v1", [P, G4, H, DH + 1], F32)
        sm = sb("sm", [P, NSM, 4 * T], F32)
        rec = sb("rec", [T, 2, 4], F32)
        o32 = sb("o32", [T, 4, 4 * DH], F32)
        o_hi, o_lo = (sb(f"o_{n}", [P, 2, KI, T], F16) for n in ("hi", "lo"))
        x1 = sb("x1", [T, G4, D], F32)
        xsum = sb("xsum", [T, G4, D], F32)
        gelu32 = neg_relu
        ff_hi, ff_lo = (sb(f"ff_{n}", [P, FT, GT], F16) for n in ("hi", "lo"))
        stats = sb("a_stats", [T, LNS, G4, 6], F32)
        mom = sb("a_mom", [T, LNS, G4, 2], F32)
        rstd = sb("a_rstd", [T, LNS, G4], F32)

        NPB = 4
        pb = [psum(f"a_pb{i}", [P, 512]) for i in range(NPB)]
        s_ps = [psum(f"a_s{i}", [P, 512]) for i in range(2)]
        o_ps = [psum(f"a_o{i}", [P, 512]) for i in range(2)]

        def several(kind, n):
            return [(kind, i) for i in range(n)]

        PRE = several("T1", KD) + several("Q", KI) + several("K", KI) + several("V", 2 * G4)
        UNITS = G4 * H // 4
        STEPS = UNITS + 8
        VALUES_AT, TURN_AT = 2, 4
        W_AT = 9
        T1_AT, Q_AT = 15, 20
        EARLY = 2

        def attention_uses(last):
            uses = []
            for t in range(STEPS):
                if TURN_AT <= t < UNITS + TURN_AT and (t - TURN_AT) % 2 == 0:
                    uses.append(("O", (t - TURN_AT) // 2))
                if t == T1_AT and not last:
                    uses += several("T1", KD)
                if t == Q_AT and not last:
                    uses += several("Q", EARLY)
                if t >= W_AT and (t - W_AT) % 4 == 0:
                    uses.append(("W", (t - W_AT) // 4))
            return uses

        MAIN = (attention_uses(False) + several("Q", KI)[EARLY:] + several("T2", KD) + several("K", KI)
                + several("F", FT) + several("V", 2 * G4) + several("Y", G4))
        LAST = attention_uses(True) + several("T2", KD) + several("F", FT) + several("Y", G4)
        PER = len(MAIN)
        assert PER % NPB == 0

        def use(g, kind, i):
            if kind in ("T1", "Q", "K", "V"):
                if isinstance(g, int) and g == 0:
                    return 0, PRE.index((kind, i))
                return g - 1, len(PRE) + MAIN.index((kind, i))
            return g, len(PRE) + (LAST if is_last(g) else MAIN).index((kind, i))

        def ready(u):
            return PER * u[0] + u[1] + 1

        def freed(u):
            return PER // NPB * u[0] + u[1] // NPB + 1

        def bank(u):
            return pb[u[1] % NPB]

        def free_of(u):
            return pb_free[u[1] % NPB]

        def is_first(g):
            return isinstance(g, int) and g == 0

        def is_last(g):
            return isinstance(g, int) and g == NG - 1

        def groups(eng, body):
            body(0)
            with eng.Fori(1, NG - 1) as g:
                body(g)
            body(NG - 1)

        pb_ready = sem("a_pb_ready")
        pb_free = [sem(f"a_pb_free{i}") for i in range(NPB)]
        stats_done, mom_done, eps_done, rstd_done, rows_done = (
            [sem(f"a_{n}{i}") for i in range(LNS)] for n in ("stats_done", "mom_done", "eps_done", "rstd_done", "rows_done"))
        h_hi_done = [sem(f"a_h_hi_done{i}") for i in range(2)]
        qz_zeroed, pads_done = sem("a_qz_zeroed"), sem("a_pads_done")
        relu_done, exp_done = sem("a_relu_done"), sem("a_exp_done")
        s_ready, s_masked, av_done, rec_done, o_done, o_hi_done = (
            sem(f"a_{n}") for n in ("s_ready", "s_masked", "av_done", "rec_done", "o_done", "o_hi_done"))
        xs1_done, xs_done = sem("a_xs1_done"), sem("a_xs_done")
        gelu_done, ff_hi_done = sem("a_gelu_done"), sem("a_ff_hi_done")
        block = stack.enter_context(nc.Block())

        @block.tensor
        def _(pe):
            def claim(u):
                at_least(pe, free_of(u), freed(u) - 1)
                return bank(u)

            def written(g, kind, n):
                for i in range(max(0, n - NPB), n):
                    u = use(g, kind, i)
                    pe.wait_ge(free_of(u), freed(u))

            def turn(g, ln):
                pe.wait_ge(rows_done[ln], g + 1)
                for k in range(KD):
                    ps = claim(use(g, f"T{ln + 1}", k))
                    for b in range(G4):
                        mm = pe.transpose(ps[:, b * T:(b + 1) * T], xh[:, b, k * P:(k + 1) * P], ident[0:T, 0:T])
                    mm.then_inc(pb_ready, 1)

            def from_h(g, ln, name, kind, m, width):
                ps = claim(use(g, kind, m))
                for k in range(KD):
                    mm = split_product(pe, ps[:, 0:GT], pair(name, k, m * P, P, width),
                                       (h_hi[:, ln, k, :], h_lo[:, ln, k, :]), k == 0, k == KD - 1)
                mm.then_inc(pb_ready, 1)

            def project_q(g, tiles):
                if tiles[0] == 0:
                    written(g, "T1", KD)
                for m in tiles:
                    from_h(g, 0, "wq", "Q", m, INNER)

            def project_k(g):
                for m in range(KI):
                    from_h(g, 0, "wk", "K", m, INNER)

            def project_v(g):
                for b in range(G4):
                    for n in range(2):
                        ps = claim(use(g, "V", 2 * b + n))
                        for k in range(KD):
                            lhs = (h_hi[:, 0, k, b * T:(b + 1) * T], h_lo[:, 0, k, b * T:(b + 1) * T])
                            mm = split_product(pe, ps[0:T, :], lhs, pair("wv", k, n * 512, 512, INNER), k == 0, k == KD - 1)
                        mm.then_inc(pb_ready, 1)

            def scores(g, u):
                b, quad = divmod(u, 4)
                at_least(pe, s_masked, UNITS * g + u - 1)
                for i in range(4):
                    h = 4 * quad + i
                    mm = pe.matmul(s_ps[u % 2][0:T, i * T:(i + 1) * T], kt[:, h // 2, b * T:(b + 1) * T],
                                   qz[:, h, b * T:(b + 1) * T], start=True, stop=True)
                mm.then_inc(s_ready, 1)

            def values(g, u):
                b, quad = divmod(u, 4)
                pe.wait_ge(s_masked, UNITS * g + u + 1)
                at_least(pe, o_done, UNITS * g + u - 1)
                for i in range(4):
                    mm = pe.matmul(o_ps[u % 2][0:T, i * (DH + 1):(i + 1) * (DH + 1)], sm[0:T + 1, u % NSM, i * T:(i + 1) * T],
                                   v1[0:T + 1, b, 4 * quad + i, :], start=True, stop=True)
                mm.then_inc(av_done, 1)

            def turn_output(g, u):
                pe.wait_ge(o_done, UNITS * g + u + 1)
                ps = claim(use(g, "O", u // 2)) if u % 2 == 0 else bank(use(g, "O", u // 2))
                for m in range(2):
                    c = (2 * (u % 2) + m) * T
                    mm = pe.transpose(ps[:, c:c + T], o32[:, u % 4, m * P:(m + 1) * P], ident[0:T, 0:T])
                if u % 2 == 1:
                    mm.then_inc(pb_ready, 1)

            def rows_out(u, name, lhs):
                ps = claim(u)
                for k in range(KI):
                    mm = split_product(pe, ps[0:T, 0:D], lhs(k), pair(name, k, 0, D, D), k == 0, k == KI - 1)
                mm.then_inc(pb_ready, 1)

            def body(g):
                written(g, "K", KI)
                written(g, "V", 2 * G4)
                for t in range(STEPS):
                    if t < UNITS:
                        scores(g, t)
                    if VALUES_AT <= t < UNITS + VALUES_AT:
                        values(g, t - VALUES_AT)
                    if TURN_AT <= t < UNITS + TURN_AT:
                        turn_output(g, t - TURN_AT)
                    if t == T1_AT and not is_last(g):
                        turn(g + 1, 0)
                    if t == Q_AT and not is_last(g):
                        project_q(g + 1, range(EARLY))
                    if t >= W_AT and (t - W_AT) % 4 == 0:
                        b = (t - W_AT) // 4
                        for u in (use(g, "O", 2 * b), use(g, "O", 2 * b + 1)):
                            pe.wait_ge(free_of(u), freed(u))
                        rows_out(use(g, "W", b), "wo", lambda k: (o_hi[:, b % 2, k, :], o_lo[:, b % 2, k, :]))
                if not is_last(g):
                    project_q(g + 1, range(EARLY, KI))
                turn(g, 1)
                if not is_last(g):
                    project_k(g + 1)
                written(g, "T2", KD)
                for f in range(FT):
                    from_h(g, 1, "w1", "F", f, FF)
                if not is_last(g):
                    project_v(g + 1)
                written(g, "F", FT)
                for b in range(G4):
                    rows_out(use(g, "Y", b), "w2", lambda k: (ff_hi[:, k, b * T:(b + 1) * T], ff_lo[:, k, b * T:(b + 1) * T]))

            turn(0, 0)
            project_q(0, range(KI))
            project_k(0)
            project_v(0)
            pe.wait_ge(pads_done, 3)
            groups(pe, body)

        @block.scalar
        def _(act):
            def ln_out(g, ln, gain, shift):
                for k in range(KD):
                    u = use(g, f"T{ln + 1}", k)
                    act.wait_ge(pb_ready, ready(u))
                    if ln:
                        last = use(g - 1, "T2", k) if is_last(g) else use(g + 1, "T1", k)
                    elif isinstance(g, int):
                        last = use(0, "T1", k) if g == 1 else None
                    else:
                        last = use(g - 2, "T2", k)
                    if last:
                        act.wait_ge(free_of(last), freed(last))
                    ps = bank(u)[:, 0:GT]
                    act.activation(h32[:, k, :], ps, ACT.Identity, bias=shift[:, k:k + 1], scale=gain[:, k:k + 1])
                    act.activation(h_hi[:, ln, k, :], ps, ACT.Identity, bias=shift[:, k:k + 1],
                                   scale=gain[:, k:k + 1]).then_inc(h_hi_done[ln], 1)

            def phi(g, kind):
                first = 2 * KI * g + (KI if kind == "K" else 0)
                for i in range(KI + 1):
                    if i < KI:
                        act.wait_ge(pb_ready, ready(use(g, kind, i)))
                        at_least(act, exp_done, first + i - 1)
                        act.activation(neg_relu[:, i % 2, :], bank(use(g, kind, i))[:, 0:GT], ACT.Relu,
                                       scale=-1.0).then_inc(relu_done, 1)
                    if i >= 1:
                        j = i - 1
                        act.wait_ge(relu_done, first + j + 1)
                        if j >= 2 or kind == "K":
                            last = use(g, kind, j - 2) if j >= 2 else use(g, "Q", KI + j - 2)
                            act.wait_ge(free_of(last), freed(last))
                        act.activation(phi_exp[:, j % 2, :], neg_relu[:, j % 2, :], ACT.Exp, scale=-1.0).then_inc(exp_done, 1)

            def take_v(g):
                for i in range(2 * G4):
                    u = use(g, "V", i)
                    b, n = divmod(i, 2)
                    act.wait_ge(pb_ready, ready(u))
                    act.activation(v1[0:T, b, 8 * n:8 * n + 8, 0:DH], bank(u)[0:T, :].rearrange("p (h d) -> p h d", d=DH),
                                   ACT.Identity, scale=UNSCALE).then_inc(free_of(u), 1)

            def out_high(g, j):
                b, half = divmod(j, 2)
                u = use(g, "O", j)
                act.wait_ge(pb_ready, ready(u))
                if half == 0 and b >= 2:
                    act.wait_ge(pb_ready, ready(use(g, "W", b - 2)))
                act.activation(o_hi[:, b % 2, 4 * half:4 * half + 4, :], bank(u)[:, 0:4 * T].rearrange("p (m t) -> p m t", t=T),
                               ACT.Identity).then_inc(o_hi_done, 1)

            def body(g):
                for t in range(STEPS):
                    if TURN_AT <= t < UNITS + TURN_AT and (t - TURN_AT) % 2 == 1:
                        out_high(g, (t - TURN_AT) // 2)
                    if t == T1_AT + 1 and not is_last(g):
                        ln_out(g + 1, 0, g1, be1)
                if not is_last(g):
                    phi(g + 1, "Q")
                ln_out(g, 1, g2, be2)
                if not is_last(g):
                    phi(g + 1, "K")
                    act.wait_ge(exp_done, 2 * KI * (g + 2))
                for f in range(FT):
                    act.wait_ge(pb_ready, ready(use(g, "F", f)))
                    at_least(act, ff_lo_count(g, f)[0], ff_lo_count(g, f)[1])
                    act.activation(gelu32[:, f % 2, :], bank(use(g, "F", f))[:, 0:GT], ACT.Gelu, bias=b1[:, f:f + 1],
                                   scale=UNSCALE).then_inc(gelu_done, 1)
                if not is_last(g):
                    take_v(g + 1)

            def ff_lo_count(g, f):
                u = use(g, "F", max(f - 2, 0))
                return free_of(u), freed(u) if f >= 2 else 0

            ln_out(0, 0, g1, be1)
            phi(0, "Q")
            phi(0, "K")
            act.wait_ge(pads_done, 3)
            take_v(0)
            groups(act, body)

        @block.vector
        def _(dve):
            def ln_stats(ln, b, rows):
                return dve.bn_stats(stats[:, ln, b, :], rows(b))

            def ln_moments(g, ln):
                settle(dve, passed, (stats_done[ln], G4 * (g + 1)))
                for b in range(G4):
                    ins = dve.bn_aggr(mom[:, ln, b, :], stats[:, ln, b, :])
                ins.then_inc(mom_done[ln], 1)

            def ln_rows(g, ln, b, rows, dst):
                if b == 0:
                    dve.wait_ge(rstd_done[ln], g + 1)
                ins = dve.tensor_scalar(dst(b), rows(b), mom[:, ln, b, 0:1], rstd[:, ln, b:b + 1], ALU.subtract, ALU.mult)
                if b == G4 - 1:
                    ins.then_inc(rows_done[ln], 1)

            def ln_low(g, ln):
                for k in range(KD):
                    u = use(g, f"T{ln + 1}", k)
                    dve.wait_ge(h_hi_done[ln], KD * g + k + 1)
                    dve.tensor_tensor(h_lo[:, ln, k, :], h32[:, k, :], h_hi[:, ln, k, :], ALU.subtract).then_inc(free_of(u), 1)

            def phi(g, kind, i):
                u = use(g, kind, i)
                ps = bank(u)
                dve.wait_ge(exp_done, 2 * KI * g + (KI if kind == "K" else 0) + i + 1)
                if kind == "Q":
                    for r in range(2):
                        rows = slice(DH * r, DH * (r + 1))
                        ins = dve.scalar_tensor_tensor(qz[rows, 2 * i + r, :], ps[rows, 0:GT], 0.0, phi_exp[rows, i % 2, :],
                                                       ALU.max, ALU.add)
                else:
                    ins = dve.scalar_tensor_tensor(kt[:, i, :], ps[:, 0:GT], 0.0, phi_exp[:, i % 2, :], ALU.max, ALU.add)
                ins.then_inc(free_of(u), 1)

            def mask(g, u):
                dve.wait_ge(s_ready, UNITS * g + u + 1)
                at_least(dve, av_done, UNITS * g + u + 1 - NSM)
                dve.tensor_tensor(sm[0:T, u % NSM, :].rearrange("p (i t) -> p i t", t=T),
                                  s_ps[u % 2][0:T, 0:4 * T].rearrange("p (i t) -> p i t", t=T),
                                  causal[:, :].unsqueeze(1).to_broadcast([T, 4, T]), ALU.mult).then_inc(s_masked, 1)

            def divide(g, u):
                ps = o_ps[u % 2][0:T, 0:4 * (DH + 1)].rearrange("p (i d) -> p i d", d=DH + 1)
                dve.wait_ge(av_done, UNITS * g + u + 1)
                at_least(dve, o_done, UNITS * g + u - 1)
                dve.reciprocal(rec[:, u % 2, :], ps[:, :, DH]).then_inc(rec_done, 1)
                dve.wait_ge(rec_done, UNITS * g + u + 1)
                if u >= 4:
                    dve.wait_ge(pb_ready, ready(use(g, "O", u // 2 - 2)))
                dve.tensor_tensor(o32[:, u % 4, :].rearrange("p (i d) -> p i d", d=DH), ps[:, :, 0:DH],
                                  rec[:, u % 2, :].unsqueeze(2).to_broadcast([T, 4, DH]), ALU.mult).then_inc(o_done, 1)

            def out_low(g, j):
                b, half = divmod(j, 2)
                u = use(g, "O", j)
                dve.wait_ge(o_hi_done, UNITS // 2 * g + j + 1)
                dve.tensor_tensor(o_lo[:, b % 2, 4 * half:4 * half + 4, :], bank(u)[:, 0:4 * T].rearrange("p (m t) -> p m t", t=T),
                                  o_hi[:, b % 2, 4 * half:4 * half + 4, :], ALU.subtract).then_inc(free_of(u), 1)

            def x_rows(g):
                return lambda b: x_sb[:, bass.ds(G4 * g + b, 1), :].rearrange("p a d -> p (a d)")

            x1_rows = lambda b: x1[:, b, :]
            xh_rows = lambda b: xh[:, b, :]
            sum_rows = lambda b: xsum[:, b, :]

            def body(g):
                for t in range(STEPS):
                    if 3 <= t < UNITS + 3:
                        divide(g, t - 3)
                    if t < UNITS:
                        mask(g, t)
                    if TURN_AT < t <= UNITS + TURN_AT and (t - TURN_AT) % 2 == 0:
                        out_low(g, (t - TURN_AT) // 2 - 1)
                    if not is_first(g):
                        if t < G4:
                            ln_stats(2, t, sum_rows).then_inc(stats_done[2], 1)
                        if t == 4:
                            ln_moments(g - 1, 2)
                        if 6 <= t < 10:
                            ln_rows(g - 1, 2, t - 6, sum_rows, x_rows(g - 1))
                    if not is_last(g):
                        if 4 <= t < 8:
                            ln_stats(0, t - 4, x_rows(g + 1)).then_inc(stats_done[0], 1)
                        if t == 8:
                            ln_moments(g + 1, 0)
                        if 10 <= t < 14:
                            ln_rows(g + 1, 0, t - 10, x_rows(g + 1), xh_rows)
                        if t == T1_AT + 2:
                            ln_low(g + 1, 0)
                    if t >= W_AT + 1 and (t - W_AT - 1) % 4 == 0:
                        b = (t - W_AT - 1) // 4
                        u = use(g, "W", b)
                        dve.wait_ge(pb_ready, ready(u))
                        at_least(dve, xs1_done, g)
                        dve.scalar_tensor_tensor(x1[:, b, :], bank(u)[0:T, 0:D], UNSCALE, x_rows(g)(b),
                                                 ALU.mult, ALU.add).then_inc(free_of(u), 1)
                    if t >= W_AT + 2 and (t - W_AT - 2) % 4 == 0:
                        b = (t - W_AT - 2) // 4
                        u = use(g, "W", b)
                        dve.wait_ge(free_of(u), freed(u))
                        ln_stats(1, b, x1_rows).then_inc(stats_done[1], 1)
                ln_moments(g, 1)
                if not is_last(g):
                    for i in range(2):
                        phi(g + 1, "Q", i)
                for b in range(G4):
                    ln_rows(g, 1, b, x1_rows, xh_rows)
                if not is_last(g):
                    for i in range(2, KI):
                        phi(g + 1, "Q", i)
                ln_low(g, 1)
                if not is_last(g):
                    for i in range(KI):
                        phi(g + 1, "K", i)
                for f in range(FT):
                    u = use(g, "F", f)
                    dve.wait_ge(gelu_done, FT * g + f + 1)
                    dve.tensor_copy(ff_hi[:, f, :], gelu32[:, f % 2, :]).then_inc(ff_hi_done, 1)
                    dve.wait_ge(ff_hi_done, FT * g + f + 1)
                    dve.tensor_tensor(ff_lo[:, f, :], gelu32[:, f % 2, :], ff_hi[:, f, :], ALU.subtract).then_inc(free_of(u), 1)
                dve.wait_ge(xs_done, g + 1)
                for b in range(G4):
                    u = use(g, "Y", b)
                    dve.wait_ge(pb_ready, ready(u))
                    dve.scalar_tensor_tensor(xsum[:, b, :], bank(u)[0:T, 0:D], UNSCALE, xsum[:, b, :],
                                             ALU.mult, ALU.add).then_inc(free_of(u), 1)
                for b in range(G4):
                    u = use(g, "Y", b)
                    dve.wait_ge(free_of(u), freed(u))

            for b in range(G4):
                ln_stats(0, b, x_rows(0)).then_inc(stats_done[0], 1)
            ln_moments(0, 0)
            for b in range(G4):
                ln_rows(0, 0, b, x_rows(0), xh_rows)
            ln_low(0, 0)
            dve.wait_ge(qz_zeroed, 1)
            for kind in ("Q", "K"):
                for i in range(KI):
                    phi(0, kind, i)
            dve.wait_ge(pads_done, 3)
            groups(dve, body)
            for b in range(G4):
                ln_stats(2, b, sum_rows).then_inc(stats_done[2], 1)
            ln_moments(NG - 1, 2)
            for b in range(G4):
                ln_rows(NG - 1, 2, b, sum_rows, x_rows(NG - 1))

        @block.gpsimd
        def _(pool):
            def ln_rstd(g, ln):
                settle(pool, passed, (mom_done[ln], g + 1))
                pool.tensor_scalar(rstd[:, ln, :], mom[:, ln, :, 1], EPS, None, ALU.add).then_inc(eps_done[ln], 1)
                pool.wait_ge(eps_done[ln], g + 1)
                pool.tensor_tensor(rstd[:, ln, :], rstd[:, ln, :], half_neg[0:T, :], ALU.pow).then_inc(rstd_done[ln], 1)

            def body(g):
                for t in range(STEPS):
                    if t == 5 and not is_first(g):
                        ln_rstd(g - 1, 2)
                    if t == 9 and not is_last(g):
                        ln_rstd(g + 1, 0)
                ln_rstd(g, 1)
                at_least(pool, rows_done[2], g)
                pool.tensor_tensor(xsum[:, :, :], x1[:, :, :], x_sb[:, bass.ds(G4 * g, G4), :], ALU.add).then_inc(xs1_done, 1)
                pool.wait_ge(xs1_done, g + 1)
                pool.tensor_tensor(xsum[:, :, :], xsum[:, :, :], b2[:, :].unsqueeze(1).to_broadcast([T, G4, D]),
                                   ALU.add).then_inc(xs_done, 1)

            pool.memset(qz[:, :, :], 0.0).then_inc(qz_zeroed, 1)
            ln_rstd(0, 0)
            pool.memset(v1[:, :, :, 0:DH], 0.0).then_inc(pads_done, 1)
            pool.memset(v1[:, :, :, DH], 1.0).then_inc(pads_done, 1)
            pool.memset(sm[:, :, :], 1e-6).then_inc(pads_done, 1)
            groups(pool, body)
            ln_rstd(NG - 1, 2)


def load_layer1(nc, a, x_sb, ident, half_neg, consts_done, causal, hi, lo, vectors, sb_in, psum_in, sem):
    stack = ExitStack()
    with stack:
        sb, psum = sb_in(stack), psum_in(stack)
        g1, be1, g2, be2, b1, b2 = vectors
        NST = 3
        stage = [sb(f"a_stage{i}", [P, WCOLS], F32) for i in range(NST)]
        raw = [sb(f"a_raw{i}", [P, KD, INNER], F32) for i in range(2)]
        turned = sb("a_turned", [P, 2 * KI // 2, 4, P], F32)
        proj2 = sb("a_proj2", [P, P], F32)
        turn_ps = [psum(f"a_turn{i}", [P, 4 * P]) for i in range(4)]
        fold_ps = [psum(f"a_fold{i}", [P, 4 * P]) for i in range(4)]
        loaded = [sem(f"a_loaded{i}") for i in range(NST)]
        hi_done, lo_done = sem("a_whi_done"), sem("a_wlo_done")
        raw_loaded, vec_loaded, x_loaded = sem("a_raw_loaded"), sem("a_vec_loaded"), sem("a_x_loaded")
        p2_zero, p2_loaded = sem("a_p2_zero"), sem("a_p2_loaded")
        turn_ready, turn_done, fold_ready, fold_hi, fold_lo = (
            sem(f"a_{n}") for n in ("turn_ready", "turn_done", "fold_ready", "fold_hi", "fold_lo"))
        rows = lambda w: w.rearrange("(k p) n -> p k n", p=P)
        jobs = [(rows(a[f"L0_attn_{n}"]), hi[n][:, :], lo[n][:, :]) for n in ("wv", "wo", "w1", "w2")]
        NT = 2 * KI * KD // 4
        block = stack.enter_context(nc.Block())

        @block.sync
        def _(sp):
            for i, n in enumerate(("L0_attn_wq", "L0_attn_wk")):
                sp.dma_start(raw[i][:, :, :], rows(a[n])).then_inc(raw_loaded, 16)
            sp.wait_ge(p2_zero, 1)
            for r in range(2):
                sp.dma_start(proj2[DH * r:DH * (r + 1), DH * r:DH * (r + 1)], a["L0_attn_proj"]).then_inc(p2_loaded, 16)
            for i, (src, _, _) in enumerate(jobs):
                at_least(sp, lo_done, i - NST + 1)
                sp.dma_start(stage[i % NST][:, :].rearrange("p (k n) -> p k n", n=src.shape[2]), src).then_inc(loaded[i % NST], 16)
            for t, n in ((g1, "g1"), (be1, "beta1"), (g2, "g2"), (be2, "beta2"), (b1, "b1")):
                sp.dma_start(t[:, :], a[f"L0_attn_{n}"].rearrange("(k p) -> p k", p=P),
                             allow_slow_non_contiguous=True).then_inc(vec_loaded, 16)
            sp.dma_start(b2[:, :], a["L0_attn_b2"].partition_broadcast(T)).then_inc(vec_loaded, 16)
            sp.dma_start(x_sb[:, :, :], a["x"].rearrange("b t d -> t b d")).then_inc(x_loaded, 16)
            sp.wait_ge(vec_loaded, 6 * 16)
            sp.wait_ge(x_loaded, 16)

        @block.gpsimd
        def _(pool):
            pool.memset(proj2[:, :], 0.0).then_inc(p2_zero, 1)
            pool.memset(ident[:, :], 1.0).then_inc(consts_done, 1)
            pool.memset(causal[:, :], 1.0).then_inc(consts_done, 1)
            pool.memset(half_neg[:, :], -0.5).then_inc(consts_done, 1)
            pool.wait_ge(consts_done, 3)
            pool.affine_select(out=ident[:, :], in_=ident[:, :], compare_op=ALU.is_equal, fill=0.0, base=0,
                               pattern=[[-1, P]], channel_multiplier=1).then_inc(consts_done, 1)
            pool.affine_select(out=causal[:, :], in_=causal[:, :], compare_op=ALU.is_ge, fill=0.0, base=0,
                               pattern=[[1, T]], channel_multiplier=-1).then_inc(consts_done, 1)

        @block.tensor
        def _(pe):
            pe.wait_ge(consts_done, 5)
            pe.wait_ge(raw_loaded, 32)
            for n in range(NT):
                w, m2 = divmod(n, KI // 2)
                at_least(pe, turn_done, n - 3)
                for i in range(4):
                    m, k = 2 * m2 + i // 2, i % 2
                    mm = pe.transpose(turn_ps[n % 4][:, i * P:(i + 1) * P], raw[w][:, k, m * P:(m + 1) * P], ident[:, :])
                mm.then_inc(turn_ready, 1)
            pe.wait_ge(p2_loaded, 32)
            for n in range(NT):
                pe.wait_ge(turn_done, n + 1)
                at_least(pe, fold_lo, n - 3)
                for i in range(4):
                    mm = pe.matmul(fold_ps[n % 4][:, i * P:(i + 1) * P], turned[:, n, i, :], proj2[:, :], start=True, stop=True)
                mm.then_inc(fold_ready, 1)

        def folded(t, n):
            w, m2 = divmod(n, KI // 2)
            return t[("wq", "wk")[w]][:, :].rearrange("p (k m c) -> p m k c", k=KD, c=P)[:, 2 * m2:2 * m2 + 2, :, :]

        def fold_bank(n):
            return fold_ps[n % 4][:, :].rearrange("p (m k c) -> p m k c", m=2, k=KD)

        @block.scalar
        def _(act):
            for n in range(NT):
                act.wait_ge(turn_ready, n + 1)
                act.activation(turned[:, n, :, :], turn_ps[n % 4][:, :].rearrange("p (i c) -> p i c", c=P),
                               ACT.Identity).then_inc(turn_done, 1)
            for n in range(NT):
                act.wait_ge(fold_ready, n + 1)
                act.activation(folded(hi, n), fold_bank(n), ACT.Identity).then_inc(fold_hi, 1)
            for i, (_, h, _) in enumerate(jobs):
                act.wait_ge(loaded[i % NST], 16 * (i // NST + 1))
                act.activation(h, stage[i % NST][:, :], ACT.Identity, scale=WSCALE).then_inc(hi_done, 1)

        @block.vector
        def _(dve):
            for n in range(NT):
                dve.wait_ge(fold_hi, n + 1)
                dve.tensor_tensor(folded(lo, n), fold_bank(n), folded(hi, n), ALU.subtract).then_inc(fold_lo, 1)
            for i, (_, h, l) in enumerate(jobs):
                dve.wait_ge(hi_done, i + 1)
                dve.scalar_tensor_tensor(l, stage[i % NST][:, :], WSCALE, h, ALU.mult, ALU.subtract).then_inc(lo_done, 1)


def layer2(nc, a, x_sb, ident, half_neg, passed, sb_in, psum_in, sem):
    stack = ExitStack()
    with stack:
        sb, psum = sb_in(stack), psum_in(stack)
        names = ["q", "k", "v", "o"]
        hi = {n: sb(f"b_w{n}_hi", [P, WCOLS], F16) for n in names}
        lo = {n: sb(f"b_w{n}_lo", [P, WCOLS], F16) for n in names}
        gx, bx, gc, bc = (sb(f"b_{n}", [P, KD], F32) for n in ("gx", "bx", "gc", "bc"))
        load_layer2(nc, a, hi, lo, (gx, bx, gc, bc), sb_in, sem)

        def pair(name, k, c0, n, width):
            c = k * width + c0
            return hi[name][:, c:c + n], lo[name][:, c:c + n]

        SP2 = S2 + 1
        NT4 = JT + 1
        ctx = sb("ctx", [JP, 2, JT, D], F32)
        mask8 = sb("mask8", [T, 2, S2], U8)
        mask_bias = sb("mask_bias", [T, 2, S2], F32)
        stats = sb("b_stats", [P, NT4, 6], F32)
        mom = sb("b_mom", [P, NT4, 2], F32)
        rstd = sb("b_rstd", [P, NT4], F32)
        shift = sb("b_shift", [P, NT4], F32)
        xc = sb("xc", [JP, JT, D], F32)
        xn = sb("xn", [T, D], F32)
        cn32 = sb("cn32", [P, KD, S2], F32)
        cn_hi, cn_lo = (sb(f"cn_{n}", [P, 2, KD, SP2], F16) for n in ("hi", "lo"))
        xt32 = sb("xt32", [P, KD, T], F32)
        xt_hi, xt_lo = (sb(f"xt_{n}", [P, 2, KD, T], F16) for n in ("hi", "lo"))
        k_hi, k_lo = (sb(f"k_{n}", [P, 2, KI, SP2], F16) for n in ("hi", "lo"))
        v2_hi, v2_lo = (sb(f"v2_{n}", [JP, 2, JT, INNER], F16) for n in ("hi", "lo"))
        qz_hi, qz_lo = (sb(f"qz_{n}", [P, 2, H, T], F16) for n in ("hi", "lo"))
        s_neg = sb("s_neg", [T, 2, S2], F32)
        neg_max = sb("neg_max", [T, 4], F32)
        p32 = sb("p32", [T, 4, S2], F32)
        p_sum = sb("p_sum", [T, 4], F32)
        p_rec = sb("p_rec", [T, 4], F32)
        p_norm = sb("p_norm", [T, 4, S2], F32)
        pt_hi, pt_lo = (sb(f"pt_{n}", [JP, 2, JT * T], F16) for n in ("hi", "lo"))
        o_hi, o_lo = (sb(f"b_o_{n}", [P, KI, T], F16) for n in ("hi", "lo"))
        z = sb("b_z", [T, D], F32)
        z_stats, z_mom, z_rstd = sb("z_stats", [T, 6], F32), sb("z_mom", [T, 2], F32), sb("z_rstd", [T, 1], F32)

        NPB = 3
        pb = [psum(f"b_pb{i}", [P, 512]) for i in range(NPB)]
        s_ps = [psum(f"b_s{i}", [P, 512]) for i in range(2)]
        t_ps, o_ps, misc_ps = psum("b_t", [P, 512]), psum("b_o", [P, 512]), psum("b_misc", [P, 512])

        NCH = 16
        AHEAD = 4
        Q0, K0, V0 = 0, 2, 2 + KI
        TURN_AT = (11, 12)
        PER = NCH + KD
        PRE = 2 * KD + NCH
        assert PER % NPB == 0

        def has_prep(b):
            return not isinstance(b, int) or b + 2 < B

        def use_piece(n, s):
            if isinstance(n, int) and n == 0:
                return 0, 2 * KD + s
            b = n - 1
            return b, PRE + s + (sum(s > at for at in TURN_AT) if has_prep(b) else 0)

        def use_turn(n, k):
            if isinstance(n, int) and n < 2:
                return 0, KD * n + k
            return n - 2, PRE + TURN_AT[k] + 1 + k

        def ready(use):
            return use[0] * PER + use[1] + 1

        def freed(use):
            return use[0] * (PER // NPB) + use[1] // NPB + 1

        def bank(use):
            return pb[use[1] % NPB]

        ctx_loaded = [sem(f"b_ctx_loaded{i}") for i in range(2)]
        mask_loaded = [sem(f"b_mask_loaded{i}") for i in range(2)]
        mask_m1, mask_done = sem("b_mask_m1"), sem("b_mask_done")
        zeroed, stats_zeroed = sem("b_zeroed"), sem("b_stats_zeroed")
        pb_ready = sem("b_pb_ready")
        pb_free = [sem(f"b_pb_free{i}") for i in range(NPB)]
        piece_hi = sem("b_piece_hi")
        stats_done, mom_done, eps_done, rstd_done, shift_neg, shift_done = (
            sem(f"b_{n}") for n in ("stats_done", "mom_done", "eps_done", "rstd_done", "shift_neg", "shift_done"))
        xc_done, xn_done, xt_ready, xt_turned, xt_hi_done, xt_done = (
            sem(f"b_{n}") for n in ("xc_done", "xn_done", "xt_ready", "xt_turned", "xt_hi_done", "xt_done"))
        cn_hi_done, cn_done = sem("b_cn_hi_done"), sem("b_cn_done")
        s_ready, s_masked, p_exp, p_sum_rec, p_norm_done = (
            sem(f"b_{n}") for n in ("s_ready", "s_masked", "p_exp", "p_sum_rec", "p_norm_done"))
        t_ready, pt_hi_done, pt_lo_done, av_done, o_hi_done, o_lo_done = (
            sem(f"b_{n}") for n in ("t_ready", "pt_hi_done", "pt_lo_done", "av_done", "o_hi_done", "o_lo_done"))
        wo_ready, z_done, z_stats_done, z_mom_done, z_eps, z_rstd_done, x_done = (
            sem(f"b_{n}") for n in ("wo_ready", "z_done", "z_stats_done", "z_mom_done", "z_eps", "z_rstd_done", "x_done"))

        def x_row(b):
            return x_sb[:, bass.ds(b, 1), :].rearrange("p a d -> p (a d)")

        def batches(eng, body):
            body(0, 0)
            body(1, 1)
            with eng.Fori(1, B // 2 - 1) as i:
                for par in range(2):
                    body(2 * i + par, par)
            body(B - 2, 0)
            body(B - 1, 1)

        def is_first(b):
            return isinstance(b, int) and b == 0

        def is_last(b):
            return isinstance(b, int) and b == B - 1

        block = stack.enter_context(nc.Block())

        @block.sync
        def _(sp):
            def load(n, par):
                settle(sp, passed, (xc_done, n - 1))
                sp.dma_start(ctx[:, par, :, :], a["ctx_1024"][bass.ds(n, 1), :, :].rearrange(
                    "a (p t) d -> p (a t) d", t=JT)).then_inc(ctx_loaded[par], 16)
                settle(sp, passed, (mask_done, n - 1))
                sp.dma_start(mask8[:, par, :], a["mask_BxS2_bf1"][bass.ds(n, 1), :].rearrange(
                    "a s -> (a s)").partition_broadcast(T)).then_inc(mask_loaded[par], 16)

            load(0, 0)
            load(1, 1)
            with sp.Fori(1, B // 2) as i:
                for par in range(2):
                    load(2 * i + par, par)

        @block.tensor
        def _(pe):
            def claim(use):
                at_least(pe, pb_free[use[1] % NPB], freed(use) - 1)
                return bank(use)

            def turn_x(n):
                pe.wait_ge(xn_done, n + 1)
                at_least(pe, z_done, n - 2)
                at_least(pe, xt_turned, n)
                for k in range(KD):
                    mm = pe.transpose(misc_ps[:, k * T:(k + 1) * T], xn[:, k * P:(k + 1) * P], ident[0:T, 0:T])
                mm.then_inc(xt_ready, 1)

            def turn_ctx(n, k):
                pe.wait_ge(xc_done, n + 1)
                ps = claim(use_turn(n, k))
                for t in range(JT):
                    mm = pe.transpose(ps[:, t * JP:(t + 1) * JP], xc[:, t, k * P:(k + 1) * P], ident[0:JP, 0:JP])
                mm.then_inc(pb_ready, 1)

            def piece(n, par, s):
                if s == Q0:
                    pe.wait_ge(xt_done, n + 1)
                if s == K0:
                    pe.wait_ge(cn_done, KD * (n + 1))
                ps = claim(use_piece(n, s))
                if s < K0:
                    for i in range(4):
                        for k in range(KD):
                            mm = split_product(pe, ps[:, i * T:(i + 1) * T], pair("q", k, (4 * s + i) * P, P, INNER),
                                               (xt_hi[:, par, k, :], xt_lo[:, par, k, :]), k == 0, k == KD - 1)
                elif s < V0:
                    for k in range(KD):
                        mm = split_product(pe, ps[:, 0:S2], pair("k", k, (s - K0) * P, P, INNER),
                                           (cn_hi[:, par, k, 0:S2], cn_lo[:, par, k, 0:S2]), k == 0, k == KD - 1)
                else:
                    t, half = divmod(s - V0, 2)
                    cols = slice(t * JP, (t + 1) * JP)
                    for k in range(KD):
                        mm = split_product(pe, ps[0:JP, :], (cn_hi[:, par, k, cols], cn_lo[:, par, k, cols]),
                                           pair("v", k, half * 512, 512, INNER), k == 0, k == KD - 1)
                mm.then_inc(pb_ready, 1)

            def written(n, s):
                use = use_piece(n, s)
                pe.wait_ge(pb_free[use[1] % NPB], freed(use))

            def scores(b, par, h):
                written(b, Q0 + h // 8)
                written(b, K0 + h // 2)
                at_least(pe, s_masked, H * b + h - 1)
                mm = split_product(pe, s_ps[h % 2][0:T, 0:S2], (qz_hi[:, par, h, :], qz_lo[:, par, h, :]),
                                   (k_hi[:, par, h // 2, 0:S2], k_lo[:, par, h // 2, 0:S2]), True, True)
                mm.then_inc(s_ready, 1)

            def turn_scores(b, h):
                pe.wait_ge(p_norm_done, H * b + h + 1)
                at_least(pe, pt_lo_done, H * b + h)
                for t in range(JT):
                    mm = pe.transpose(t_ps[0:JP, t * T:(t + 1) * T], p_norm[:, h % 4, t * JP:(t + 1) * JP], ident[0:T, 0:T])
                mm.then_inc(t_ready, 1)

            def values(b, par, h):
                if h == 0:
                    for s in range(NCH - NPB, NCH):
                        written(b, s)
                pe.wait_ge(pt_lo_done, H * b + h + 1)
                if h % 8 == 0:
                    at_least(pe, o_lo_done, 2 * b + h // 8)
                r, c = DH * (h % 2), (h // 2 % 4) * T
                for t in range(JT):
                    cols = slice(h * DH, (h + 1) * DH)
                    mm = split_product(pe, o_ps[r:r + DH, c:c + T], (v2_hi[:, par, t, cols], v2_lo[:, par, t, cols]),
                                       (pt_hi[:, h % 2, t * T:(t + 1) * T], pt_lo[:, h % 2, t * T:(t + 1) * T]),
                                       t == 0, t == JT - 1)
                mm.then_inc(av_done, 1)

            def out_rows(b):
                pe.wait_ge(o_lo_done, 2 * b + 2)
                at_least(pe, xt_turned, min(b + 3, B) if isinstance(b, int) else b + 3)
                at_least(pe, z_done, b)
                for m in range(KI):
                    mm = split_product(pe, misc_ps[0:T, 0:D], (o_hi[:, m, :], o_lo[:, m, :]), pair("o", m, 0, D, D),
                                       m == 0, m == KI - 1)
                mm.then_inc(wo_ready, 1)

            def body(b, par):
                for s in range(H):
                    turn_scores(b, s)
                    if not is_last(b):
                        piece(b + 1, 1 - par, s)
                    if s + AHEAD < H:
                        scores(b, par, s + AHEAD)
                    elif not is_last(b):
                        scores(b + 1, 1 - par, s + AHEAD - H)
                    if s > 0:
                        values(b, par, s - 1)
                    elif not is_first(b):
                        values(b - 1, 1 - par, H - 1)
                    if s == 3 and not is_first(b):
                        out_rows(b - 1)
                    if has_prep(b):
                        if s == 10:
                            turn_x(b + 2)
                        if s in TURN_AT:
                            turn_ctx(b + 2, TURN_AT.index(s))

            for n in range(2):
                turn_x(n)
                for k in range(KD):
                    turn_ctx(n, k)
            for s in range(NCH):
                piece(0, 0, s)
            for h in range(AHEAD):
                scores(0, 0, h)
            batches(pe, body)
            values(B - 1, 1, H - 1)
            out_rows(B - 1)

        @block.scalar
        def _(act):
            def x_columns(n):
                act.wait_ge(xt_ready, n + 1)
                at_least(act, xt_done, n)
                for k in range(KD):
                    ins = act.activation(xt32[:, k, :], misc_ps[:, k * T:(k + 1) * T], ACT.Identity, bias=bx[:, k:k + 1],
                                         scale=gx[:, k:k + 1])
                ins.then_inc(xt_turned, 1)

            def ctx_columns(n, k):
                use = use_turn(n, k)
                act.wait_ge(pb_ready, ready(use))
                at_least(act, cn_done, KD * (n - 1) + k + 1)
                act.activation(cn32[:, k, :], bank(use)[:, 0:S2], ACT.Identity, bias=bc[:, k:k + 1],
                               scale=gc[:, k:k + 1]).then_inc(pb_free[use[1] % NPB], 1)

            def piece_high(n, par, s):
                use = use_piece(n, s)
                act.wait_ge(pb_ready, ready(use))
                ps = bank(use)
                if s < K0:
                    for r in range(2):
                        rows = slice(DH * r, DH * (r + 1))
                        ins = act.activation(qz_hi[rows, par, 8 * s + r:8 * s + 8:2, :],
                                             ps[rows, 0:4 * T].rearrange("p (m t) -> p m t", t=T), ACT.Identity,
                                             scale=UNSCALE * DH ** -0.5)
                elif s < V0:
                    ins = act.activation(k_hi[:, par, s - K0, 0:S2], ps[:, 0:S2], ACT.Identity, scale=UNSCALE)
                else:
                    t, half = divmod(s - V0, 2)
                    ins = act.activation(v2_hi[:, par, t, half * 512:(half + 1) * 512], ps[0:JP, :], ACT.Identity, scale=UNSCALE)
                ins.then_inc(piece_hi, 1)

            def softmax_exp(b, h):
                act.wait_ge(s_masked, H * b + h + 1)
                at_least(act, p_norm_done, H * b + h - 3)
                act.activation(p32[:, h % 4, :], s_neg[:, h % 2, :], ACT.Exp, bias=neg_max[:, h % 4:h % 4 + 1], scale=-1.0,
                               accum_out=p_sum[:, h % 4:h % 4 + 1]).then_inc(p_exp, 1)

            def turned_high(b, h):
                act.wait_ge(t_ready, H * b + h + 1)
                at_least(act, av_done, H * b + h - 1)
                act.activation(pt_hi[:, h % 2, :], t_ps[0:JP, 0:JT * T], ACT.Identity).then_inc(pt_hi_done, 1)

            def out_high(b, half):
                act.wait_ge(av_done, H * b + 8 * half + 8)
                if half == 0:
                    at_least(act, wo_ready, b)
                act.activation(o_hi[:, 4 * half:4 * half + 4, :], o_ps[:, 0:4 * T].rearrange("p (m t) -> p m t", t=T),
                               ACT.Identity).then_inc(o_hi_done, 1)

            def body(b, par):
                for s in range(H):
                    if s == 1 and not is_first(b):
                        out_high(b - 1, 1)
                    if s == 9:
                        out_high(b, 0)
                    if s + 2 < H:
                        softmax_exp(b, s + 2)
                    elif not is_last(b):
                        softmax_exp(b + 1, s + 2 - H)
                    turned_high(b, s)
                    if not is_last(b):
                        piece_high(b + 1, 1 - par, s)
                    if has_prep(b):
                        if s == 11:
                            x_columns(b + 2)
                        if s - 1 in TURN_AT:
                            ctx_columns(b + 2, TURN_AT.index(s - 1))

            for n in range(2):
                x_columns(n)
                for k in range(KD):
                    ctx_columns(n, k)
            act.wait_ge(zeroed, 2)
            for s in range(NCH):
                piece_high(0, 0, s)
            for h in range(2):
                softmax_exp(0, h)
            batches(act, body)
            out_high(B - 1, 1)

        @block.vector
        def _(dve):
            def prep_stats(n, par, tiles):
                dve.wait_ge(ctx_loaded[par], 16 * (half_of(n) + 1))
                at_least(dve, mom_done, n)
                for t in tiles:
                    src = ctx[:, par, t, :] if t < JT else x_row(n)
                    ins = dve.bn_stats(stats[0:JP if t < JT else T, t, :], src)
                if JT in tiles:
                    ins.then_inc(stats_done, 1)

            def prep_moments(n):
                settle(dve, passed, (stats_done, n + 1), (xc_done, n))
                for t in range(NT4):
                    ins = dve.bn_aggr(mom[0:JP if t < JT else T, t, :], stats[0:JP if t < JT else T, t, :])
                ins.then_inc(mom_done, 1)

            def prep_x(n):
                dve.wait_ge(rstd_done, n + 1)
                at_least(dve, xt_ready, n)
                dve.tensor_scalar(xn[:, :], x_row(n), mom[0:T, JT, 0:1], rstd[0:T, JT:JT + 1], ALU.subtract,
                                  ALU.mult).then_inc(xn_done, 1)

            def piece_low(n, par, s):
                use = use_piece(n, s)
                dve.wait_ge(piece_hi, NCH * n + s + 1)
                ps = bank(use)
                if s < K0:
                    for r in range(2):
                        rows = slice(DH * r, DH * (r + 1))
                        heads = slice(8 * s + r, 8 * s + 8, 2)
                        ins = dve.scalar_tensor_tensor(qz_lo[rows, par, heads, :], ps[rows, 0:4 * T].rearrange("p (m t) -> p m t", t=T),
                                                       UNSCALE * DH ** -0.5, qz_hi[rows, par, heads, :], ALU.mult, ALU.subtract)
                elif s < V0:
                    ins = dve.scalar_tensor_tensor(k_lo[:, par, s - K0, 0:S2], ps[:, 0:S2], UNSCALE, k_hi[:, par, s - K0, 0:S2],
                                                   ALU.mult, ALU.subtract)
                else:
                    t, half = divmod(s - V0, 2)
                    cols = slice(half * 512, (half + 1) * 512)
                    ins = dve.scalar_tensor_tensor(v2_lo[:, par, t, cols], ps[0:JP, :], UNSCALE, v2_hi[:, par, t, cols],
                                                   ALU.mult, ALU.subtract)
                ins.then_inc(pb_free[use[1] % NPB], 1)

            def mask_max(b, par, h):
                waits = [(s_ready, H * b + h + 1), (p_exp, H * b + h - 1)]
                if h == 0:
                    waits.append((mask_done, b + 1))
                settle(dve, passed, *waits)
                dve.tensor_tensor_reduce(s_neg[:, h % 2, :], s_ps[h % 2][0:T, 0:S2], mask_bias[:, par, :], -1.0, 3.4e38,
                                         ALU.add, ALU.min, neg_max[:, h % 4:h % 4 + 1]).then_inc(s_masked, 1)

            def sum_reciprocal(b, h):
                dve.wait_ge(p_exp, H * b + h + 1)
                dve.reciprocal(p_rec[:, h % 4:h % 4 + 1], p_sum[:, h % 4:h % 4 + 1]).then_inc(p_sum_rec, 1)

            def turned_low(b, h):
                dve.wait_ge(pt_hi_done, H * b + h + 1)
                dve.tensor_tensor(pt_lo[:, h % 2, :], t_ps[0:JP, 0:JT * T], pt_hi[:, h % 2, :],
                                  ALU.subtract).then_inc(pt_lo_done, 1)

            def out_low(b, half):
                dve.wait_ge(o_hi_done, 2 * b + half + 1)
                dve.tensor_tensor(o_lo[:, 4 * half:4 * half + 4, :], o_ps[:, 0:4 * T].rearrange("p (m t) -> p m t", t=T),
                                  o_hi[:, 4 * half:4 * half + 4, :], ALU.subtract).then_inc(o_lo_done, 1)

            def residual(b):
                dve.wait_ge(wo_ready, b + 1)
                at_least(dve, x_done, b)
                dve.scalar_tensor_tensor(z[:, :], misc_ps[0:T, 0:D], UNSCALE, x_row(b), ALU.mult, ALU.add).then_inc(z_done, 1)
                dve.wait_ge(z_done, b + 1)
                dve.bn_stats(z_stats[:, :], z[:, :]).then_inc(z_stats_done, 1)

            def residual_moments(b):
                settle(dve, passed, (z_stats_done, b + 1))
                dve.bn_aggr(z_mom[:, :], z_stats[:, :]).then_inc(z_mom_done, 1)

            def norm_out(b):
                dve.wait_ge(z_rstd_done, b + 1)
                dve.tensor_scalar(x_row(b), z[:, :], z_mom[:, 0:1], z_rstd[:, :], ALU.subtract, ALU.mult).then_inc(x_done, 1)

            def body(b, par):
                for s in range(H):
                    if s == 1 and not is_first(b):
                        out_low(b - 1, 1)
                    if s == 9:
                        out_low(b, 0)
                    if s + 1 < H:
                        sum_reciprocal(b, s + 1)
                    elif not is_last(b):
                        sum_reciprocal(b + 1, 0)
                    if s + 3 < H:
                        mask_max(b, par, s + 3)
                    elif not is_last(b):
                        mask_max(b + 1, 1 - par, s + 3 - H)
                    turned_low(b, s)
                    if not is_first(b):
                        if s == 4:
                            residual(b - 1)
                        if s == 5:
                            residual_moments(b - 1)
                        if s == 7:
                            norm_out(b - 1)
                    if not is_last(b):
                        piece_low(b + 1, 1 - par, s)
                    if has_prep(b):
                        if s == 2:
                            prep_stats(b + 2, par, (0, 1))
                        if s == 4:
                            prep_stats(b + 2, par, (2, JT))
                        if s == 5:
                            prep_moments(b + 2)
                        if s == 7:
                            prep_x(b + 2)

            def half_of(n):
                return n // 2 if isinstance(n, int) else halves[0]

            halves = [None]
            dve.wait_ge(stats_zeroed, 1)
            for n in range(2):
                prep_stats(n, n, (0, 1, 2, JT))
                prep_moments(n)
                prep_x(n)
            dve.wait_ge(zeroed, 2)
            for s in range(NCH):
                piece_low(0, 0, s)
            for h in range(3):
                mask_max(0, 0, h)
            sum_reciprocal(0, 0)
            body(0, 0)
            body(1, 1)
            with dve.Fori(1, B // 2 - 1) as i:
                halves[0] = i + 1
                for par in range(2):
                    body(2 * i + par, par)
            body(B - 2, 0)
            body(B - 1, 1)
            out_low(B - 1, 1)
            residual(B - 1)
            residual_moments(B - 1)
            norm_out(B - 1)

        @block.gpsimd
        def _(pool):
            def mask(n, par):
                settle(pool, passed, (mask_loaded[par], 16 * (half_of(n) + 1)),
                       (s_masked, H * (n - 1)))
                pool.tensor_scalar(mask_bias[:, par, :].rearrange("q (t p) -> q t p", t=JT),
                                   mask8[:, par, :].rearrange("q (p t) -> q t p", t=JT), -1.0, MASKED, ALU.add,
                                   ALU.mult).then_inc(mask_done, 1)

            def prep_rstd(n):
                settle(pool, passed, (mom_done, n + 1), (xc_done, n))
                pool.tensor_scalar(rstd[:, :], mom[:, :, 1], EPS, None, ALU.add).then_inc(eps_done, 1)
                pool.wait_ge(eps_done, n + 1)
                pool.tensor_tensor(rstd[:, :], rstd[:, :], half_neg[:, :], ALU.pow).then_inc(rstd_done, 1)
                pool.wait_ge(rstd_done, n + 1)
                pool.tensor_tensor(shift[:, :], mom[:, :, 0], rstd[:, :], ALU.mult).then_inc(shift_neg, 1)
                settle(pool, passed, (shift_neg, n + 1))
                pool.tensor_scalar(shift[:, :], shift[:, :], -1.0, None, ALU.mult).then_inc(shift_done, 1)

            def prep_rows(n, par):
                waits = [(shift_done, n + 1), (xn_done, n + 1)]
                if not is_first(n):
                    waits.append((pb_ready, ready(use_turn(n - 1, KD - 1))))
                settle(pool, passed, *waits)
                for t in range(JT):
                    ins = pool.tensor_scalar(xc[:, t, :], ctx[:, par, t, :], rstd[0:JP, t:t + 1], shift[0:JP, t:t + 1],
                                             ALU.mult, ALU.add)
                ins.then_inc(xc_done, 1)

            def split_x(n, par):
                settle(pool, passed, (xt_turned, n + 1))
                pool.tensor_copy(xt_hi[:, par, :, :], xt32[:, :, :]).then_inc(xt_hi_done, 1)
                pool.wait_ge(xt_hi_done, n + 1)
                pool.tensor_tensor(xt_lo[:, par, :, :], xt32[:, :, :], xt_hi[:, par, :, :], ALU.subtract).then_inc(xt_done, 1)

            def split_ctx(n, par, k):
                use = use_turn(n, k)
                settle(pool, passed, (pb_free[use[1] % NPB], freed(use)))
                pool.tensor_copy(cn_hi[:, par, k, 0:S2], cn32[:, k, :]).then_inc(cn_hi_done, 1)
                pool.wait_ge(cn_hi_done, KD * n + k + 1)
                pool.tensor_tensor(cn_lo[:, par, k, 0:S2], cn32[:, k, :], cn_hi[:, par, k, 0:S2], ALU.subtract).then_inc(cn_done, 1)

            def residual_rstd(b):
                settle(pool, passed, (z_mom_done, b + 1))
                pool.tensor_scalar(z_rstd[:, :], z_mom[:, 1:2], EPS, None, ALU.add).then_inc(z_eps, 1)
                pool.wait_ge(z_eps, b + 1)
                pool.tensor_tensor(z_rstd[:, :], z_rstd[:, :], half_neg[0:T, 0:1], ALU.pow).then_inc(z_rstd_done, 1)

            def normalise(b, h):
                settle(pool, passed, (p_sum_rec, H * b + h + 1), (t_ready, H * b + h - 3))
                pool.tensor_scalar(p_norm[:, h % 4, :], p32[:, h % 4, :], p_rec[:, h % 4:h % 4 + 1], 0.0, ALU.mult,
                                   ALU.add).then_inc(p_norm_done, 1)

            def body(b, par):
                for s in range(H):
                    if s + 1 < H:
                        normalise(b, s + 1)
                    elif not is_last(b):
                        normalise(b + 1, 0)
                    if s == 0 and not is_last(b):
                        mask(b + 1, 1 - par)
                    if s == 6 and not is_first(b):
                        residual_rstd(b - 1)
                    if has_prep(b):
                        if s == 6:
                            prep_rstd(b + 2)
                        if s == 8:
                            prep_rows(b + 2, par)
                        if s == 12:
                            split_x(b + 2, par)
                        if s - 2 in TURN_AT:
                            split_ctx(b + 2, par, TURN_AT.index(s - 2))

            def half_of(n):
                return n // 2 if isinstance(n, int) else halves[par_of[0]]

            halves, par_of = [None, None], [0]
            pool.memset(mom[:, :, :], 1.0).then_inc(stats_zeroed, 1)
            pool.memset(qz_hi[:, :, :, :], 0.0).then_inc(zeroed, 1)
            pool.memset(qz_lo[:, :, :, :], 0.0).then_inc(zeroed, 1)
            mask(0, 0)
            for n in range(2):
                prep_rstd(n)
                prep_rows(n, n)
                split_x(n, n)
                for k in range(KD):
                    split_ctx(n, n, k)
            normalise(0, 0)
            body(0, 0)
            body(1, 1)
            with pool.Fori(1, B // 2 - 1) as i:
                halves[0], halves[1] = i + 1, i
                for par in range(2):
                    par_of[0] = 1 - par
                    body(2 * i + par, par)
            body(B - 2, 0)
            body(B - 1, 1)
            residual_rstd(B - 1)


def load_layer2(nc, a, hi, lo, vectors, sb_in, sem):
    stack = ExitStack()
    with stack:
        sb = sb_in(stack)
        NST = 3
        stage = [sb(f"b_stage{i}", [P, WCOLS], F32) for i in range(NST)]
        loaded = [sem(f"b_loaded{i}") for i in range(NST)]
        hi_done, lo_done, vec_loaded = sem("b_whi_done"), sem("b_wlo_done"), sem("b_vec_loaded")
        rows = lambda w: w.rearrange("(k p) n -> p k n", p=P)
        wkv = a["L0_xattn_Wkv"]
        jobs = [(rows(a["L0_xattn_Wq"]), "q"), (rows(wkv[:, 0:INNER]), "k"), (rows(wkv[:, INNER:2 * INNER]), "v"),
                (rows(a["L0_xattn_Wo"]), "o")]
        block = stack.enter_context(nc.Block())

        @block.sync
        def _(sp):
            for i, (src, _) in enumerate(jobs):
                at_least(sp, lo_done, i - NST + 1)
                sp.dma_start(stage[i % NST][:, :].rearrange("p (k n) -> p k n", n=src.shape[2]), src).then_inc(loaded[i % NST], 16)
            for t, n in zip(vectors, ("norm_w", "norm_b", "ctx_norm_w", "ctx_norm_b")):
                sp.dma_start(t[:, :], a[f"L0_xattn_{n}"].rearrange("(k p) -> p k", p=P),
                             allow_slow_non_contiguous=True).then_inc(vec_loaded, 16)
            sp.wait_ge(vec_loaded, 4 * 16)

        @block.scalar
        def _(act):
            for i, (_, n) in enumerate(jobs):
                act.wait_ge(loaded[i % NST], 16 * (i // NST + 1))
                act.activation(hi[n][:, :], stage[i % NST][:, :], ACT.Identity, scale=WSCALE).then_inc(hi_done, 1)

        @block.vector
        def _(dve):
            for i, (_, n) in enumerate(jobs):
                dve.wait_ge(hi_done, i + 1)
                dve.scalar_tensor_tensor(lo[n][:, :], stage[i % NST][:, :], WSCALE, hi[n][:, :], ALU.mult,
                                         ALU.subtract).then_inc(lo_done, 1)


def layer3(nc, a, out, x_sb, ident, half_neg, passed, sb_in, psum_in, sem):
    stack = ExitStack()
    with stack:
        sb = sb_in(stack)
        wr = sb("wr", [P, KD, E], F32)
        br = sb("br", [T, E], F32)
        b1, b2 = sb("c_b1", [P, E, FF // P], F32), sb("c_b2", [P, E, KD], F32)
        rev = sb("rev", [T, E], F32)
        slot_id = sb("slot_id", [T, CAP], F32)
        earlier = sb("earlier", [T, T], F32)
        FAR = 1024.0
        probs = sb("probs", [T, B, E], F32)
        place = sb("place", [T, B, E], F32)
        gather = sb("gather", [T, B, SLOTS], F16)
        y_t = sb("y_t", [P, KD, E, ES], F32)
        w1_loaded = [sem(f"c_w1_loaded{i}") for i in range(2)]
        w2_loaded = [sem(f"c_w2_loaded{i}") for i in range(2)]

        mid = ExitStack()
        with mid:
            sbm = sb_in(mid)
            w1_raw, w2_raw = sbm("w1_raw", [P, 2, WCOLS], F32), sbm("w2_raw", [P, 2, WCOLS], F32)
            buf_hi, buf_lo = (sbm(f"buf_{n}", [P, KD, E, ES], F16) for n in ("hi", "lo"))

            def load_expert(sp, e, par):
                sp.dma_start(w1_raw[:, par, :].rearrange("p (k n) -> p k n", k=KD),
                             a["L0_ffn_W1"][bass.ds(e, 1), :, :].rearrange("a (k p) n -> p (a k) n", p=P)).then_inc(w1_loaded[par], 16)
                sp.dma_start(w2_raw[:, par, :].rearrange("p (k n) -> p k n", n=D),
                             a["L0_ffn_W2"][bass.ds(e, 1), :, :].rearrange("a (k p) n -> p (a k) n", p=P)).then_inc(w2_loaded[par], 16)

            route(nc, a, x_sb, ident, passed, wr, br, b1, b2, rev, slot_id, earlier, FAR, probs, place, load_expert, sb_in, psum_in, sem)
            dispatch(nc, x_sb, slot_id, place, gather, buf_hi, buf_lo, sb_in, psum_in, sem)
            experts(nc, passed, w1_raw, w2_raw, w1_loaded, w2_loaded, load_expert, b1, b2, buf_hi, buf_lo, y_t, sb_in, psum_in, sem)
        combine(nc, out, x_sb, ident, half_neg, passed, probs, gather, y_t, sb_in, psum_in, sem)


def route(nc, a, x_sb, ident, passed, wr, br, b1, b2, rev, slot_id, earlier, FAR, probs, place, load_expert, sb_in, psum_in, sem):
    stack = ExitStack()
    with stack:
        sb, psum = sb_in(stack), psum_in(stack)
        xs = sb("r_xs", [T, 2, G4, D], F32)
        xt = sb("r_xt", [P, 2, KD, GT], F32)
        logits = sb("logits", [T, B, E], F32)
        work = {n: sb(f"r_{n}", [T, B, E], F32) for n in ("exp", "eq", "one", "two", "left")}
        top = {n: sb(f"r_{n}", [T, B], F32) for n in ("max", "sum", "rec", "max1", "id1", "max2", "id2")}
        turn_ps = [psum(f"r_turn{i}", [P, 512]) for i in range(2 * KD)]
        logit_ps = [psum(f"r_logit{i}", [P, 512]) for i in range(2)]
        count_ps = psum("r_count", [P, 512])
        vec_loaded, const_done, xs_done, turn_ready, xt_done, logit_ready, logit_done = (
            sem(f"r_{n}") for n in ("vec_loaded", "const_done", "xs_done", "turn_ready", "xt_done", "logit_ready", "logit_done"))
        step, exp_done, count_ready = sem("r_step"), sem("r_exp_done"), sem("r_count_ready")
        block = stack.enter_context(nc.Block())

        def groups(eng, body):
            body(0, 0)
            body(1, 1)
            with eng.Fori(1, NG // 2) as i:
                for par in range(2):
                    body(2 * i + par, par)

        @block.sync
        def _(sp):
            sp.dma_start(wr[:, :, :], a["L0_ffn_Wr"].rearrange("(k p) e -> p k e", p=P)).then_inc(vec_loaded, 16)
            sp.dma_start(br[:, :], a["L0_ffn_br"].partition_broadcast(T)).then_inc(vec_loaded, 16)
            for e in range(E):
                sp.dma_start(b1[:, e, :], a["L0_ffn_b1"][e, :].rearrange("(f p) -> p f", p=P),
                             allow_slow_non_contiguous=True).then_inc(vec_loaded, 16)
                sp.dma_start(b2[:, e, :], a["L0_ffn_b2"][e, :].rearrange("(f p) -> p f", p=P),
                             allow_slow_non_contiguous=True).then_inc(vec_loaded, 16)
            for e in range(2):
                load_expert(sp, e, e)
            sp.wait_ge(vec_loaded, 16 * (2 + 2 * E))

        @block.gpsimd
        def _(pool):
            for e in range(E):
                ins = pool.memset(rev[:, e:e + 1], float(E - e))
            ins.then_inc(const_done, 1)
            for c in range(CAP):
                ins = pool.memset(slot_id[:, c:c + 1], c - FAR)
            ins.then_inc(const_done, 1)
            pool.memset(earlier[:, :], 1.0).then_inc(const_done, 1)
            pool.wait_ge(const_done, 3)
            pool.affine_select(out=earlier[:, :], in_=earlier[:, :], compare_op=ALU.is_gt, fill=0.0, base=0,
                               pattern=[[1, T]], channel_multiplier=-1).then_inc(const_done, 1)

            def body(g, par):
                settle(pool, passed, (turn_ready, g - 1))
                pool.tensor_copy(xs[:, par, :, :], x_sb[:, bass.ds(G4 * g, G4), :]).then_inc(xs_done, 1)

            groups(pool, body)

        @block.tensor
        def _(pe):
            pe.wait_ge(vec_loaded, 16 * (2 + 2 * E))

            def body(g, par):
                pe.wait_ge(xs_done, g + 1)
                at_least(pe, xt_done, g - 1)
                for k in range(KD):
                    for b in range(G4):
                        mm = pe.transpose(turn_ps[2 * par + k][:, b * T:(b + 1) * T], xs[:, par, b, k * P:(k + 1) * P], ident[0:T, 0:T])
                mm.then_inc(turn_ready, 1)
                pe.wait_ge(xt_done, g + 1)
                at_least(pe, logit_done, g - 1)
                for b in range(G4):
                    for k in range(KD):
                        mm = pe.matmul(logit_ps[par][0:T, b * E:(b + 1) * E], xt[:, par, k, b * T:(b + 1) * T], wr[:, k, :],
                                       start=(k == 0), stop=(k == KD - 1))
                mm.then_inc(logit_ready, 1)

            groups(pe, body)
            pe.wait_ge(step, 16)
            pe.wait_ge(const_done, 4)
            pe.matmul(count_ps[0:T, 0:B * E], earlier[:, :], work["left"][:, :, :].rearrange("p b e -> p (b e)"),
                      start=True, stop=True).then_inc(count_ready, 1)

        @block.scalar
        def _(act):
            def body(g, par):
                act.wait_ge(turn_ready, g + 1)
                at_least(act, logit_ready, g - 1)
                for k in range(KD):
                    ins = act.activation(xt[:, par, k, :], turn_ps[2 * par + k][:, 0:GT], ACT.Identity)
                ins.then_inc(xt_done, 1)

            groups(act, body)
            act.wait_ge(step, 2)
            act.activation(work["exp"][:, :, :], logits[:, :, :], ACT.Exp).then_inc(exp_done, 1)

        @block.vector
        def _(dve):
            dve.wait_ge(vec_loaded, 16 * (2 + 2 * E))

            def body(g, par):
                dve.wait_ge(logit_ready, g + 1)
                dve.tensor_tensor(logits[:, bass.ds(G4 * g, G4), :], logit_ps[par][0:T, 0:G4 * E].rearrange("p (b e) -> p b e", e=E),
                                  br[:, :].unsqueeze(1).to_broadcast([T, G4, E]), ALU.add).then_inc(logit_done, 1)

            groups(dve, body)
            dve.wait_ge(logit_done, NG)
            dve.wait_ge(const_done, 2)
            count = [0]

            def then(ins):
                count[0] += 1
                ins.then_inc(step, 1)
                dve.wait_ge(step, count[0])

            over = lambda t: t[:, :].unsqueeze(2).to_broadcast([T, B, E])
            revs = rev[:, :].unsqueeze(1).to_broadcast([T, B, E])
            w = {n: t[:, :, :] for n, t in work.items()}
            then(dve.tensor_reduce(top["max"][:, :], logits[:, :, :], AXX, ALU.max))
            then(dve.tensor_tensor(logits[:, :, :], logits[:, :, :], over(top["max"]), ALU.subtract))
            dve.wait_ge(exp_done, 1)
            then(dve.tensor_reduce(top["sum"][:, :], w["exp"], AXX, ALU.add))
            then(dve.reciprocal(top["rec"][:, :], top["sum"][:, :]))
            then(dve.tensor_tensor(probs[:, :, :], w["exp"], over(top["rec"]), ALU.mult))
            then(dve.tensor_reduce(top["max1"][:, :], probs[:, :, :], AXX, ALU.max))
            then(dve.tensor_tensor(w["eq"], probs[:, :, :], over(top["max1"]), ALU.is_equal))
            then(dve.tensor_tensor(w["eq"], w["eq"], revs, ALU.mult))
            then(dve.tensor_reduce(top["id1"][:, :], w["eq"], AXX, ALU.max))
            then(dve.tensor_tensor(w["one"], revs, over(top["id1"]), ALU.is_equal))
            then(dve.scalar_tensor_tensor(w["left"], w["one"], -4.0, probs[:, :, :], ALU.mult, ALU.add))
            then(dve.tensor_reduce(top["max2"][:, :], w["left"], AXX, ALU.max))
            then(dve.tensor_tensor(w["eq"], w["left"], over(top["max2"]), ALU.is_equal))
            then(dve.tensor_tensor(w["eq"], w["eq"], revs, ALU.mult))
            then(dve.tensor_reduce(top["id2"][:, :], w["eq"], AXX, ALU.max))
            dve.tensor_tensor(w["two"], revs, over(top["id2"]), ALU.is_equal).then_inc(exp_done, 1)
            dve.wait_ge(exp_done, 2)
            then(dve.tensor_tensor(w["left"], w["one"], w["two"], ALU.add))
            dve.wait_ge(count_ready, 1)
            dve.scalar_tensor_tensor(place[:, :, :].rearrange("p b e -> p (b e)"), w["left"].rearrange("p b e -> p (b e)"), -FAR,
                                     count_ps[0:T, 0:B * E], ALU.mult, ALU.add).then_inc(step, 1)


def dispatch(nc, x_sb, slot_id, place, gather, buf_hi, buf_lo, sb_in, psum_in, sem):
    stack = ExitStack()
    with stack:
        sb, psum = sb_in(stack), psum_in(stack)
        x_hi, x_lo = (sb(f"d_x_{n}", [T, 2, G4, D], F16) for n in ("hi", "lo"))
        hi_ps = [psum(f"d_hi{i}", [P, 512]) for i in range(G4)]
        lo_ps = [psum(f"d_lo{i}", [P, 512]) for i in range(G4)]
        gather_done, x_hi_done, x_lo_done, hi_ready, lo_ready, hi_done, lo_done = (
            sem(f"d_{n}") for n in ("gather_done", "x_hi_done", "x_lo_done", "hi_ready", "lo_ready", "hi_done", "lo_done"))
        block = stack.enter_context(nc.Block())

        def groups(eng, body):
            body(0, 0)
            body(1, 1)
            with eng.Fori(1, NG // 2) as i:
                for par in range(2):
                    body(2 * i + par, par)

        def slots_of(buf, b):
            return buf[:, :, :, bass.ds(b * CAP, CAP)]

        @block.scalar
        def _(act):
            def split(g, par):
                at_least(act, lo_ready, G4 * (g - 1))
                act.activation(x_hi[:, par, :, :], x_sb[:, bass.ds(G4 * g, G4), :], ACT.Identity).then_inc(x_hi_done, 1)

            def body(g, par):
                split(g, par)
                for b in range(G4):
                    act.wait_ge(hi_ready, G4 * g + b + 1)
                    act.activation(slots_of(buf_hi, G4 * g + b), hi_ps[b][:, 0:KD * SLOTS].rearrange("p (k e c) -> p k e c", k=KD, e=E),
                                   ACT.Identity).then_inc(hi_done, 1)

            groups(act, body)

        @block.vector
        def _(dve):
            def body(g, par):
                at_b = bass.ds(G4 * g, G4)
                dve.tensor_tensor(gather[:, at_b, :].rearrange("p b (e c) -> p (b e) c", c=CAP),
                                  place[:, at_b, :].rearrange("p b e -> p (b e)").unsqueeze(2).to_broadcast([T, G4 * E, CAP]),
                                  slot_id[:, :].unsqueeze(1).to_broadcast([T, G4 * E, CAP]), ALU.is_equal).then_inc(gather_done, 1)
                dve.wait_ge(x_hi_done, g + 1)
                at_least(dve, lo_ready, G4 * (g - 1))
                dve.tensor_tensor(x_lo[:, par, :, :], x_sb[:, at_b, :], x_hi[:, par, :, :], ALU.subtract).then_inc(x_lo_done, 1)
                for b in range(G4):
                    dve.wait_ge(lo_ready, G4 * g + b + 1)
                    dve.tensor_copy(slots_of(buf_lo, G4 * g + b),
                                    lo_ps[b][:, 0:KD * SLOTS].rearrange("p (k e c) -> p k e c", k=KD, e=E)).then_inc(lo_done, 1)

            groups(dve, body)

        @block.tensor
        def _(pe):
            def body(g, par):
                pe.wait_ge(gather_done, g + 1)
                pe.wait_ge(x_lo_done, g + 1)
                for b in range(G4):
                    at_least(pe, hi_done, G4 * (g - 1) + b + 1)
                    at_least(pe, lo_done, G4 * (g - 1) + b + 1)
                    for src, ps, done in ((x_hi, hi_ps, hi_ready), (x_lo, lo_ps, lo_ready)):
                        for k in range(KD):
                            mm = pe.matmul(ps[b][:, k * SLOTS:(k + 1) * SLOTS], src[:, par, b, k * P:(k + 1) * P],
                                           gather[:, bass.ds(G4 * g + b, 1), :].rearrange("p a s -> p (a s)"), start=True, stop=True)
                        mm.then_inc(done, 1)

            groups(pe, body)


def experts(nc, passed, w1_raw, w2_raw, w1_loaded, w2_loaded, load_expert, b1, b2, buf_hi, buf_lo, y_t, sb_in, psum_in, sem):
    stack = ExitStack()
    with stack:
        sb, psum = sb_in(stack), psum_in(stack)
        FT, HALF = FF // P, ES // 2
        w1_hi, w1_lo, w2_hi, w2_lo = (sb(f"e_{n}", [P, 2, WCOLS], F16) for n in ("w1_hi", "w1_lo", "w2_hi", "w2_lo"))
        h_hi, h_lo = (sb(f"e_h_{n}", [P, FT, ES], F16) for n in ("hi", "lo"))
        r32 = sb("r32", [P, 2, ES], F32)
        NPB = 4
        pb = [psum(f"e_pb{i}", [P, 2, 512]) for i in range(NPB)]
        USES = FT + KD
        pb_ready = sem("e_pb_ready")
        pb_free = [sem(f"e_pb_free{i}") for i in range(NPB)]
        w_hi_done, w_lo_done, relu_done, h_hi_done, h_lo_done = (
            sem(f"e_{n}") for n in ("w_hi_done", "w_lo_done", "relu_done", "h_hi_done", "h_lo_done"))
        block = stack.enter_context(nc.Block())

        def each(eng, body):
            for par in range(2):
                body(0, par)
            with eng.Fori(1, E // 2 - 1) as i:
                for par in range(2):
                    body(i, par)
            for par in range(2):
                body(E // 2 - 1, par)

        def is_last(i, par):
            return isinstance(i, int) and i == E // 2 - 1 and par == 1

        def ready(i, par, use):
            return 2 * USES * i + USES * par + use + 1

        def freed(i, par, use):
            return 2 * USES // NPB * i + (USES * par + use) // NPB + 1

        def bank(par, use):
            return (USES * par + use) % NPB

        def of_expert(t, k, e):
            return t[:, k, bass.ds(e, 1), :].rearrange("p a n -> p (a n)")

        @block.sync
        def _(sp):
            def load(i, par):
                settle(sp, passed, (w_lo_done, 2 * (2 * i + par - 2) + 2))
                load_expert(sp, 2 * i + par, par)

            for par in range(2):
                load(1, par)
            with sp.Fori(2, E // 2) as i:
                for par in range(2):
                    load(i, par)

        def next_expert(i, par):
            return (i, 1) if par == 0 else (i + 1, 0)

        @block.scalar
        def _(act):
            def split(i, par, which):
                raw, loaded, hi = ((w1_raw, w1_loaded, w1_hi), (w2_raw, w2_loaded, w2_hi))[which]
                act.wait_ge(loaded[par], 16 * (i + 1))
                if not (isinstance(i, int) and i == 0):
                    act.wait_ge(pb_ready, ready(i - 1, par, (FT, USES)[which] - 1))
                act.activation(hi[:, par, :], raw[:, par, :], ACT.Identity, scale=WSCALE).then_inc(w_hi_done, 1)

            def body(i, par):
                e = 2 * i + par
                for f in range(FT):
                    act.wait_ge(pb_ready, ready(i, par, f))
                    at_least(act, h_lo_done, FT * e + f - 1)
                    act.activation(r32[:, f % 2, :].rearrange("p (a n) -> p a n", a=2), pb[bank(par, f)][:, :, 0:HALF], ACT.Relu,
                                   bias=b1[:, bass.ds(e, 1), f], scale=UNSCALE).then_inc(pb_free[bank(par, f)], 1)
                    if f in (1, 4) and not is_last(i, par):
                        split(*next_expert(i, par), (1, 4).index(f))
                for c in range(KD):
                    use = FT + c
                    act.wait_ge(pb_ready, ready(i, par, use))
                    act.activation(of_expert(y_t, c, e).rearrange("p (a n) -> p a n", a=2), pb[bank(par, use)][:, :, 0:HALF],
                                   ACT.Identity, bias=b2[:, bass.ds(e, 1), c], scale=UNSCALE).then_inc(pb_free[bank(par, use)], 1)

            for which in range(2):
                split(0, 0, which)
            each(act, body)

        @block.vector
        def _(dve):
            def split(i, par, which):
                raw, hi, lo = ((w1_raw, w1_hi, w1_lo), (w2_raw, w2_hi, w2_lo))[which]
                dve.wait_ge(w_hi_done, 2 * (2 * i + par) + which + 1)
                dve.scalar_tensor_tensor(lo[:, par, :], raw[:, par, :], WSCALE, hi[:, par, :], ALU.mult,
                                         ALU.subtract).then_inc(w_lo_done, 1)

            def body(i, par):
                e = 2 * i + par
                for f in range(FT):
                    dve.wait_ge(h_hi_done, FT * e + f + 1)
                    dve.tensor_tensor(h_lo[:, f, :], r32[:, f % 2, :], h_hi[:, f, :], ALU.subtract).then_inc(h_lo_done, 1)
                    if f in (1, 4) and not is_last(i, par):
                        split(*next_expert(i, par), (1, 4).index(f))

            for which in range(2):
                split(0, 0, which)
            each(dve, body)

        @block.gpsimd
        def _(pool):
            def body(i, par):
                e = 2 * i + par
                if par == 1:
                    pool.wait_ge(pb_ready, ready(i, 0, USES - 1))
                elif not (isinstance(i, int) and i == 0):
                    pool.wait_ge(pb_ready, ready(i - 1, 1, USES - 1))
                for f in range(FT):
                    settle(pool, passed, (pb_free[bank(par, f)], freed(i, par, f)))
                    pool.tensor_copy(h_hi[:, f, :], r32[:, f % 2, :]).then_inc(h_hi_done, 1)

            each(pool, body)

        @block.tensor
        def _(pe):
            def claim(i, par, use):
                at_least(pe, pb_free[bank(par, use)], freed(i, par, use) - 1)
                return pb[bank(par, use)]

            def body(i, par):
                e = 2 * i + par
                pe.wait_ge(w_lo_done, 2 * e + 1)
                for f in range(FT):
                    ps = claim(i, par, f)
                    for n in range(2):
                        cols = slice(n * HALF, (n + 1) * HALF)
                        for k in range(KD):
                            c0 = k * FF + f * P
                            mm = split_product(pe, ps[:, n, 0:HALF], (w1_hi[:, par, c0:c0 + P], w1_lo[:, par, c0:c0 + P]),
                                               (of_expert(buf_hi, k, e)[:, cols], of_expert(buf_lo, k, e)[:, cols]),
                                               k == 0, k == KD - 1)
                    mm.then_inc(pb_ready, 1)
                pe.wait_ge(w_lo_done, 2 * e + 2)
                for c in range(KD):
                    ps = claim(i, par, FT + c)
                    for n in range(2):
                        cols = slice(n * HALF, (n + 1) * HALF)
                        for f in range(FT):
                            if c == 0 and n == 0:
                                pe.wait_ge(h_lo_done, FT * e + f + 1)
                            c0 = f * D + c * P
                            mm = split_product(pe, ps[:, n, 0:HALF], (w2_hi[:, par, c0:c0 + P], w2_lo[:, par, c0:c0 + P]),
                                               (h_hi[:, f, cols], h_lo[:, f, cols]), f == 0, f == FT - 1)
                    mm.then_inc(pb_ready, 1)

            each(pe, body)


def combine(nc, out, x_sb, ident, half_neg, passed, probs, gather, y_t, sb_in, psum_in, sem):
    stack = ExitStack()
    with stack:
        sb, psum = sb_in(stack), psum_in(stack)
        HS = SLOTS // 2
        yb = sb("yb", [P, 2, KD, SLOTS], F32)
        gw = sb("gw", [T, 2, SLOTS], F32)
        gw_t = sb("gw_t", [HS, 2, 2 * T], F32)
        y_n = sb("y_n", [HS, 2, 2 * D], F32)
        z = sb("c_z", [T, 2, G4, D], F32)
        zo = sb("c_zo", [T, 2, G4, D], F32)
        stats, mom, rstd = sb("c_stats", [T, G4, 6], F32), sb("c_mom", [T, G4, 2], F32), sb("c_rstd", [T, G4], F32)
        g_ps = [psum(f"c_g{i}", [P, 512]) for i in range(2)]
        y_ps = [psum(f"c_y{i}", [P, 512]) for i in range(2)]
        o_ps = [psum(f"c_o{i}", [P, 512]) for i in range(2)]
        yb_done, gw_done, g_ready, y_ready, gw_t_done, y_n_done, o_ready, z_done = (
            sem(f"c_{n}") for n in ("yb_done", "gw_done", "g_ready", "y_ready", "gw_t_done", "y_n_done", "o_ready", "z_done"))
        stats_done, mom_done, eps_done, rstd_done, zo_done = (
            sem(f"c_{n}") for n in ("stats_done", "mom_done", "eps_done", "rstd_done", "zo_done"))
        stored = [sem(f"c_stored{i}") for i in range(2)]
        block = stack.enter_context(nc.Block())

        def groups(eng, body):
            body(0, 0)
            body(1, 1)
            with eng.Fori(1, NG // 2) as i:
                for par in range(2):
                    body(2 * i + par, par)

        @block.gpsimd
        def _(pool):
            def copies(g):
                for q in range(G4):
                    b = G4 * g + q
                    settle(pool, passed, (y_ready, b - 1))
                    pool.tensor_copy(yb[:, q % 2, :, :].rearrange("p k (e c) -> p k e c", c=CAP),
                                     y_t[:, :, :, bass.ds(b * CAP, CAP)]).then_inc(yb_done, 1)

            def body(g, par):
                copies(g)
                settle(pool, passed, (mom_done, g + 1))
                pool.tensor_scalar(rstd[:, :], mom[:, :, 1], EPS, None, ALU.add).then_inc(eps_done, 1)
                pool.wait_ge(eps_done, g + 1)
                pool.tensor_tensor(rstd[:, :], rstd[:, :], half_neg[0:T, :], ALU.pow).then_inc(rstd_done, 1)

            groups(pool, body)

        @block.vector
        def _(dve):
            def weights(b, q):
                at_least(dve, g_ready, b - 1)
                dve.tensor_tensor(gw[:, q % 2, :].rearrange("p (e c) -> p e c", c=CAP),
                                  gather[:, bass.ds(b, 1), :].rearrange("p a (e c) -> p (a e) c", c=CAP),
                                  probs[:, bass.ds(b, 1), :].rearrange("p a e -> p (a e)").unsqueeze(2).to_broadcast([T, E, CAP]),
                                  ALU.mult).then_inc(gw_done, 1)

            def body(g, par):
                for q in range(G4 + 1):
                    if q < G4:
                        weights(G4 * g + q, q)
                    if q >= 1:
                        b = G4 * g + q - 1
                        dve.wait_ge(o_ready, b + 1)
                        if q == 1:
                            at_least(dve, zo_done, g - 1)
                        dve.tensor_tensor(z[:, par, q - 1, :], o_ps[(q - 1) % 2][0:T, 0:D],
                                          x_sb[:, bass.ds(b, 1), :].rearrange("p a d -> p (a d)"), ALU.add).then_inc(z_done, 1)
                dve.wait_ge(z_done, G4 * (g + 1))
                at_least(dve, mom_done, g)
                for q in range(G4):
                    ins = dve.bn_stats(stats[:, q, :], z[:, par, q, :])
                ins.then_inc(stats_done, 1)
                settle(dve, passed, (stats_done, g + 1), (zo_done, g))
                for q in range(G4):
                    ins = dve.bn_aggr(mom[:, q, :], stats[:, q, :])
                ins.then_inc(mom_done, 1)
                dve.wait_ge(rstd_done, g + 1)
                if not (isinstance(g, int) and g < 2):
                    dve.wait_ge(stored[par], stored_before(g))
                for q in range(G4):
                    ins = dve.tensor_scalar(zo[:, par, q, :], z[:, par, q, :], mom[:, q, 0:1], rstd[:, q:q + 1], ALU.subtract, ALU.mult)
                ins.then_inc(zo_done, 1)

            pairs = [None]

            def stored_before(g):
                return 16 * pairs[0]

            body(0, 0)
            body(1, 1)
            with dve.Fori(1, NG // 2) as i:
                pairs[0] = i
                for par in range(2):
                    body(2 * i + par, par)

        @block.scalar
        def _(act):
            def body(g, par):
                for q in range(G4):
                    b = G4 * g + q
                    act.wait_ge(g_ready, b + 1)
                    at_least(act, o_ready, b - 1)
                    act.activation(gw_t[:, q % 2, :], g_ps[q % 2][0:HS, 0:2 * T], ACT.Identity).then_inc(gw_t_done, 1)
                    act.wait_ge(y_ready, b + 1)
                    act.activation(y_n[:, q % 2, :], y_ps[q % 2][0:HS, :], ACT.Identity).then_inc(y_n_done, 1)

            groups(act, body)

        @block.tensor
        def _(pe):
            def turn(b, q):
                pe.wait_ge(gw_done, b + 1)
                at_least(pe, gw_t_done, b - 1)
                for s in range(2):
                    mm = pe.transpose(g_ps[q % 2][0:HS, s * T:(s + 1) * T], gw[:, q % 2, s * HS:(s + 1) * HS], ident[0:T, 0:T])
                mm.then_inc(g_ready, 1)
                pe.wait_ge(yb_done, b + 1)
                at_least(pe, y_n_done, b - 1)
                for s in range(2):
                    for k in range(KD):
                        mm = pe.transpose(y_ps[q % 2][0:HS, s * D + k * P:s * D + (k + 1) * P],
                                          yb[:, q % 2, k, s * HS:(s + 1) * HS], ident[:, :])
                mm.then_inc(y_ready, 1)

            def bring_back(b, q):
                pe.wait_ge(gw_t_done, b + 1)
                pe.wait_ge(y_n_done, b + 1)
                at_least(pe, z_done, b - 1)
                for s in range(2):
                    mm = pe.matmul(o_ps[q % 2][0:T, 0:D], gw_t[:, q % 2, s * T:(s + 1) * T], y_n[:, q % 2, s * D:(s + 1) * D],
                                   start=(s == 0), stop=(s == 1))
                mm.then_inc(o_ready, 1)

            def body(g, par):
                for q in range(G4 + 1):
                    if q < G4:
                        turn(G4 * g + q, q)
                    if q >= 1:
                        bring_back(G4 * g + q - 1, q - 1)

            groups(pe, body)

        @block.sync
        def _(sp):
            def body(g, par):
                sp.wait_ge(zo_done, g + 1)
                sp.dma_start(out[bass.ds(G4 * g, G4), :, :].rearrange("b t d -> t b d"), zo[:, par, :, :]).then_inc(stored[par], 16)

            groups(sp, body)
            for par in range(2):
                sp.wait_ge(stored[par], 16 * NG // 2)


_INS = ['x', 'ctx_1024', 'mask_BxS2_bf1', 'L0_attn_wq', 'L0_attn_wk', 'L0_attn_wv', 'L0_attn_wo', 'L0_attn_proj',
        'L0_attn_w1', 'L0_attn_b1', 'L0_attn_w2', 'L0_attn_b2', 'L0_attn_g1', 'L0_attn_beta1', 'L0_attn_g2',
        'L0_attn_beta2', 'L0_xattn_norm_w', 'L0_xattn_norm_b', 'L0_xattn_ctx_norm_w', 'L0_xattn_ctx_norm_b',
        'L0_xattn_Wq', 'L0_xattn_Wkv', 'L0_xattn_Wo', 'L0_ffn_Wr', 'L0_ffn_br', 'L0_ffn_W1', 'L0_ffn_b1',
        'L0_ffn_W2', 'L0_ffn_b2']


def kernel(**inputs):
    import numpy as _np
    import concourse.bacc as _bacc
    from concourse.bass_utils import run_bass_kernel_spmd as _run

    nc = _bacc.Bacc("TRN2", target_bir_lowering=False, num_devices=1)
    arrays, args = {}, {}
    for name in _INS:
        a = _np.ascontiguousarray(inputs[name])
        if a.dtype == _np.bool_:
            a = a.view(_np.uint8)
        arrays[f"in_{name}_dram"] = a
        args[name] = nc.dram_tensor(f"in_{name}_dram", a.shape, mybir.dt.from_np(a.dtype), kind="ExternalInput").ap()
    out = nc.dram_tensor("out_dram", (B, T, D), F32, kind="ExternalOutput").ap()
    decoder_kernel(nc, args, out)
    r = _run(nc, [arrays], core_ids=[0])
    return r.results[0]["out_dram"]
```

```python
from contextlib import ExitStack

import concourse.bass as bass
from concourse import mybir

F32 = mybir.dt.float32
F16 = mybir.dt.float16
U8 = mybir.dt.uint8
ALU = mybir.AluOpType
ACT = mybir.ActivationFunctionType
AXX = mybir.AxisListType.X

P = 128
B, T, D = 32, 112, 256
S2 = 375
H, DH = 16, 64
INNER = H * DH
FF = 1024
KD = D // P
KI = INNER // P
E = 8
CAP = max(1, int(T / E * 1.25))
SLOTS = E * CAP
ES = B * CAP
G4 = 4
NG = B // G4
GT = G4 * T
JT, JP = 3, S2 // 3
WSCALE = 64.0
UNSCALE = 1.0 / WSCALE
EPS = 1e-5
MASKED = 3.0e38
WCOLS = KD * INNER


def at_least(eng, sem, n):
    if isinstance(n, int) and n <= 0:
        return
    eng.wait_ge(sem, n)


def settle(eng, passed, *waits):
    for sem, n in waits:
        at_least(eng, sem, n)
    eng.sem_inc(passed, 1)


def split_product(pe, out, lhs, rhs, first, last):
    (lh, ll), (rh, rl) = lhs, rhs
    pe.matmul(out, lh, rh, start=first, stop=False)
    pe.matmul(out, lh, rl, start=False, stop=False)
    return pe.matmul(out, ll, rh, start=False, stop=last)


def decoder_kernel(nc, a, out):
    root = ExitStack()
    with root:
        def sem(name):
            return root.enter_context(nc.semaphore(name))

        def sb_in(stack):
            return lambda name, shape, dt: stack.enter_context(nc.sbuf_tensor(name, shape, dt))

        def psum_in(stack):
            return lambda name, shape, dt=F32: stack.enter_context(nc.psum_tensor(name, shape, dt))

        sb = sb_in(root)
        x_sb = sb("x_sb", [T, B, D], F32)
        ident = sb("ident", [P, P], F32)
        half_neg = sb("half_neg", [P, 4], F32)
        consts_done = sem("consts_done")
        passed = sem("passed")

        layer1(nc, a, x_sb, ident, half_neg, consts_done, passed, sb_in, psum_in, sem)
        layer2(nc, a, x_sb, ident, half_neg, passed, sb_in, psum_in, sem)
        layer3(nc, a, out, x_sb, ident, half_neg, passed, sb_in, psum_in, sem)


def layer1(nc, a, x_sb, ident, half_neg, consts_done, passed, sb_in, psum_in, sem):
    stack = ExitStack()
    with stack:
        sb, psum = sb_in(stack), psum_in(stack)
        names = ["wq", "wk", "wv", "wo", "w1", "w2"]
        hi = {n: sb(f"a_{n}_hi", [P, WCOLS], F16) for n in names}
        lo = {n: sb(f"a_{n}_lo", [P, WCOLS], F16) for n in names}
        g1, be1, g2, be2 = (sb(f"a_{n}", [P, KD], F32) for n in ("g1", "be1", "g2", "be2"))
        b1 = sb("a_b1", [P, FF // P], F32)
        b2 = sb("a_b2", [T, D], F32)
        causal = sb("causal", [T, T], F32)
        load_layer1(nc, a, x_sb, ident, half_neg, consts_done, causal, hi, lo, (g1, be1, g2, be2, b1, b2), sb_in, psum_in, sem)

        def pair(name, k, c0, n, width):
            c = k * width + c0
            return hi[name][:, c:c + n], lo[name][:, c:c + n]

        FT = FF // P
        LNS = 3
        NSM = 2
        xh = sb("xh", [T, G4, D], F32)
        h32 = sb("h32", [P, KD, GT], F32)
        h_hi, h_lo = (sb(f"h_{n}", [P, 2, KD, GT], F16) for n in ("hi", "lo"))
        neg_relu = sb("neg_relu", [P, 2, GT], F32)
        phi_exp = sb("phi_exp", [P, 2, GT], F32)
        qt = sb("qt", [P, KI, GT], F32)
        kz = sb("kz", [P, H, GT], F32)
        v1 = sb("v1", [P, G4, H, DH + 1], F32)
        sm = sb("sm", [P, NSM, 4 * T], F32)
        rec = sb("rec", [T, 2, 4], F32)
        o32 = sb("o32", [T, 4, 4 * DH], F32)
        o_hi, o_lo = (sb(f"o_{n}", [P, 2, KI, T], F16) for n in ("hi", "lo"))
        x1 = sb("x1", [T, G4, D], F32)
        xsum = sb("xsum", [T, G4, D], F32)
        gelu32 = neg_relu
        ff = sb("ff", [P, 2, FT, GT], F16)
        ff_hi, ff_lo = ff[:, 0, :, :], ff[:, 1, :, :]
        late_stage = ff[:, :, :, :].rearrange("p a f t -> p (a f t)").bitcast(F32)[:, 0:WCOLS]
        late = ("wv", "wo", "w1", "w2")
        stats = sb("a_stats", [T, LNS, G4, 6], F32)
        mom = sb("a_mom", [T, LNS, G4, 2], F32)
        rstd = sb("a_rstd", [T, LNS, G4], F32)

        NPB = 4
        pb = [psum(f"a_pb{i}", [P, 512]) for i in range(NPB)]
        s_ps = [psum(f"a_s{i}", [P, 512]) for i in range(2)]
        o_ps = [psum(f"a_o{i}", [P, 512]) for i in range(2)]

        def several(kind, n):
            return [(kind, i) for i in range(n)]

        PRE = several("T1", KD) + several("Q", KI) + several("K", KI) + several("V", 2 * G4)
        UNITS = G4 * H // 4
        STEPS = UNITS + 8
        VALUES_AT, TURN_AT = 2, 4
        W_AT = 9
        T1_AT, Q_AT = 15, 20
        SPLIT_AT = 12
        EARLY = 2

        K, K_EARLY = several("K", KI), 2
        V, V_EARLY = several("V", 2 * G4), 2

        def attention_uses(last):
            uses = []
            for t in range(STEPS):
                if TURN_AT <= t < UNITS + TURN_AT and (t - TURN_AT) % 2 == 0:
                    uses.append(("O", (t - TURN_AT) // 2))
                if t == T1_AT and not last:
                    uses += several("T1", KD)
                if t == Q_AT and not last:
                    uses += several("Q", EARLY)
                if t >= W_AT and (t - W_AT) % 4 == 0:
                    uses.append(("W", (t - W_AT) // 4))
            return uses

        MAIN = (attention_uses(False) + several("Q", KI)[EARLY:] + K[:K_EARLY] + several("T2", KD) + K[K_EARLY:]
                + V[:V_EARLY] + several("F", FT) + V[V_EARLY:] + several("Y", G4))
        LAST = attention_uses(True) + several("T2", KD) + several("F", FT) + several("Y", G4)
        PER = len(MAIN)
        assert PER % NPB == 0

        def use(g, kind, i):
            if kind in ("T1", "Q", "K", "V"):
                if isinstance(g, int) and g == 0:
                    return 0, PRE.index((kind, i))
                return g - 1, len(PRE) + MAIN.index((kind, i))
            return g, len(PRE) + (LAST if is_last(g) else MAIN).index((kind, i))

        def ready(u):
            return PER * u[0] + u[1] + 1

        def freed(u):
            return PER // NPB * u[0] + u[1] // NPB + 1

        def bank(u):
            return pb[u[1] % NPB]

        def free_of(u):
            return pb_free[u[1] % NPB]

        def is_first(g):
            return isinstance(g, int) and g == 0

        def is_last(g):
            return isinstance(g, int) and g == NG - 1

        def groups(eng, body):
            body(0)
            with eng.Fori(1, NG - 1) as g:
                body(g)
            body(NG - 1)

        pb_ready = sem("a_pb_ready")
        pb_free = [sem(f"a_pb_free{i}") for i in range(NPB)]
        stats_done, mom_done, eps_done, rstd_done, rows_done = (
            [sem(f"a_{n}{i}") for i in range(LNS)] for n in ("stats_done", "mom_done", "eps_done", "rstd_done", "rows_done"))
        h_hi_done = [sem(f"a_h_hi_done{i}") for i in range(2)]
        kz_zeroed, pads_done = sem("a_kz_zeroed"), sem("a_pads_done")
        relu_done, exp_done = sem("a_relu_done"), sem("a_exp_done")
        s_ready, s_masked, av_done, rec_done, o_done, o_hi_done = (
            sem(f"a_{n}") for n in ("s_ready", "s_masked", "av_done", "rec_done", "o_done", "o_hi_done"))
        xs1_done, xs_done = sem("a_xs1_done"), sem("a_xs_done")
        gelu_done, ff_hi_done = sem("a_gelu_done"), sem("a_ff_hi_done")
        late_loaded, late_hi_done, late_lo_done, x_rest = (
            sem(f"a_{n}") for n in ("late_loaded", "late_hi_done", "late_lo_done", "x_rest"))
        block = stack.enter_context(nc.Block())

        @block.sync
        def _(sp):
            for i, n in enumerate(late):
                at_least(sp, late_lo_done, i)
                src = a[f"L0_attn_{n}"].rearrange("(k p) n -> p k n", p=P)
                sp.dma_start(late_stage.rearrange("p (k n) -> p k n", n=src.shape[2]), src).then_inc(late_loaded, 16)
                if i == 1:
                    sp.dma_start(x_sb[:, G4:B, :], a["x"][G4:B, :, :].rearrange("b t d -> t b d")).then_inc(x_rest, 16)

        @block.tensor
        def _(pe):
            def claim(u):
                at_least(pe, free_of(u), freed(u) - 1)
                return bank(u)

            def written(g, kind, n):
                for i in range(max(0, n - NPB), n):
                    u = use(g, kind, i)
                    pe.wait_ge(free_of(u), freed(u))

            def turn(g, ln):
                pe.wait_ge(rows_done[ln], g + 1)
                for k in range(KD):
                    ps = claim(use(g, f"T{ln + 1}", k))
                    for b in range(G4):
                        mm = pe.transpose(ps[:, b * T:(b + 1) * T], xh[:, b, k * P:(k + 1) * P], ident[0:T, 0:T])
                    mm.then_inc(pb_ready, 1)

            def from_h(g, ln, name, kind, m, width):
                ps = claim(use(g, kind, m))
                for k in range(KD):
                    mm = split_product(pe, ps[:, 0:GT], pair(name, k, m * P, P, width),
                                       (h_hi[:, ln, k, :], h_lo[:, ln, k, :]), k == 0, k == KD - 1)
                mm.then_inc(pb_ready, 1)

            def project_q(g, tiles):
                if tiles[0] == 0:
                    written(g, "T1", KD)
                for m in tiles:
                    from_h(g, 0, "wq", "Q", m, INNER)

            def project_k(g, tiles):
                for m in tiles:
                    from_h(g, 0, "wk", "K", m, INNER)

            def project_v(g, pieces):
                for i in pieces:
                    b, n = divmod(i, 2)
                    ps = claim(use(g, "V", i))
                    for k in range(KD):
                        lhs = (h_hi[:, 0, k, b * T:(b + 1) * T], h_lo[:, 0, k, b * T:(b + 1) * T])
                        mm = split_product(pe, ps[0:T, :], lhs, pair("wv", k, n * 512, 512, INNER), k == 0, k == KD - 1)
                    mm.then_inc(pb_ready, 1)

            def scores(g, u):
                b, quad = divmod(u, 4)
                at_least(pe, s_masked, UNITS * g + u - 1)
                for i in range(4):
                    h = 4 * quad + i
                    mm = pe.matmul(s_ps[u % 2][0:T, i * T:(i + 1) * T], kz[:, h, b * T:(b + 1) * T],
                                   qt[:, h // 2, b * T:(b + 1) * T], start=True, stop=True)
                mm.then_inc(s_ready, 1)

            def values(g, u):
                b, quad = divmod(u, 4)
                pe.wait_ge(s_masked, UNITS * g + u + 1)
                at_least(pe, o_done, UNITS * g + u - 1)
                for i in range(4):
                    mm = pe.matmul(o_ps[u % 2][0:T, i * (DH + 1):(i + 1) * (DH + 1)], sm[0:T + 1, u % NSM, i * T:(i + 1) * T],
                                   v1[0:T + 1, b, 4 * quad + i, :], start=True, stop=True)
                mm.then_inc(av_done, 1)

            def turn_output(g, u):
                pe.wait_ge(o_done, UNITS * g + u + 1)
                ps = claim(use(g, "O", u // 2)) if u % 2 == 0 else bank(use(g, "O", u // 2))
                for m in range(2):
                    c = (2 * (u % 2) + m) * T
                    mm = pe.transpose(ps[:, c:c + T], o32[:, u % 4, m * P:(m + 1) * P], ident[0:T, 0:T])
                if u % 2 == 1:
                    mm.then_inc(pb_ready, 1)

            def rows_out(u, name, lhs):
                ps = claim(u)
                for k in range(KI):
                    mm = split_product(pe, ps[0:T, 0:D], lhs(k), pair(name, k, 0, D, D), k == 0, k == KI - 1)
                mm.then_inc(pb_ready, 1)

            def body(g):
                written(g, "K", KI)
                written(g, "V", 2 * G4)
                for t in range(STEPS):
                    if t < UNITS:
                        scores(g, t)
                    if VALUES_AT <= t < UNITS + VALUES_AT:
                        values(g, t - VALUES_AT)
                    if TURN_AT <= t < UNITS + TURN_AT:
                        turn_output(g, t - TURN_AT)
                    if t == T1_AT and not is_last(g):
                        turn(g + 1, 0)
                    if t == Q_AT and not is_last(g):
                        project_q(g + 1, range(EARLY))
                    if t >= W_AT and (t - W_AT) % 4 == 0:
                        b = (t - W_AT) // 4
                        if is_first(g):
                            pe.wait_ge(late_lo_done, 2)
                        for u in (use(g, "O", 2 * b), use(g, "O", 2 * b + 1)):
                            pe.wait_ge(free_of(u), freed(u))
                        rows_out(use(g, "W", b), "wo", lambda k: (o_hi[:, b % 2, k, :], o_lo[:, b % 2, k, :]))
                if not is_last(g):
                    project_q(g + 1, range(EARLY, KI))
                    project_k(g + 1, range(K_EARLY))
                turn(g, 1)
                if not is_last(g):
                    project_k(g + 1, range(K_EARLY, KI))
                    project_v(g + 1, range(V_EARLY))
                written(g, "T2", KD)
                if is_first(g):
                    pe.wait_ge(late_lo_done, len(late))
                for f in range(FT):
                    from_h(g, 1, "w1", "F", f, FF)
                if not is_last(g):
                    project_v(g + 1, range(V_EARLY, 2 * G4))
                written(g, "F", FT)
                for b in range(G4):
                    rows_out(use(g, "Y", b), "w2", lambda k: (ff_hi[:, k, b * T:(b + 1) * T], ff_lo[:, k, b * T:(b + 1) * T]))

            turn(0, 0)
            project_q(0, range(KI))
            project_k(0, range(KI))
            pe.wait_ge(late_lo_done, 1)
            project_v(0, range(2 * G4))
            pe.wait_ge(pads_done, 3)
            groups(pe, body)

        @block.scalar
        def _(act):
            def ln_out(g, ln, gain, shift):
                for k in range(KD):
                    u = use(g, f"T{ln + 1}", k)
                    act.wait_ge(pb_ready, ready(u))
                    if ln:
                        last = use(g - 1, "T2", k) if is_last(g) else use(g + 1, "T1", k)
                    elif isinstance(g, int):
                        last = use(0, "T1", k) if g == 1 else None
                    else:
                        last = use(g - 2, "T2", k)
                    if last:
                        act.wait_ge(free_of(last), freed(last))
                    ps = bank(u)[:, 0:GT]
                    act.activation(h32[:, k, :], ps, ACT.Identity, bias=shift[:, k:k + 1], scale=gain[:, k:k + 1])
                    act.activation(h_hi[:, ln, k, :], ps, ACT.Identity, bias=shift[:, k:k + 1],
                                   scale=gain[:, k:k + 1]).then_inc(h_hi_done[ln], 1)

            def phi(g, kind, start, end):
                first = 2 * KI * g + (KI if kind == "K" else 0)
                for i in range(start, end + 1):
                    if i < end:
                        act.wait_ge(pb_ready, ready(use(g, kind, i)))
                        at_least(act, exp_done, first + i - 1)
                        act.activation(neg_relu[:, i % 2, :], bank(use(g, kind, i))[:, 0:GT], ACT.Relu,
                                       scale=-1.0).then_inc(relu_done, 1)
                    if i > start:
                        j = i - 1
                        act.wait_ge(relu_done, first + j + 1)
                        if j >= 2 or kind == "K":
                            last = use(g, kind, j - 2) if j >= 2 else use(g, "Q", KI + j - 2)
                            act.wait_ge(free_of(last), freed(last))
                        act.activation(phi_exp[:, j % 2, :], neg_relu[:, j % 2, :], ACT.Exp, scale=-1.0).then_inc(exp_done, 1)

            def take_v(g, pieces):
                for i in pieces:
                    u = use(g, "V", i)
                    b, n = divmod(i, 2)
                    act.wait_ge(pb_ready, ready(u))
                    act.activation(v1[0:T, b, 8 * n:8 * n + 8, 0:DH], bank(u)[0:T, :].rearrange("p (h d) -> p h d", d=DH),
                                   ACT.Identity, scale=UNSCALE).then_inc(free_of(u), 1)

            def out_high(g, j):
                b, half = divmod(j, 2)
                u = use(g, "O", j)
                act.wait_ge(pb_ready, ready(u))
                if half == 0 and b >= 2:
                    act.wait_ge(pb_ready, ready(use(g, "W", b - 2)))
                act.activation(o_hi[:, b % 2, 4 * half:4 * half + 4, :], bank(u)[:, 0:4 * T].rearrange("p (m t) -> p m t", t=T),
                               ACT.Identity).then_inc(o_hi_done, 1)

            def split_high(i):
                act.wait_ge(late_loaded, 16 * (i + 1))
                act.activation(hi[late[i]][:, :], late_stage, ACT.Identity, scale=WSCALE).then_inc(late_hi_done, 1)

            def body(g):
                for t in range(STEPS):
                    if TURN_AT <= t < UNITS + TURN_AT and (t - TURN_AT) % 2 == 1:
                        out_high(g, (t - TURN_AT) // 2)
                    if t == T1_AT + 1 and not is_last(g):
                        ln_out(g + 1, 0, g1, be1)
                    if t == SPLIT_AT and is_first(g):
                        split_high(3)
                if not is_last(g):
                    phi(g + 1, "Q", 0, KI)
                    phi(g + 1, "K", 0, K_EARLY)
                ln_out(g, 1, g2, be2)
                if not is_last(g):
                    phi(g + 1, "K", K_EARLY, KI)
                    take_v(g + 1, range(V_EARLY))
                    act.wait_ge(exp_done, 2 * KI * (g + 2))
                for f in range(FT):
                    act.wait_ge(pb_ready, ready(use(g, "F", f)))
                    at_least(act, ff_lo_count(g, f)[0], ff_lo_count(g, f)[1])
                    act.activation(gelu32[:, f % 2, :], bank(use(g, "F", f))[:, 0:GT], ACT.Gelu, bias=b1[:, f:f + 1],
                                   scale=UNSCALE).then_inc(gelu_done, 1)
                if not is_last(g):
                    take_v(g + 1, range(V_EARLY, 2 * G4))

            def ff_lo_count(g, f):
                u = use(g, "F", max(f - 2, 0))
                return free_of(u), freed(u) if f >= 2 else 0

            ln_out(0, 0, g1, be1)
            split_high(0)
            for i, kind in enumerate(("Q", "K")):
                phi(0, kind, 0, KI)
                split_high(i + 1)
            act.wait_ge(pads_done, 3)
            take_v(0, range(2 * G4))
            groups(act, body)

        @block.vector
        def _(dve):
            def ln_stats(ln, b, rows):
                return dve.bn_stats(stats[:, ln, b, :], rows(b))

            def ln_moments(g, ln):
                settle(dve, passed, (stats_done[ln], G4 * (g + 1)))
                for b in range(G4):
                    ins = dve.bn_aggr(mom[:, ln, b, :], stats[:, ln, b, :])
                ins.then_inc(mom_done[ln], 1)

            def ln_rows(g, ln, b, rows, dst):
                if b == 0:
                    dve.wait_ge(rstd_done[ln], g + 1)
                ins = dve.tensor_scalar(dst(b), rows(b), mom[:, ln, b, 0:1], rstd[:, ln, b:b + 1], ALU.subtract, ALU.mult)
                if b == G4 - 1:
                    ins.then_inc(rows_done[ln], 1)

            def ln_low(g, ln):
                for k in range(KD):
                    u = use(g, f"T{ln + 1}", k)
                    dve.wait_ge(h_hi_done[ln], KD * g + k + 1)
                    dve.tensor_tensor(h_lo[:, ln, k, :], h32[:, k, :], h_hi[:, ln, k, :], ALU.subtract).then_inc(free_of(u), 1)

            def phi(g, kind, i):
                u = use(g, kind, i)
                ps = bank(u)
                dve.wait_ge(exp_done, 2 * KI * g + (KI if kind == "K" else 0) + i + 1)
                if kind == "K":
                    for r in range(2):
                        rows = slice(DH * r, DH * (r + 1))
                        ins = dve.scalar_tensor_tensor(kz[rows, 2 * i + r, :], ps[rows, 0:GT], 0.0, phi_exp[rows, i % 2, :],
                                                       ALU.max, ALU.add)
                else:
                    ins = dve.scalar_tensor_tensor(qt[:, i, :], ps[:, 0:GT], 0.0, phi_exp[:, i % 2, :], ALU.max, ALU.add)
                ins.then_inc(free_of(u), 1)

            def mask(g, u):
                dve.wait_ge(s_ready, UNITS * g + u + 1)
                at_least(dve, av_done, UNITS * g + u + 1 - NSM)
                dve.tensor_tensor(sm[0:T, u % NSM, :].rearrange("p (i t) -> p i t", t=T),
                                  s_ps[u % 2][0:T, 0:4 * T].rearrange("p (i t) -> p i t", t=T),
                                  causal[:, :].unsqueeze(1).to_broadcast([T, 4, T]), ALU.mult).then_inc(s_masked, 1)

            def divide(g, u):
                ps = o_ps[u % 2][0:T, 0:4 * (DH + 1)].rearrange("p (i d) -> p i d", d=DH + 1)
                dve.wait_ge(av_done, UNITS * g + u + 1)
                at_least(dve, o_done, UNITS * g + u - 1)
                dve.reciprocal(rec[:, u % 2, :], ps[:, :, DH]).then_inc(rec_done, 1)
                dve.wait_ge(rec_done, UNITS * g + u + 1)
                if u >= 4:
                    dve.wait_ge(pb_ready, ready(use(g, "O", u // 2 - 2)))
                dve.tensor_tensor(o32[:, u % 4, :].rearrange("p (i d) -> p i d", d=DH), ps[:, :, 0:DH],
                                  rec[:, u % 2, :].unsqueeze(2).to_broadcast([T, 4, DH]), ALU.mult).then_inc(o_done, 1)

            def out_low(g, j):
                b, half = divmod(j, 2)
                u = use(g, "O", j)
                dve.wait_ge(o_hi_done, UNITS // 2 * g + j + 1)
                dve.tensor_tensor(o_lo[:, b % 2, 4 * half:4 * half + 4, :], bank(u)[:, 0:4 * T].rearrange("p (m t) -> p m t", t=T),
                                  o_hi[:, b % 2, 4 * half:4 * half + 4, :], ALU.subtract).then_inc(free_of(u), 1)

            def x_rows(g):
                return lambda b: x_sb[:, bass.ds(G4 * g + b, 1), :].rearrange("p a d -> p (a d)")

            x1_rows = lambda b: x1[:, b, :]
            xh_rows = lambda b: xh[:, b, :]
            sum_rows = lambda b: xsum[:, b, :]

            def split_low(i):
                dve.wait_ge(late_hi_done, i + 1)
                dve.scalar_tensor_tensor(lo[late[i]][:, :], late_stage, WSCALE, hi[late[i]][:, :], ALU.mult,
                                         ALU.subtract).then_inc(late_lo_done, 1)

            def body(g):
                for t in range(STEPS):
                    if 3 <= t < UNITS + 3:
                        divide(g, t - 3)
                    if t < UNITS:
                        mask(g, t)
                    if TURN_AT < t <= UNITS + TURN_AT and (t - TURN_AT) % 2 == 0:
                        out_low(g, (t - TURN_AT) // 2 - 1)
                    if not is_first(g):
                        if t < G4:
                            ln_stats(2, t, sum_rows).then_inc(stats_done[2], 1)
                        if t == 4:
                            ln_moments(g - 1, 2)
                        if 6 <= t < 10:
                            ln_rows(g - 1, 2, t - 6, sum_rows, x_rows(g - 1))
                    if not is_last(g):
                        if 4 <= t < 8:
                            ln_stats(0, t - 4, x_rows(g + 1)).then_inc(stats_done[0], 1)
                        if t == 8:
                            ln_moments(g + 1, 0)
                        if 10 <= t < 14:
                            ln_rows(g + 1, 0, t - 10, x_rows(g + 1), xh_rows)
                        if t == T1_AT + 2:
                            ln_low(g + 1, 0)
                        if t == SPLIT_AT and is_first(g):
                            split_low(3)
                        if t == Q_AT + 1:
                            for i in range(EARLY):
                                phi(g + 1, "Q", i)
                    if t >= W_AT + 1 and (t - W_AT - 1) % 4 == 0:
                        b = (t - W_AT - 1) // 4
                        u = use(g, "W", b)
                        dve.wait_ge(pb_ready, ready(u))
                        at_least(dve, xs1_done, g)
                        dve.scalar_tensor_tensor(x1[:, b, :], bank(u)[0:T, 0:D], UNSCALE, x_rows(g)(b),
                                                 ALU.mult, ALU.add).then_inc(free_of(u), 1)
                    if t >= W_AT + 2 and (t - W_AT - 2) % 4 == 0:
                        b = (t - W_AT - 2) // 4
                        u = use(g, "W", b)
                        dve.wait_ge(free_of(u), freed(u))
                        ln_stats(1, b, x1_rows).then_inc(stats_done[1], 1)
                ln_moments(g, 1)
                if not is_last(g):
                    for i in range(EARLY, EARLY + 2):
                        phi(g + 1, "Q", i)
                for b in range(G4):
                    ln_rows(g, 1, b, x1_rows, xh_rows)
                if not is_last(g):
                    for i in range(EARLY + 2, KI):
                        phi(g + 1, "Q", i)
                    for i in range(K_EARLY):
                        phi(g + 1, "K", i)
                ln_low(g, 1)
                if not is_last(g):
                    for i in range(K_EARLY, KI):
                        phi(g + 1, "K", i)
                if is_first(g):
                    dve.wait_ge(late_lo_done, len(late))
                for f in range(FT):
                    u = use(g, "F", f)
                    dve.wait_ge(gelu_done, FT * g + f + 1)
                    dve.tensor_copy(ff_hi[:, f, :], gelu32[:, f % 2, :]).then_inc(ff_hi_done, 1)
                    dve.wait_ge(ff_hi_done, FT * g + f + 1)
                    dve.tensor_tensor(ff_lo[:, f, :], gelu32[:, f % 2, :], ff_hi[:, f, :], ALU.subtract).then_inc(free_of(u), 1)
                dve.wait_ge(xs_done, g + 1)
                for b in range(G4):
                    u = use(g, "Y", b)
                    dve.wait_ge(pb_ready, ready(u))
                    dve.scalar_tensor_tensor(xsum[:, b, :], bank(u)[0:T, 0:D], UNSCALE, xsum[:, b, :],
                                             ALU.mult, ALU.add).then_inc(free_of(u), 1)
                for b in range(G4):
                    u = use(g, "Y", b)
                    dve.wait_ge(free_of(u), freed(u))

            for b in range(G4):
                ln_stats(0, b, x_rows(0)).then_inc(stats_done[0], 1)
            ln_moments(0, 0)
            for b in range(G4):
                ln_rows(0, 0, b, x_rows(0), xh_rows)
            ln_low(0, 0)
            dve.wait_ge(kz_zeroed, 1)
            split_low(0)
            for n, kind in enumerate(("Q", "K")):
                for i in range(KI):
                    phi(0, kind, i)
                split_low(n + 1)
            dve.wait_ge(x_rest, 16)
            dve.wait_ge(pads_done, 3)
            groups(dve, body)
            for b in range(G4):
                ln_stats(2, b, sum_rows).then_inc(stats_done[2], 1)
            ln_moments(NG - 1, 2)
            for b in range(G4):
                ln_rows(NG - 1, 2, b, sum_rows, x_rows(NG - 1))

        @block.gpsimd
        def _(pool):
            def ln_rstd(g, ln):
                settle(pool, passed, (mom_done[ln], g + 1))
                pool.tensor_scalar(rstd[:, ln, :], mom[:, ln, :, 1], EPS, None, ALU.add).then_inc(eps_done[ln], 1)
                pool.wait_ge(eps_done[ln], g + 1)
                pool.tensor_tensor(rstd[:, ln, :], rstd[:, ln, :], half_neg[0:T, :], ALU.pow).then_inc(rstd_done[ln], 1)

            def body(g):
                for t in range(STEPS):
                    if t == 5 and not is_first(g):
                        ln_rstd(g - 1, 2)
                    if t == 9 and not is_last(g):
                        ln_rstd(g + 1, 0)
                ln_rstd(g, 1)
                at_least(pool, rows_done[2], g)
                pool.tensor_tensor(xsum[:, :, :], x1[:, :, :], x_sb[:, bass.ds(G4 * g, G4), :], ALU.add).then_inc(xs1_done, 1)
                pool.wait_ge(xs1_done, g + 1)
                pool.tensor_tensor(xsum[:, :, :], xsum[:, :, :], b2[:, :].unsqueeze(1).to_broadcast([T, G4, D]),
                                   ALU.add).then_inc(xs_done, 1)

            ln_rstd(0, 0)
            pool.memset(kz[:, :, :], 0.0).then_inc(kz_zeroed, 1)
            pool.memset(v1[:, :, :, 0:DH], 0.0).then_inc(pads_done, 1)
            pool.memset(v1[:, :, :, DH], 1.0).then_inc(pads_done, 1)
            pool.memset(sm[:, :, :], 1e-6).then_inc(pads_done, 1)
            groups(pool, body)
            ln_rstd(NG - 1, 2)


def load_layer1(nc, a, x_sb, ident, half_neg, consts_done, causal, hi, lo, vectors, sb_in, psum_in, sem):
    stack = ExitStack()
    with stack:
        sb, psum = sb_in(stack), psum_in(stack)
        g1, be1, g2, be2, b1, b2 = vectors
        raw = [sb(f"a_raw{i}", [P, KD, INNER], F32) for i in range(2)]
        turned = sb("a_turned", [P, 2 * KI // 2, 4, P], F32)
        proj2 = sb("a_proj2", [P, P], F32)
        turn_ps = [psum(f"a_turn{i}", [P, 4 * P]) for i in range(4)]
        fold_ps = [psum(f"a_fold{i}", [P, 4 * P]) for i in range(4)]
        raw_loaded, vec_loaded, x_loaded = sem("a_raw_loaded"), sem("a_vec_loaded"), sem("a_x_loaded")
        p2_zero, p2_loaded = sem("a_p2_zero"), sem("a_p2_loaded")
        turn_ready, turn_done, fold_ready, fold_hi, fold_lo = (
            sem(f"a_{n}") for n in ("turn_ready", "turn_done", "fold_ready", "fold_hi", "fold_lo"))
        rows = lambda w: w.rearrange("(k p) n -> p k n", p=P)
        NT = 2 * KI * KD // 4
        block = stack.enter_context(nc.Block())

        @block.sync
        def _(sp):
            for i, n in enumerate(("L0_attn_wq", "L0_attn_wk")):
                sp.dma_start(raw[i][:, :, :], rows(a[n])).then_inc(raw_loaded, 16)
            sp.wait_ge(p2_zero, 1)
            for r in range(2):
                sp.dma_start(proj2[DH * r:DH * (r + 1), DH * r:DH * (r + 1)], a["L0_attn_proj"]).then_inc(p2_loaded, 16)
            sp.dma_start(x_sb[:, 0:G4, :], a["x"][0:G4, :, :].rearrange("b t d -> t b d")).then_inc(x_loaded, 16)
            for t, n in ((g1, "g1"), (be1, "beta1"), (g2, "g2"), (be2, "beta2"), (b1, "b1")):
                sp.dma_start(t[:, :], a[f"L0_attn_{n}"].rearrange("(k p) -> p k", p=P),
                             allow_slow_non_contiguous=True).then_inc(vec_loaded, 16)
            sp.dma_start(b2[:, :], a["L0_attn_b2"].partition_broadcast(T)).then_inc(vec_loaded, 16)
            sp.wait_ge(vec_loaded, 6 * 16)
            sp.wait_ge(x_loaded, 16)

        @block.gpsimd
        def _(pool):
            pool.memset(proj2[:, :], 0.0).then_inc(p2_zero, 1)
            pool.memset(ident[:, :], 1.0).then_inc(consts_done, 1)
            pool.memset(causal[:, :], 1.0).then_inc(consts_done, 1)
            pool.memset(half_neg[:, :], -0.5).then_inc(consts_done, 1)
            pool.wait_ge(consts_done, 3)
            pool.affine_select(out=ident[:, :], in_=ident[:, :], compare_op=ALU.is_equal, fill=0.0, base=0,
                               pattern=[[-1, P]], channel_multiplier=1).then_inc(consts_done, 1)
            pool.affine_select(out=causal[:, :], in_=causal[:, :], compare_op=ALU.is_ge, fill=0.0, base=0,
                               pattern=[[1, T]], channel_multiplier=-1).then_inc(consts_done, 1)

        @block.tensor
        def _(pe):
            pe.wait_ge(consts_done, 5)
            pe.wait_ge(raw_loaded, 32)
            for n in range(NT):
                w, m2 = divmod(n, KI // 2)
                at_least(pe, turn_done, n - 3)
                for i in range(4):
                    m, k = 2 * m2 + i // 2, i % 2
                    mm = pe.transpose(turn_ps[n % 4][:, i * P:(i + 1) * P], raw[w][:, k, m * P:(m + 1) * P], ident[:, :])
                mm.then_inc(turn_ready, 1)
            pe.wait_ge(p2_loaded, 32)
            for n in range(NT):
                pe.wait_ge(turn_done, n + 1)
                at_least(pe, fold_lo, n - 3)
                for i in range(4):
                    mm = pe.matmul(fold_ps[n % 4][:, i * P:(i + 1) * P], turned[:, n, i, :], proj2[:, :], start=True, stop=True)
                mm.then_inc(fold_ready, 1)

        def folded(t, n):
            w, m2 = divmod(n, KI // 2)
            return t[("wq", "wk")[w]][:, :].rearrange("p (k m c) -> p m k c", k=KD, c=P)[:, 2 * m2:2 * m2 + 2, :, :]

        def fold_bank(n):
            return fold_ps[n % 4][:, :].rearrange("p (m k c) -> p m k c", m=2, k=KD)

        @block.scalar
        def _(act):
            for n in range(NT):
                act.wait_ge(turn_ready, n + 1)
                act.activation(turned[:, n, :, :], turn_ps[n % 4][:, :].rearrange("p (i c) -> p i c", c=P),
                               ACT.Identity).then_inc(turn_done, 1)
            for n in range(NT):
                act.wait_ge(fold_ready, n + 1)
                act.activation(folded(hi, n), fold_bank(n), ACT.Identity).then_inc(fold_hi, 1)
        @block.vector
        def _(dve):
            for n in range(NT):
                dve.wait_ge(fold_hi, n + 1)
                dve.tensor_tensor(folded(lo, n), fold_bank(n), folded(hi, n), ALU.subtract).then_inc(fold_lo, 1)


def layer2(nc, a, x_sb, ident, half_neg, passed, sb_in, psum_in, sem):
    stack = ExitStack()
    with stack:
        sb, psum = sb_in(stack), psum_in(stack)
        names = ["q", "k", "v", "o"]
        hi = {n: sb(f"b_w{n}_hi", [P, WCOLS], F16) for n in names}
        lo = {n: sb(f"b_w{n}_lo", [P, WCOLS], F16) for n in names}
        gx, bx, gc, bc = (sb(f"b_{n}", [P, KD], F32) for n in ("gx", "bx", "gc", "bc"))
        NST = 3
        stage = [sb(f"b_stage{i}", [P, WCOLS], F32) for i in range(NST)]
        by_rows = lambda w: w.rearrange("(k p) n -> p k n", p=P)
        wkv = a["L0_xattn_Wkv"]
        weights = {"v": by_rows(wkv[:, INNER:2 * INNER]), "k": by_rows(wkv[:, 0:INNER]),
                   "q": by_rows(a["L0_xattn_Wq"]), "o": by_rows(a["L0_xattn_Wo"])}

        def pair(name, k, c0, n, width):
            c = k * width + c0
            return hi[name][:, c:c + n], lo[name][:, c:c + n]

        SP2 = S2 + 1
        NT4 = JT + 1
        ctx = sb("ctx", [JP, 2, JT, D], F32)
        mask8 = sb("mask8", [T, 2, S2], U8)
        mask_bias = sb("mask_bias", [T, 2, S2], F32)
        stats = sb("b_stats", [P, NT4, 6], F32)
        mom = sb("b_mom", [P, NT4, 2], F32)
        rstd = sb("b_rstd", [P, NT4], F32)
        shift = sb("b_shift", [P, NT4], F32)
        xc = sb("xc", [JP, JT, D], F32)
        xn = sb("xn", [T, D], F32)
        cn32 = sb("cn32", [P, KD, S2], F32)
        cn_hi, cn_lo = (sb(f"cn_{n}", [P, 2, KD, SP2], F16) for n in ("hi", "lo"))
        xt32 = sb("xt32", [P, KD, T], F32)
        xt_hi, xt_lo = (sb(f"xt_{n}", [P, 2, KD, T], F16) for n in ("hi", "lo"))
        k2 = sb("k2", [P, 2, H, SP2], F16)
        v2_hi, v2_lo = (sb(f"v2_{n}", [JP, 2, JT, INNER], F16) for n in ("hi", "lo"))
        q2_hi = sb("q2_hi", [P, 2, H, T], F16)
        qz_lo = sb("qz_lo", [P, 2, H, T], F16)
        s_neg = sb("s_neg", [T, 2, S2], F32)
        neg_max = sb("neg_max", [T, 4], F32)
        p32 = sb("p32", [T, 4, S2], F32)
        p_sum = sb("p_sum", [T, 4], F32)
        p_rec = sb("p_rec", [T, 4], F32)
        p_norm = sb("p_norm", [T, 4, S2], F32)
        pt_hi, pt_lo = (sb(f"pt_{n}", [JP, 4, JT * T], F16) for n in ("hi", "lo"))
        o_hi, o_lo = (sb(f"b_o_{n}", [P, KI, T], F16) for n in ("hi", "lo"))
        z = sb("b_z", [T, D], F32)
        z_stats, z_mom, z_rstd = sb("z_stats", [T, 6], F32), sb("z_mom", [T, 2], F32), sb("z_rstd", [T, 1], F32)

        NPB = 3
        pb = [psum(f"b_pb{i}", [P, 512]) for i in range(NPB)]
        s_ps = [psum(f"b_s{i}", [P, 512]) for i in range(2)]
        t_ps = [psum(f"b_t{i}", [P, 512]) for i in range(2)]
        o_ps = psum("b_o", [P, 512])

        PIECES = [(kind, int(n)) for kind, n in ("v0", "k0", "k1", "q0", "v1", "k2", "q1", "v2",
                                                 "v3", "k3", "k4", "v4", "k5", "k6", "v5", "k7")]
        NCH = len(PIECES)
        half_rows = (slice(0, DH), slice(DH, P))
        AHEAD = 4
        LAG = 1
        STATS_AT = (0, 1, 2, 4)
        X_AT, C_AT = (13, 14), (9, 11)
        SPLIT_O_AT = 12
        W_AT = 3
        PREP_AT = 6

        def turns(n):
            return [(kind, n, k) for kind in ("X", "C") for k in range(KD)]

        PRE = (turns(0) + [("P", 0, s) for s in range(PREP_AT)] + turns(1) + [("P", 0, s) for s in range(PREP_AT, NCH)])

        def body_uses(b):
            uses = []
            for s in range(H):
                if not is_last(b):
                    uses.append(("P", s))
                if s == W_AT and not is_first(b):
                    uses.append(("W", 0))
                if has_prep(b):
                    uses += [(kind, at.index(s)) for kind, at in (("X", X_AT), ("C", C_AT)) if s in at]
            if is_last(b):
                uses.append(("W", 1))
            return uses

        def is_first(b):
            return isinstance(b, int) and b == 0

        def is_last(b):
            return isinstance(b, int) and b == B - 1

        def has_prep(b):
            return not isinstance(b, int) or b + 2 < B

        PER = len(body_uses(None))
        assert PER % NPB == 0

        def use_in(b, item):
            less = 0 if is_first(b) else PER - len(body_uses(0))
            if is_last(b):
                less += PER - len(body_uses(B - 2))
            return b, len(PRE) - less + body_uses(b).index(item)

        def use_piece(n, s):
            return (0, PRE.index(("P", 0, s))) if is_first(n) else use_in(n - 1, ("P", s))

        def use_turn(n, kind, k):
            return (0, PRE.index((kind, n, k))) if isinstance(n, int) and n < 2 else use_in(n - 2, (kind, k))

        def use_out(b):
            return use_in(b, ("W", 1)) if is_last(b) else use_in(b + 1, ("W", 0))

        def ready(use):
            return use[0] * PER + use[1] + 1

        def freed(use):
            return use[0] * (PER // NPB) + use[1] // NPB + 1

        def bank(use):
            return pb[use[1] % NPB]

        def free_of(use):
            return pb_free[use[1] % NPB]

        w_loaded = [sem(f"b_w_loaded{i}") for i in range(NST)]
        w_hi_done, w_lo_done, vec_loaded = sem("b_w_hi_done"), sem("b_w_lo_done"), sem("b_vec_loaded")
        ctx_loaded = [sem(f"b_ctx_loaded{i}") for i in range(2)]
        mask_loaded = [sem(f"b_mask_loaded{i}") for i in range(2)]
        mask_m1, mask_done = sem("b_mask_m1"), sem("b_mask_done")
        zeroed, stats_zeroed = sem("b_zeroed"), sem("b_stats_zeroed")
        pb_ready = sem("b_pb_ready")
        pb_free = [sem(f"b_pb_free{i}") for i in range(NPB)]
        piece_hi = sem("b_piece_hi")
        stats_done, mom_done, eps_done, rstd_done, shift_neg, shift_done = (
            sem(f"b_{n}") for n in ("stats_done", "mom_done", "eps_done", "rstd_done", "shift_neg", "shift_done"))
        xc_done, xn_done, xt_hi_done, xt_done = (
            sem(f"b_{n}") for n in ("xc_done", "xn_done", "xt_hi_done", "xt_done"))
        cn_hi_done, cn_done = sem("b_cn_hi_done"), sem("b_cn_done")
        s_ready, s_masked, p_exp, p_sum_rec, p_norm_done = (
            sem(f"b_{n}") for n in ("s_ready", "s_masked", "p_exp", "p_sum_rec", "p_norm_done"))
        t_ready, pt_hi_done, pt_lo_done, av_done, o_hi_done, o_lo_done = (
            sem(f"b_{n}") for n in ("t_ready", "pt_hi_done", "pt_lo_done", "av_done", "o_hi_done", "o_lo_done"))
        z_stats_done, z_mom_done, z_eps, z_rstd_done, x_done = (
            sem(f"b_{n}") for n in ("z_stats_done", "z_mom_done", "z_eps", "z_rstd_done", "x_done"))

        def x_row(b):
            return x_sb[:, bass.ds(b, 1), :].rearrange("p a d -> p (a d)")

        def batches(eng, body):
            body(0, 0)
            body(1, 1)
            with eng.Fori(1, B // 2 - 1) as i:
                for par in range(2):
                    body(2 * i + par, par)
            body(B - 2, 0)
            body(B - 1, 1)

        block = stack.enter_context(nc.Block())

        @block.sync
        def _(sp):
            def load(n, par):
                settle(sp, passed, (xc_done, n - 1))
                sp.dma_start(ctx[:, par, :, :], a["ctx_1024"][bass.ds(n, 1), :, :].rearrange(
                    "a (p t) d -> p (a t) d", t=JT)).then_inc(ctx_loaded[par], 16)
                settle(sp, passed, (mask_done, n - 1))
                sp.dma_start(mask8[:, par, :], a["mask_BxS2_bf1"][bass.ds(n, 1), :].rearrange(
                    "a s -> (a s)").partition_broadcast(T)).then_inc(mask_loaded[par], 16)

            load(0, 0)
            for t, n in ((gx, "norm_w"), (bx, "norm_b"), (gc, "ctx_norm_w"), (bc, "ctx_norm_b")):
                sp.dma_start(t[:, :], a[f"L0_xattn_{n}"].rearrange("(k p) -> p k", p=P),
                             allow_slow_non_contiguous=True).then_inc(vec_loaded, 16)
            for i, src in enumerate(weights.values()):
                at_least(sp, w_lo_done, i - NST + 1)
                sp.dma_start(stage[i % NST][:, :].rearrange("p (k n) -> p k n", n=src.shape[2]), src).then_inc(w_loaded[i % NST], 16)
                if i == 0:
                    load(1, 1)
            with sp.Fori(1, B // 2) as i:
                for par in range(2):
                    load(2 * i + par, par)

        @block.tensor
        def _(pe):
            def claim(use):
                at_least(pe, pb_free[use[1] % NPB], freed(use) - 1)
                return bank(use)

            def turn_x(n, k):
                pe.wait_ge(xn_done, n + 1)
                ps = claim(use_turn(n, "X", k))
                pe.transpose(ps[:, 0:T], xn[:, k * P:(k + 1) * P], ident[0:T, 0:T]).then_inc(pb_ready, 1)

            def turn_ctx(n, k):
                pe.wait_ge(xc_done, n + 1)
                ps = claim(use_turn(n, "C", k))
                for t in range(JT):
                    mm = pe.transpose(ps[:, t * JP:(t + 1) * JP], xc[:, t, k * P:(k + 1) * P], ident[0:JP, 0:JP])
                mm.then_inc(pb_ready, 1)

            def piece(n, par, s):
                kind, j = PIECES[s]
                if s == PIECES.index(("q", 0)):
                    pe.wait_ge(xt_done, n + 1)
                if s == 0:
                    pe.wait_ge(cn_done, KD * (n + 1))
                ps = claim(use_piece(n, s))
                if kind == "q":
                    for i in range(4):
                        for k in range(KD):
                            mm = split_product(pe, ps[:, i * T:(i + 1) * T], pair("q", k, (4 * j + i) * P, P, INNER),
                                               (xt_hi[:, par, k, :], xt_lo[:, par, k, :]), k == 0, k == KD - 1)
                elif kind == "k":
                    for k in range(KD):
                        mm = split_product(pe, ps[:, 0:S2], pair("k", k, j * P, P, INNER),
                                           (cn_hi[:, par, k, 0:S2], cn_lo[:, par, k, 0:S2]), k == 0, k == KD - 1)
                else:
                    t, half = divmod(j, 2)
                    cols = slice(t * JP, (t + 1) * JP)
                    for k in range(KD):
                        mm = split_product(pe, ps[0:JP, :], (cn_hi[:, par, k, cols], cn_lo[:, par, k, cols]),
                                           pair("v", k, half * 512, 512, INNER), k == 0, k == KD - 1)
                mm.then_inc(pb_ready, 1)

            def written(n, *pieces):
                last = {}
                for s in sorted(PIECES.index(piece) for piece in pieces):
                    use = use_piece(n, s)
                    last[use[1] % NPB] = use
                for use in last.values():
                    pe.wait_ge(free_of(use), freed(use))

            def scores(b, par, h):
                written(b, ("q", h // 8), ("k", h // 2))
                at_least(pe, s_masked, H * b + h - 1)
                ps, keys = s_ps[h % 2][0:T, 0:S2], k2[:, par, h, 0:S2]
                pe.matmul(ps, q2_hi[:, par, h, :], keys, start=True, stop=False)
                pe.matmul(ps, qz_lo[:, par, h, :], keys, start=False, stop=True).then_inc(s_ready, 1)

            def turn_scores(b, h):
                pe.wait_ge(p_norm_done, H * b + h + 1)
                at_least(pe, pt_lo_done, H * b + h - 1)
                for t in range(JT):
                    mm = pe.transpose(t_ps[h % 2][0:JP, t * T:(t + 1) * T], p_norm[:, h % 4, t * JP:(t + 1) * JP], ident[0:T, 0:T])
                mm.then_inc(t_ready, 1)

            def values(b, par, h):
                if h == 0:
                    written(b, *(("v", j) for j in range(2 * JT)))
                pe.wait_ge(pt_lo_done, H * b + h + 1)
                if h % 8 == 0:
                    at_least(pe, o_lo_done, 2 * b + h // 8)
                r, c = DH * (h % 2), (h // 2 % 4) * T
                for t in range(JT):
                    cols = slice(h * DH, (h + 1) * DH)
                    mm = split_product(pe, o_ps[r:r + DH, c:c + T], (v2_hi[:, par, t, cols], v2_lo[:, par, t, cols]),
                                       (pt_hi[:, h % 4, t * T:(t + 1) * T], pt_lo[:, h % 4, t * T:(t + 1) * T]),
                                       t == 0, t == JT - 1)
                mm.then_inc(av_done, 1)

            def out_rows(b):
                pe.wait_ge(o_lo_done, 2 * b + 2)
                if is_first(b):
                    pe.wait_ge(w_lo_done, len(weights))
                ps = claim(use_out(b))
                for m in range(KI):
                    mm = split_product(pe, ps[0:T, 0:D], (o_hi[:, m, :], o_lo[:, m, :]), pair("o", m, 0, D, D),
                                       m == 0, m == KI - 1)
                mm.then_inc(pb_ready, 1)

            def body(b, par):
                for s in range(H):
                    turn_scores(b, s)
                    if not is_last(b):
                        piece(b + 1, 1 - par, s)
                    if s + AHEAD < H:
                        scores(b, par, s + AHEAD)
                    elif not is_last(b):
                        scores(b + 1, 1 - par, s + AHEAD - H)
                    if s >= LAG:
                        values(b, par, s - LAG)
                    elif not is_first(b):
                        values(b - 1, 1 - par, s - LAG + H)
                    if s == W_AT and not is_first(b):
                        out_rows(b - 1)
                    if has_prep(b):
                        if s in X_AT:
                            turn_x(b + 2, X_AT.index(s))
                        if s in C_AT:
                            turn_ctx(b + 2, C_AT.index(s))

            def turns_of(n):
                for k in range(KD):
                    turn_x(n, k)
                for k in range(KD):
                    turn_ctx(n, k)

            turns_of(0)
            for s in range(NCH):
                if s == PREP_AT:
                    turns_of(1)
                if PIECES[s][1] == 0:
                    pe.wait_ge(w_lo_done, list(weights).index(PIECES[s][0]) + 1)
                piece(0, 0, s)
            for h in range(AHEAD):
                scores(0, 0, h)
            batches(pe, body)
            for h in range(H - LAG, H):
                values(B - 1, 1, h)
            out_rows(B - 1)

        @block.scalar
        def _(act):
            def x_columns(n, k):
                use = use_turn(n, "X", k)
                act.wait_ge(pb_ready, ready(use))
                at_least(act, xt_done, n)
                act.activation(xt32[:, k, :], bank(use)[:, 0:T], ACT.Identity, bias=bx[:, k:k + 1],
                               scale=gx[:, k:k + 1]).then_inc(free_of(use), 1)

            def ctx_columns(n, k):
                use = use_turn(n, "C", k)
                act.wait_ge(pb_ready, ready(use))
                at_least(act, cn_done, KD * (n - 1) + k + 1)
                act.activation(cn32[:, k, :], bank(use)[:, 0:S2], ACT.Identity, bias=bc[:, k:k + 1],
                               scale=gc[:, k:k + 1]).then_inc(free_of(use), 1)

            def piece_high(n, par, s):
                use = use_piece(n, s)
                kind, j = PIECES[s]
                act.wait_ge(pb_ready, ready(use))
                ps = bank(use)
                if kind == "q":
                    for r in range(2):
                        for rows in half_rows:
                            ins = act.activation(q2_hi[rows, par, 8 * j + r:8 * j + 8:2, :],
                                                 ps[half_rows[r], 0:4 * T].rearrange("p (m t) -> p m t", t=T), ACT.Identity,
                                                 scale=UNSCALE * DH ** -0.5)
                elif kind == "k":
                    for r, rows in enumerate(half_rows):
                        ins = act.activation(k2[rows, par, 2 * j + r, 0:S2], ps[rows, 0:S2], ACT.Identity, scale=UNSCALE)
                else:
                    t, half = divmod(j, 2)
                    ins = act.activation(v2_hi[:, par, t, half * 512:(half + 1) * 512], ps[0:JP, :], ACT.Identity, scale=UNSCALE)
                ins.then_inc(piece_hi, 1)

            def softmax_exp(b, h):
                act.wait_ge(s_masked, H * b + h + 1)
                at_least(act, p_norm_done, H * b + h - 3)
                act.activation(p32[:, h % 4, :], s_neg[:, h % 2, :], ACT.Exp, bias=neg_max[:, h % 4:h % 4 + 1], scale=-1.0,
                               accum_out=p_sum[:, h % 4:h % 4 + 1]).then_inc(p_exp, 1)

            def turned_high(b, h):
                act.wait_ge(t_ready, H * b + h + 1)
                at_least(act, av_done, H * b + h - 3)
                act.activation(pt_hi[:, h % 4, :], t_ps[h % 2][0:JP, 0:JT * T], ACT.Identity).then_inc(pt_hi_done, 1)

            def out_high(b, half):
                act.wait_ge(av_done, H * b + 8 * half + 8)
                if half == 0 and not is_first(b):
                    act.wait_ge(pb_ready, ready(use_out(b - 1)))
                act.activation(o_hi[:, 4 * half:4 * half + 4, :], o_ps[:, 0:4 * T].rearrange("p (m t) -> p m t", t=T),
                               ACT.Identity).then_inc(o_hi_done, 1)

            def split_high(name):
                i = list(weights).index(name)
                act.wait_ge(w_loaded[i % NST], 16 * (i // NST + 1))
                act.activation(hi[name][:, :], stage[i % NST][:, :], ACT.Identity, scale=WSCALE).then_inc(w_hi_done, 1)

            def body(b, par):
                for s in range(H):
                    if s == LAG and not is_first(b):
                        out_high(b - 1, 1)
                    if s == LAG + 8:
                        out_high(b, 0)
                    if s + 2 < H:
                        softmax_exp(b, s + 2)
                    elif not is_last(b):
                        softmax_exp(b + 1, s + 2 - H)
                    turned_high(b, s)
                    if not is_last(b):
                        piece_high(b + 1, 1 - par, s)
                    if s == SPLIT_O_AT and is_first(b):
                        split_high("o")
                    if has_prep(b):
                        if s - 1 in X_AT:
                            x_columns(b + 2, X_AT.index(s - 1))
                        if s - 1 in C_AT:
                            ctx_columns(b + 2, C_AT.index(s - 1))

            act.wait_ge(vec_loaded, 4 * 16)
            def columns(n):
                for k in range(KD):
                    x_columns(n, k)
                for k in range(KD):
                    ctx_columns(n, k)

            split_high("v")
            columns(0)
            split_high("k")
            split_high("q")
            for s in range(NCH):
                if s == PREP_AT:
                    columns(1)
                piece_high(0, 0, s)
            for h in range(2):
                softmax_exp(0, h)
            batches(act, body)
            out_high(B - 1, 1)

        @block.vector
        def _(dve):
            def prep_stats(n, par, tiles):
                dve.wait_ge(ctx_loaded[par], 16 * (half_of(n) + 1))
                at_least(dve, mom_done, n)
                for t in tiles:
                    src = ctx[:, par, t, :] if t < JT else x_row(n)
                    ins = dve.bn_stats(stats[0:JP if t < JT else T, t, :], src)
                if JT in tiles:
                    ins.then_inc(stats_done, 1)

            def prep_moments(n):
                settle(dve, passed, (stats_done, n + 1), (shift_neg, n), (xn_done, n))
                for t in range(NT4):
                    ins = dve.bn_aggr(mom[0:JP if t < JT else T, t, :], stats[0:JP if t < JT else T, t, :])
                ins.then_inc(mom_done, 1)

            def prep_x(n):
                dve.wait_ge(rstd_done, n + 1)
                if not is_first(n):
                    dve.wait_ge(pb_ready, ready(use_turn(n - 1, "X", KD - 1)))
                dve.tensor_scalar(xn[:, :], x_row(n), mom[0:T, JT, 0:1], rstd[0:T, JT:JT + 1], ALU.subtract,
                                  ALU.mult).then_inc(xn_done, 1)

            def piece_low(n, par, s):
                use = use_piece(n, s)
                kind, j = PIECES[s]
                dve.wait_ge(piece_hi, NCH * n + s + 1)
                ps = bank(use)
                if kind == "q":
                    for r, rows in enumerate(half_rows):
                        heads = slice(8 * j + r, 8 * j + 8, 2)
                        ins = dve.scalar_tensor_tensor(qz_lo[rows, par, heads, :], ps[rows, 0:4 * T].rearrange("p (m t) -> p m t", t=T),
                                                       UNSCALE * DH ** -0.5, q2_hi[rows, par, heads, :], ALU.mult, ALU.subtract)
                elif kind == "k":
                    for r, rows in enumerate(half_rows):
                        h = 2 * j + r
                        ins = dve.scalar_tensor_tensor(k2[half_rows[1 - r], par, h, 0:S2], ps[rows, 0:S2], UNSCALE,
                                                       k2[rows, par, h, 0:S2], ALU.mult, ALU.subtract)
                else:
                    t, half = divmod(j, 2)
                    cols = slice(half * 512, (half + 1) * 512)
                    ins = dve.scalar_tensor_tensor(v2_lo[:, par, t, cols], ps[0:JP, :], UNSCALE, v2_hi[:, par, t, cols],
                                                   ALU.mult, ALU.subtract)
                ins.then_inc(pb_free[use[1] % NPB], 1)

            def mask_max(b, par, h):
                waits = [(s_ready, H * b + h + 1), (p_exp, H * b + h - 1)]
                if h == 0:
                    waits.append((mask_done, b + 1))
                settle(dve, passed, *waits)
                dve.tensor_tensor_reduce(s_neg[:, h % 2, :], s_ps[h % 2][0:T, 0:S2], mask_bias[:, par, :], -1.0, 3.4e38,
                                         ALU.add, ALU.min, neg_max[:, h % 4:h % 4 + 1]).then_inc(s_masked, 1)

            def sum_reciprocal(b, h):
                dve.wait_ge(p_exp, H * b + h + 1)
                dve.reciprocal(p_rec[:, h % 4:h % 4 + 1], p_sum[:, h % 4:h % 4 + 1]).then_inc(p_sum_rec, 1)

            def turned_low(b, h):
                dve.wait_ge(pt_hi_done, H * b + h + 1)
                dve.tensor_tensor(pt_lo[:, h % 4, :], t_ps[h % 2][0:JP, 0:JT * T], pt_hi[:, h % 4, :],
                                  ALU.subtract).then_inc(pt_lo_done, 1)

            def out_low(b, half):
                dve.wait_ge(o_hi_done, 2 * b + half + 1)
                dve.tensor_tensor(o_lo[:, 4 * half:4 * half + 4, :], o_ps[:, 0:4 * T].rearrange("p (m t) -> p m t", t=T),
                                  o_hi[:, 4 * half:4 * half + 4, :], ALU.subtract).then_inc(o_lo_done, 1)

            def residual(b):
                use = use_out(b)
                dve.wait_ge(pb_ready, ready(use))
                at_least(dve, x_done, b)
                dve.scalar_tensor_tensor(z[:, :], bank(use)[0:T, 0:D], UNSCALE, x_row(b), ALU.mult, ALU.add).then_inc(free_of(use), 1)
                dve.wait_ge(free_of(use), freed(use))
                dve.bn_stats(z_stats[:, :], z[:, :]).then_inc(z_stats_done, 1)

            def residual_moments(b):
                settle(dve, passed, (z_stats_done, b + 1))
                dve.bn_aggr(z_mom[:, :], z_stats[:, :]).then_inc(z_mom_done, 1)

            def norm_out(b):
                dve.wait_ge(z_rstd_done, b + 1)
                dve.tensor_scalar(x_row(b), z[:, :], z_mom[:, 0:1], z_rstd[:, :], ALU.subtract, ALU.mult).then_inc(x_done, 1)

            def split_low(name):
                i = list(weights).index(name)
                dve.wait_ge(w_hi_done, i + 1)
                dve.scalar_tensor_tensor(lo[name][:, :], stage[i % NST][:, :], WSCALE, hi[name][:, :], ALU.mult,
                                         ALU.subtract).then_inc(w_lo_done, 1)

            def body(b, par):
                for s in range(H):
                    if s == LAG and not is_first(b):
                        out_low(b - 1, 1)
                    if s == LAG + 8:
                        out_low(b, 0)
                    if s > 0 and not is_last(b):
                        piece_low(b + 1, 1 - par, s - 1)
                    elif s == 0 and not is_first(b):
                        piece_low(b, par, NCH - 1)
                    turned_low(b, s)
                    if s + 3 < H:
                        mask_max(b, par, s + 3)
                    elif not is_last(b):
                        mask_max(b + 1, 1 - par, s + 3 - H)
                    if s + 2 < H:
                        sum_reciprocal(b, s + 2)
                    elif not is_last(b):
                        sum_reciprocal(b + 1, s + 2 - H)
                    if not is_first(b):
                        if s == W_AT + 1:
                            residual(b - 1)
                        if s == W_AT + 2:
                            residual_moments(b - 1)
                        if s == 10:
                            norm_out(b - 1)
                    if has_prep(b):
                        if s in STATS_AT:
                            prep_stats(b + 2, par, (STATS_AT.index(s),))
                        if s == 5:
                            prep_moments(b + 2)
                        if s == 11:
                            prep_x(b + 2)
                    if s == SPLIT_O_AT and is_first(b):
                        split_low("o")

            def half_of(n):
                return n // 2 if isinstance(n, int) else halves[0]

            halves = [None]
            dve.wait_ge(stats_zeroed, 1)
            def prep(n):
                prep_stats(n, n, (0, 1, 2, JT))
                prep_moments(n)

            prep(0)
            prep_x(0)
            split_low("v")
            split_low("k")
            prep(1)
            split_low("q")
            prep_x(1)
            dve.wait_ge(zeroed, 1)
            for s in range(NCH):
                piece_low(0, 0, s)
            for h in range(3):
                mask_max(0, 0, h)
            for h in range(2):
                sum_reciprocal(0, h)
            body(0, 0)
            body(1, 1)
            with dve.Fori(1, B // 2 - 1) as i:
                halves[0] = i + 1
                for par in range(2):
                    body(2 * i + par, par)
            body(B - 2, 0)
            body(B - 1, 1)
            out_low(B - 1, 1)
            residual(B - 1)
            residual_moments(B - 1)
            norm_out(B - 1)

        @block.gpsimd
        def _(pool):
            def mask(n, par):
                settle(pool, passed, (mask_loaded[par], 16 * (half_of(n) + 1)),
                       (s_masked, H * (n - 1)))
                pool.tensor_scalar(mask_bias[:, par, :].rearrange("q (t p) -> q t p", t=JT),
                                   mask8[:, par, :].rearrange("q (p t) -> q t p", t=JT), -1.0, MASKED, ALU.add,
                                   ALU.mult).then_inc(mask_done, 1)

            def prep_rstd(n):
                settle(pool, passed, (mom_done, n + 1), (xc_done, n), (xn_done, n))
                pool.tensor_scalar(rstd[:, :], mom[:, :, 1], EPS, None, ALU.add).then_inc(eps_done, 1)
                pool.wait_ge(eps_done, n + 1)
                pool.tensor_tensor(rstd[:, :], rstd[:, :], half_neg[:, :], ALU.pow).then_inc(rstd_done, 1)
                pool.wait_ge(rstd_done, n + 1)
                pool.tensor_tensor(shift[:, :], mom[:, :, 0], rstd[:, :], ALU.mult).then_inc(shift_neg, 1)
                settle(pool, passed, (shift_neg, n + 1))
                pool.tensor_scalar(shift[:, :], shift[:, :], -1.0, None, ALU.mult).then_inc(shift_done, 1)

            def prep_rows(n, par):
                waits = [(shift_done, n + 1)]
                if not is_first(n):
                    waits.append((pb_ready, ready(use_turn(n - 1, "C", KD - 1))))
                settle(pool, passed, *waits)
                for t in range(JT):
                    ins = pool.tensor_scalar(xc[:, t, :], ctx[:, par, t, :], rstd[0:JP, t:t + 1], shift[0:JP, t:t + 1],
                                             ALU.mult, ALU.add)
                ins.then_inc(xc_done, 1)

            def split_x(n, par):
                last = use_turn(n, "X", KD - 1)
                settle(pool, passed, (free_of(last), freed(last)))
                pool.tensor_copy(xt_hi[:, par, :, :], xt32[:, :, :]).then_inc(xt_hi_done, 1)
                pool.wait_ge(xt_hi_done, n + 1)
                pool.tensor_tensor(xt_lo[:, par, :, :], xt32[:, :, :], xt_hi[:, par, :, :], ALU.subtract).then_inc(xt_done, 1)

            def split_ctx(n, par, k):
                use = use_turn(n, "C", k)
                settle(pool, passed, (pb_free[use[1] % NPB], freed(use)))
                pool.tensor_copy(cn_hi[:, par, k, 0:S2], cn32[:, k, :]).then_inc(cn_hi_done, 1)
                pool.wait_ge(cn_hi_done, KD * n + k + 1)
                pool.tensor_tensor(cn_lo[:, par, k, 0:S2], cn32[:, k, :], cn_hi[:, par, k, 0:S2], ALU.subtract).then_inc(cn_done, 1)

            def residual_rstd(b):
                settle(pool, passed, (z_mom_done, b + 1))
                pool.tensor_scalar(z_rstd[:, :], z_mom[:, 1:2], EPS, None, ALU.add).then_inc(z_eps, 1)
                pool.wait_ge(z_eps, b + 1)
                pool.tensor_tensor(z_rstd[:, :], z_rstd[:, :], half_neg[0:T, 0:1], ALU.pow).then_inc(z_rstd_done, 1)

            def normalise(b, h):
                settle(pool, passed, (p_sum_rec, H * b + h + 1), (t_ready, H * b + h - 3))
                pool.tensor_scalar(p_norm[:, h % 4, :], p32[:, h % 4, :], p_rec[:, h % 4:h % 4 + 1], 0.0, ALU.mult,
                                   ALU.add).then_inc(p_norm_done, 1)

            def body(b, par):
                for s in range(H):
                    if s + 2 < H:
                        normalise(b, s + 2)
                    elif not is_last(b):
                        normalise(b + 1, s + 2 - H)
                    if s == 0 and not is_last(b):
                        mask(b + 1, 1 - par)
                    if s == W_AT + 3 and not is_first(b):
                        residual_rstd(b - 1)
                    if has_prep(b):
                        if s == 5:
                            prep_rstd(b + 2)
                        if s == 6:
                            prep_rows(b + 2, par)
                        if s == 15:
                            split_x(b + 2, par)
                        if s - 2 in C_AT:
                            split_ctx(b + 2, par, C_AT.index(s - 2))

            def half_of(n):
                return n // 2 if isinstance(n, int) else halves[par_of[0]]

            halves, par_of = [None, None], [0]
            pool.memset(mom[:, :, :], 1.0).then_inc(stats_zeroed, 1)
            pool.memset(qz_lo[:, :, :, :], 0.0).then_inc(zeroed, 1)
            mask(0, 0)
            for n in range(2):
                prep_rstd(n)
                prep_rows(n, n)
                for k in range(KD):
                    split_ctx(n, n, k)
                split_x(n, n)
            for h in range(2):
                normalise(0, h)
            body(0, 0)
            body(1, 1)
            with pool.Fori(1, B // 2 - 1) as i:
                halves[0], halves[1] = i + 1, i
                for par in range(2):
                    par_of[0] = 1 - par
                    body(2 * i + par, par)
            body(B - 2, 0)
            body(B - 1, 1)
            residual_rstd(B - 1)


def layer3(nc, a, out, x_sb, ident, half_neg, passed, sb_in, psum_in, sem):
    stack = ExitStack()
    with stack:
        sb = sb_in(stack)
        wr = sb("wr", [P, KD, E], F32)
        br = sb("br", [T, E], F32)
        b1, b2 = sb("c_b1", [P, E, FF // P], F32), sb("c_b2", [P, E, KD], F32)
        rev = sb("rev", [T, E], F32)
        slot_id = sb("slot_id", [T, CAP], F32)
        earlier = sb("earlier", [T, T], F32)
        FAR = 1024.0
        probs = sb("probs", [T, B, E], F32)
        place = sb("place", [T, B, E], F32)
        gather = sb("gather", [T, B, SLOTS], F16)
        y_t = sb("y_t", [P, KD, E, ES], F32)
        x_split = y_t[:, :, :, :].rearrange("p k e n -> p (k e n)").bitcast(F16)
        x_hi, x_lo = (x_split[0:T, i * B * D:(i + 1) * B * D].rearrange("p (b d) -> p b d", d=D) for i in range(2))
        w1_loaded = [sem(f"c_w1_loaded{i}") for i in range(2)]
        w2_loaded = [sem(f"c_w2_loaded{i}") for i in range(2)]

        mid = ExitStack()
        with mid:
            sbm = sb_in(mid)
            w1_raw, w2_raw = sbm("w1_raw", [P, 2, WCOLS], F32), sbm("w2_raw", [P, 2, WCOLS], F32)
            buf_hi, buf_lo = (sbm(f"buf_{n}", [P, KD, E, ES], F16) for n in ("hi", "lo"))

            def load_expert(sp, e, par):
                sp.dma_start(w1_raw[:, par, :].rearrange("p (k n) -> p k n", k=KD),
                             a["L0_ffn_W1"][bass.ds(e, 1), :, :].rearrange("a (k p) n -> p (a k) n", p=P)).then_inc(w1_loaded[par], 16)
                sp.dma_start(w2_raw[:, par, :].rearrange("p (k n) -> p k n", n=D),
                             a["L0_ffn_W2"][bass.ds(e, 1), :, :].rearrange("a (k p) n -> p (a k) n", p=P)).then_inc(w2_loaded[par], 16)

            w1_hi, w1_lo, w2_hi, w2_lo = (sbm(f"e_{n}", [P, 2, WCOLS], F16) for n in ("w1_hi", "w1_lo", "w2_hi", "w2_lo"))
            w_hi_done, w_lo_done = sem("e_w_hi_done"), sem("e_w_lo_done")

            def weights_high(act, e, par, before, which):
                raw, loaded, hi = ((w1_raw, w1_loaded, w1_hi), (w2_raw, w2_loaded, w2_hi))[which]
                act.wait_ge(loaded[par], 16 * (before + 1))
                act.activation(hi[:, par, :], raw[:, par, :], ACT.Identity, scale=WSCALE).then_inc(w_hi_done, 1)

            def weights_low(dve, e, par, which):
                raw, hi, lo = ((w1_raw, w1_hi, w1_lo), (w2_raw, w2_hi, w2_lo))[which]
                dve.wait_ge(w_hi_done, 2 * e + which + 1)
                dve.scalar_tensor_tensor(lo[:, par, :], raw[:, par, :], WSCALE, hi[:, par, :], ALU.mult,
                                         ALU.subtract).then_inc(w_lo_done, 1)

            route(nc, a, x_sb, ident, passed, wr, br, b1, b2, rev, slot_id, earlier, FAR, probs, place, x_hi, x_lo, buf_hi, weights_high, weights_low,
                  load_expert, sb_in, psum_in, sem)
            dispatch(nc, x_hi, x_lo, slot_id, place, gather, buf_hi, buf_lo, sb_in, psum_in, sem)
            experts(nc, passed, (w1_hi, w1_lo, w2_hi, w2_lo), w_lo_done, weights_high, weights_low, load_expert, b1, b2,
                    buf_hi, buf_lo, y_t, sb_in, psum_in, sem)
        combine(nc, out, x_sb, ident, half_neg, passed, probs, gather, y_t, sb_in, psum_in, sem)


def route(nc, a, x_sb, ident, passed, wr, br, b1, b2, rev, slot_id, earlier, FAR, probs, place, x_hi, x_lo, buf_hi, weights_high, weights_low,
          load_expert, sb_in, psum_in, sem):
    stack = ExitStack()
    with stack:
        sb, psum = sb_in(stack), psum_in(stack)
        spare = buf_hi[:, :, :, :].rearrange("p k e n -> p (k e n)").bitcast(F32)
        xs = spare[0:T, 0:2 * G4 * D].rearrange("p (a b d) -> p a b d", a=2, b=G4)
        xt = spare[:, 2 * G4 * D:2 * (G4 * D + KD * GT)].rearrange("p (a k t) -> p a k t", a=2, k=KD)
        logits = sb("logits", [T, B, E], F32)
        work = {n: sb(f"r_{n}", [T, B, E], F32) for n in ("exp", "eq", "one", "two", "left")}
        top = {n: sb(f"r_{n}", [T, B], F32) for n in ("max", "sum", "rec", "max1", "id1", "max2", "id2")}
        turn_ps = [psum(f"r_turn{i}", [P, 512]) for i in range(2 * KD)]
        logit_ps = [psum(f"r_logit{i}", [P, 512]) for i in range(2)]
        count_ps = psum("r_count", [P, 512])
        router_loaded, vec_loaded, const_done, xs_done, turn_ready, xt_done, logit_ready, logit_done = (
            sem(f"r_{n}") for n in ("router_loaded", "vec_loaded", "const_done", "xs_done", "turn_ready", "xt_done", "logit_ready", "logit_done"))
        x_hi_done = sem("r_x_hi_done")
        step, exp_done, count_ready = sem("r_step"), sem("r_exp_done"), sem("r_count_ready")
        block = stack.enter_context(nc.Block())

        def groups(eng, body):
            body(0, 0)
            body(1, 1)
            with eng.Fori(1, NG // 2 - 1) as i:
                for par in range(2):
                    body(2 * i + par, par)
            body(NG - 2, 0)
            body(NG - 1, 1)

        def is_first(g):
            return isinstance(g, int) and g == 0

        def is_last(g):
            return isinstance(g, int) and g == NG - 1

        @block.sync
        def _(sp):
            sp.dma_start(wr[:, :, :], a["L0_ffn_Wr"].rearrange("(k p) e -> p k e", p=P)).then_inc(router_loaded, 16)
            sp.dma_start(br[:, :], a["L0_ffn_br"].partition_broadcast(T)).then_inc(router_loaded, 16)
            for e in range(2):
                load_expert(sp, e, e)
            for e in range(E):
                sp.dma_start(b1[:, e, :], a["L0_ffn_b1"][e, :].rearrange("(f p) -> p f", p=P),
                             allow_slow_non_contiguous=True).then_inc(vec_loaded, 16)
                sp.dma_start(b2[:, e, :], a["L0_ffn_b2"][e, :].rearrange("(f p) -> p f", p=P),
                             allow_slow_non_contiguous=True).then_inc(vec_loaded, 16)
            sp.wait_ge(vec_loaded, 16 * 2 * E)

        @block.gpsimd
        def _(pool):
            for e in range(E):
                ins = pool.memset(rev[:, e:e + 1], float(E - e))
            ins.then_inc(const_done, 1)
            for c in range(CAP):
                ins = pool.memset(slot_id[:, c:c + 1], c - FAR)
            ins.then_inc(const_done, 1)
            pool.memset(earlier[:, :], 1.0).then_inc(const_done, 1)
            pool.wait_ge(const_done, 3)
            pool.affine_select(out=earlier[:, :], in_=earlier[:, :], compare_op=ALU.is_gt, fill=0.0, base=0,
                               pattern=[[1, T]], channel_multiplier=-1).then_inc(const_done, 1)

        @block.tensor
        def _(pe):
            def logits_of(g, par):
                if is_first(g):
                    pe.wait_ge(router_loaded, 32)
                pe.wait_ge(xt_done, g + 1)
                at_least(pe, logit_done, g - 1)
                for b in range(G4):
                    for k in range(KD):
                        mm = pe.matmul(logit_ps[par][0:T, b * E:(b + 1) * E], xt[:, par, k, b * T:(b + 1) * T], wr[:, k, :],
                                       start=(k == 0), stop=(k == KD - 1))
                mm.then_inc(logit_ready, 1)

            def body(g, par):
                pe.wait_ge(xs_done, g + 1)
                at_least(pe, xt_done, g - 1)
                for k in range(KD):
                    for b in range(G4):
                        mm = pe.transpose(turn_ps[2 * par + k][:, b * T:(b + 1) * T], xs[:, par, b, k * P:(k + 1) * P], ident[0:T, 0:T])
                mm.then_inc(turn_ready, 1)
                if not is_first(g):
                    logits_of(g - 1, 1 - par)

            groups(pe, body)
            logits_of(NG - 1, 1)
            pe.wait_ge(step, 16)
            pe.wait_ge(const_done, 4)
            pe.matmul(count_ps[0:T, 0:B * E], earlier[:, :], work["left"][:, :, :].rearrange("p b e -> p (b e)"),
                      start=True, stop=True).then_inc(count_ready, 1)

        @block.scalar
        def _(act):
            def body(g, par):
                act.wait_ge(turn_ready, g + 1)
                at_least(act, logit_ready, g - 1)
                for k in range(KD):
                    ins = act.activation(xt[:, par, k, :], turn_ps[2 * par + k][:, 0:GT], ACT.Identity)
                ins.then_inc(xt_done, 1)
                act.activation(x_hi[:, bass.ds(G4 * g, G4), :], x_sb[:, bass.ds(G4 * g, G4), :], ACT.Identity).then_inc(x_hi_done, 1)
                if isinstance(g, int) and g == NG - 2:
                    weights_high(act, 0, 0, 0, 0)

            groups(act, body)
            act.wait_ge(step, 2)
            act.activation(work["exp"][:, :, :], logits[:, :, :], ACT.Exp).then_inc(exp_done, 1)
            weights_high(act, 0, 0, 0, 1)

        @block.vector
        def _(dve):
            def add_bias(g, par):
                if is_first(g):
                    dve.wait_ge(router_loaded, 32)
                dve.wait_ge(logit_ready, g + 1)
                dve.tensor_tensor(logits[:, bass.ds(G4 * g, G4), :], logit_ps[par][0:T, 0:G4 * E].rearrange("p (b e) -> p b e", e=E),
                                  br[:, :].unsqueeze(1).to_broadcast([T, G4, E]), ALU.add).then_inc(logit_done, 1)

            def split_low(g):
                at_g = bass.ds(G4 * g, G4)
                dve.wait_ge(x_hi_done, g + 1)
                dve.tensor_tensor(x_lo[:, at_g, :], x_sb[:, at_g, :], x_hi[:, at_g, :], ALU.subtract)

            def body(g, par):
                at_least(dve, turn_ready, g - 1)
                dve.tensor_copy(xs[:, par, :, :], x_sb[:, bass.ds(G4 * g, G4), :]).then_inc(xs_done, 1)
                if not (isinstance(g, int) and g < 2):
                    add_bias(g - 2, par)
                if not is_first(g):
                    split_low(g - 1)
                if is_last(g):
                    weights_low(dve, 0, 0, 0)
                    split_low(g)

            groups(dve, body)
            for par in range(2):
                add_bias(NG - 2 + par, par)
            dve.wait_ge(logit_done, NG)
            dve.wait_ge(const_done, 2)
            count = [0]

            def then(ins):
                count[0] += 1
                ins.then_inc(step, 1)
                dve.wait_ge(step, count[0])

            over = lambda t: t[:, :].unsqueeze(2).to_broadcast([T, B, E])
            revs = rev[:, :].unsqueeze(1).to_broadcast([T, B, E])
            w = {n: t[:, :, :] for n, t in work.items()}
            then(dve.tensor_reduce(top["max"][:, :], logits[:, :, :], AXX, ALU.max))
            then(dve.tensor_tensor(logits[:, :, :], logits[:, :, :], over(top["max"]), ALU.subtract))
            dve.wait_ge(exp_done, 1)
            then(dve.tensor_reduce(top["sum"][:, :], w["exp"], AXX, ALU.add))
            then(dve.reciprocal(top["rec"][:, :], top["sum"][:, :]))
            then(dve.tensor_tensor(probs[:, :, :], w["exp"], over(top["rec"]), ALU.mult))
            then(dve.tensor_reduce(top["max1"][:, :], probs[:, :, :], AXX, ALU.max))
            then(dve.tensor_tensor(w["eq"], probs[:, :, :], over(top["max1"]), ALU.is_equal))
            then(dve.tensor_tensor(w["eq"], w["eq"], revs, ALU.mult))
            then(dve.tensor_reduce(top["id1"][:, :], w["eq"], AXX, ALU.max))
            then(dve.tensor_tensor(w["one"], revs, over(top["id1"]), ALU.is_equal))
            then(dve.scalar_tensor_tensor(w["left"], w["one"], -4.0, probs[:, :, :], ALU.mult, ALU.add))
            then(dve.tensor_reduce(top["max2"][:, :], w["left"], AXX, ALU.max))
            then(dve.tensor_tensor(w["eq"], w["left"], over(top["max2"]), ALU.is_equal))
            then(dve.tensor_tensor(w["eq"], w["eq"], revs, ALU.mult))
            then(dve.tensor_reduce(top["id2"][:, :], w["eq"], AXX, ALU.max))
            dve.tensor_tensor(w["two"], revs, over(top["id2"]), ALU.is_equal).then_inc(exp_done, 1)
            dve.wait_ge(exp_done, 2)
            then(dve.tensor_tensor(w["left"], w["one"], w["two"], ALU.add))
            dve.wait_ge(count_ready, 1)
            dve.scalar_tensor_tensor(place[:, :, :].rearrange("p b e -> p (b e)"), w["left"].rearrange("p b e -> p (b e)"), -FAR,
                                     count_ps[0:T, 0:B * E], ALU.mult, ALU.add).then_inc(step, 1)


def dispatch(nc, x_hi, x_lo, slot_id, place, gather, buf_hi, buf_lo, sb_in, psum_in, sem):
    stack = ExitStack()
    with stack:
        sb, psum = sb_in(stack), psum_in(stack)
        hi_ps = [psum(f"d_hi{i}", [P, 512]) for i in range(G4)]
        lo_ps = [psum(f"d_lo{i}", [P, 512]) for i in range(G4)]
        gather_done, hi_ready, lo_ready, hi_done, lo_done = (
            sem(f"d_{n}") for n in ("gather_done", "hi_ready", "lo_ready", "hi_done", "lo_done"))
        block = stack.enter_context(nc.Block())

        def groups(eng, body):
            body(0, 0)
            body(1, 1)
            with eng.Fori(1, NG // 2) as i:
                for par in range(2):
                    body(2 * i + par, par)

        def is_first(g):
            return isinstance(g, int) and g == 0

        def slots_of(buf, b):
            return buf[:, :, :, bass.ds(b * CAP, CAP)]

        @block.scalar
        def _(act):
            def take(g):
                for b in range(G4):
                    act.wait_ge(hi_ready, G4 * g + b + 1)
                    act.activation(slots_of(buf_hi, G4 * g + b), hi_ps[b][:, 0:KD * SLOTS].rearrange("p (k e c) -> p k e c", k=KD, e=E),
                                   ACT.Identity).then_inc(hi_done, 1)

            groups(act, lambda g, par: take(g))

        @block.vector
        def _(dve):
            def take(g):
                for b in range(G4):
                    dve.wait_ge(lo_ready, G4 * g + b + 1)
                    dve.tensor_copy(slots_of(buf_lo, G4 * g + b),
                                    lo_ps[b][:, 0:KD * SLOTS].rearrange("p (k e c) -> p k e c", k=KD, e=E)).then_inc(lo_done, 1)

            def body(g, par):
                at_b = bass.ds(G4 * g, G4)
                dve.tensor_tensor(gather[:, at_b, :].rearrange("p b (e c) -> p (b e) c", c=CAP),
                                  place[:, at_b, :].rearrange("p b e -> p (b e)").unsqueeze(2).to_broadcast([T, G4 * E, CAP]),
                                  slot_id[:, :].unsqueeze(1).to_broadcast([T, G4 * E, CAP]), ALU.is_equal).then_inc(gather_done, 1)
                if not is_first(g):
                    take(g - 1)

            groups(dve, body)
            take(NG - 1)

        @block.tensor
        def _(pe):
            def body(g, par):
                pe.wait_ge(gather_done, g + 1)
                for b in range(G4):
                    if b % 2 == 0:
                        at_least(pe, hi_done, G4 * (g - 1) + b + 2)
                        at_least(pe, lo_done, G4 * (g - 1) + b + 2)
                    for src, ps, done in ((x_hi, hi_ps, hi_ready), (x_lo, lo_ps, lo_ready)):
                        for k in range(KD):
                            mm = pe.matmul(ps[b][:, k * SLOTS:(k + 1) * SLOTS], src[:, bass.ds(G4 * g + b, 1), k * P:(k + 1) * P].rearrange("p a d -> p (a d)"),
                                           gather[:, bass.ds(G4 * g + b, 1), :].rearrange("p a s -> p (a s)"), start=True, stop=True)
                        mm.then_inc(done, 1)

            groups(pe, body)


def experts(nc, passed, split_weights, w_lo_done, weights_high, weights_low, load_expert, b1, b2, buf_hi, buf_lo, y_t, sb_in, psum_in, sem):
    stack = ExitStack()
    with stack:
        sb, psum = sb_in(stack), psum_in(stack)
        FT, HALF = FF // P, ES // 2
        w1_hi, w1_lo, w2_hi, w2_lo = split_weights
        h_hi, h_lo = (sb(f"e_h_{n}", [P, FT, ES], F16) for n in ("hi", "lo"))
        NR = 4
        r32 = sb("r32", [P, NR, ES], F32)
        NPB = 4
        pb = [psum(f"e_pb{i}", [P, 2, 512]) for i in range(NPB)]
        USES = FT + KD
        pb_ready = sem("e_pb_ready")
        pb_free = [sem(f"e_pb_free{i}") for i in range(NPB)]
        h_hi_done, h_lo_done = sem("e_h_hi_done"), sem("e_h_lo_done")
        block = stack.enter_context(nc.Block())

        def each(eng, body):
            for par in range(2):
                body(0, par)
            with eng.Fori(1, E // 2 - 1) as i:
                for par in range(2):
                    body(i, par)
            for par in range(2):
                body(E // 2 - 1, par)

        def is_last(i, par):
            return isinstance(i, int) and i == E // 2 - 1 and par == 1

        def ready(i, par, use):
            return 2 * USES * i + USES * par + use + 1

        def freed(i, par, use):
            return 2 * USES // NPB * i + (USES * par + use) // NPB + 1

        def bank(par, use):
            return (USES * par + use) % NPB

        def of_expert(t, k, e):
            return t[:, k, bass.ds(e, 1), :].rearrange("p a n -> p (a n)")

        @block.sync
        def _(sp):
            def load(i, par):
                settle(sp, passed, (w_lo_done, 2 * (2 * i + par - 2) + 2))
                load_expert(sp, 2 * i + par, par)

            for par in range(2):
                load(1, par)
            with sp.Fori(2, E // 2) as i:
                for par in range(2):
                    load(i, par)

        def next_expert(i, par):
            return (i, 1) if par == 0 else (i + 1, 0)

        @block.scalar
        def _(act):
            def split(i, par, which):
                if not (isinstance(i, int) and i == 0):
                    act.wait_ge(pb_ready, ready(i - 1, par, (FT, USES)[which] - 1))
                weights_high(act, 2 * i + par, par, i, which)

            def body(i, par):
                e = 2 * i + par
                for f in range(FT):
                    act.wait_ge(pb_ready, ready(i, par, f))
                    at_least(act, h_lo_done, FT * e + f + 1 - NR)
                    act.activation(r32[:, f % NR, :].rearrange("p (a n) -> p a n", a=2), pb[bank(par, f)][:, :, 0:HALF], ACT.Relu,
                                   bias=b1[:, bass.ds(e, 1), f], scale=UNSCALE).then_inc(pb_free[bank(par, f)], 1)
                if not is_last(i, par):
                    for which in range(2):
                        split(*next_expert(i, par), which)
                for c in range(KD):
                    use = FT + c
                    act.wait_ge(pb_ready, ready(i, par, use))
                    act.activation(of_expert(y_t, c, e).rearrange("p (a n) -> p a n", a=2), pb[bank(par, use)][:, :, 0:HALF],
                                   ACT.Identity, bias=b2[:, bass.ds(e, 1), c], scale=UNSCALE).then_inc(pb_free[bank(par, use)], 1)

            each(act, body)

        @block.vector
        def _(dve):
            def body(i, par):
                e = 2 * i + par
                if par == 1:
                    dve.wait_ge(pb_ready, ready(i, 0, USES - 1))
                elif not (isinstance(i, int) and i == 0):
                    dve.wait_ge(pb_ready, ready(i - 1, 1, USES - 1))
                for f in range(FT):
                    dve.wait_ge(pb_free[bank(par, f)], freed(i, par, f))
                    dve.tensor_copy(h_hi[:, f, :], r32[:, f % NR, :]).then_inc(h_hi_done, 1)
                    dve.wait_ge(h_hi_done, FT * e + f + 1)
                    dve.tensor_tensor(h_lo[:, f, :], r32[:, f % NR, :], h_hi[:, f, :], ALU.subtract).then_inc(h_lo_done, 1)
                if not is_last(i, par):
                    for which in range(2):
                        weights_low(dve, e + 1, 1 - par, which)

            weights_low(dve, 0, 0, 1)
            each(dve, body)

        @block.tensor
        def _(pe):
            def claim(i, par, use):
                at_least(pe, pb_free[bank(par, use)], freed(i, par, use) - 1)
                return pb[bank(par, use)]

            def body(i, par):
                e = 2 * i + par
                pe.wait_ge(w_lo_done, 2 * e + 1)
                for f in range(FT):
                    ps = claim(i, par, f)
                    for n in range(2):
                        cols = slice(n * HALF, (n + 1) * HALF)
                        for k in range(KD):
                            c0 = k * FF + f * P
                            mm = split_product(pe, ps[:, n, 0:HALF], (w1_hi[:, par, c0:c0 + P], w1_lo[:, par, c0:c0 + P]),
                                               (of_expert(buf_hi, k, e)[:, cols], of_expert(buf_lo, k, e)[:, cols]),
                                               k == 0, k == KD - 1)
                    mm.then_inc(pb_ready, 1)
                pe.wait_ge(w_lo_done, 2 * e + 2)
                for c in range(KD):
                    ps = claim(i, par, FT + c)
                    for n in range(2):
                        cols = slice(n * HALF, (n + 1) * HALF)
                        for f in range(FT):
                            if c == 0 and n == 0:
                                pe.wait_ge(h_lo_done, FT * e + f + 1)
                            c0 = f * D + c * P
                            mm = split_product(pe, ps[:, n, 0:HALF], (w2_hi[:, par, c0:c0 + P], w2_lo[:, par, c0:c0 + P]),
                                               (h_hi[:, f, cols], h_lo[:, f, cols]), f == 0, f == FT - 1)
                    mm.then_inc(pb_ready, 1)

            each(pe, body)


def combine(nc, out, x_sb, ident, half_neg, passed, probs, gather, y_t, sb_in, psum_in, sem):
    stack = ExitStack()
    with stack:
        sb, psum = sb_in(stack), psum_in(stack)
        HS = SLOTS // 2
        SUM_LAG = 2
        yb = sb("yb", [P, G4, KD, SLOTS], F32)
        gw = sb("gw", [T, 2, SLOTS], F32)
        gw_t = sb("gw_t", [HS, 2, 2 * T], F32)
        y_n = sb("y_n", [HS, 2, 2 * D], F32)
        z = sb("c_z", [T, 2, G4, D], F32)
        stats, mom, rstd = sb("c_stats", [T, G4, 6], F32), sb("c_mom", [T, G4, 2], F32), sb("c_rstd", [T, G4], F32)
        g_ps = [psum(f"c_g{i}", [P, 512]) for i in range(2)]
        y_ps = [psum(f"c_y{i}", [P, 512]) for i in range(2)]
        o_ps = [psum(f"c_o{i}", [P, 512]) for i in range(2)]
        yb_done, gw_done, g_ready, y_ready, gw_t_done, y_n_done, o_ready, z_done = (
            sem(f"c_{n}") for n in ("yb_done", "gw_done", "g_ready", "y_ready", "gw_t_done", "y_n_done", "o_ready", "z_done"))
        stats_done, mom_done, eps_done, rstd_done, rows_done = (
            sem(f"c_{n}") for n in ("stats_done", "mom_done", "eps_done", "rstd_done", "rows_done"))
        stored = [sem(f"c_stored{i}") for i in range(2)]
        block = stack.enter_context(nc.Block())

        def is_first(g):
            return isinstance(g, int) and g == 0

        def is_last(g):
            return isinstance(g, int) and g == NG - 1

        def groups(eng, body):
            body(0, 0, 0)
            body(1, 1, 0)
            with eng.Fori(1, NG // 2 - 1) as i:
                for par in range(2):
                    body(2 * i + par, par, i)
            for par in range(2):
                body(NG - 2 + par, par, NG // 2 - 1)

        @block.gpsimd
        def _(pool):
            def row_scale(g):
                settle(pool, passed, (mom_done, g + 1))
                pool.tensor_scalar(rstd[:, :], mom[:, :, 1], EPS, None, ALU.add).then_inc(eps_done, 1)
                pool.wait_ge(eps_done, g + 1)
                pool.tensor_tensor(rstd[:, :], rstd[:, :], half_neg[0:T, :], ALU.pow).then_inc(rstd_done, 1)

            def body(g, par, before):
                for q in range(G4):
                    b = G4 * g + q
                    settle(pool, passed, (y_ready, b + 1 - G4))
                    pool.tensor_copy(yb[:, q, :, :].rearrange("p k (e c) -> p k e c", c=CAP),
                                     y_t[:, :, :, bass.ds(b * CAP, CAP)]).then_inc(yb_done, 1)
                    if q == G4 - 1 and not is_first(g):
                        row_scale(g - 1)

            groups(pool, body)
            row_scale(NG - 1)

        @block.vector
        def _(dve):
            def weights(b, q):
                at_least(dve, g_ready, b - 1)
                dve.tensor_tensor(gw[:, q % 2, :].rearrange("p (e c) -> p e c", c=CAP),
                                  gather[:, bass.ds(b, 1), :].rearrange("p a (e c) -> p (a e) c", c=CAP),
                                  probs[:, bass.ds(b, 1), :].rearrange("p a e -> p (a e)").unsqueeze(2).to_broadcast([T, E, CAP]),
                                  ALU.mult).then_inc(gw_done, 1)

            def add_x(g, par, q, before):
                b = G4 * g + q
                if q == 0:
                    at_least(dve, stored[par], 16 * before)
                    at_least(dve, mom_done, g)
                dve.wait_ge(o_ready, b + 1)
                dve.tensor_tensor(z[:, par, q, :], o_ps[q % 2][0:T, 0:D],
                                  x_sb[:, bass.ds(b, 1), :].rearrange("p a d -> p (a d)"), ALU.add).then_inc(z_done, 1)
                dve.wait_ge(z_done, b + 1)
                dve.bn_stats(stats[:, q, :], z[:, par, q, :]).then_inc(stats_done, 1)

            def moments(g):
                settle(dve, passed, (stats_done, G4 * (g + 1)), (rows_done, g))
                for q in range(G4):
                    ins = dve.bn_aggr(mom[:, q, :], stats[:, q, :])
                ins.then_inc(mom_done, 1)

            def rows(g, par):
                dve.wait_ge(rstd_done, g + 1)
                for q in range(G4):
                    ins = dve.tensor_scalar(z[:, par, q, :], z[:, par, q, :], mom[:, q, 0:1], rstd[:, q:q + 1], ALU.subtract, ALU.mult)
                ins.then_inc(rows_done, 1)

            def body(g, par, before):
                for q in range(G4):
                    if not (is_last(g) and q == G4 - 1):
                        weights(G4 * g + q + 1, q + 1)
                    if q >= SUM_LAG:
                        add_x(g, par, q - SUM_LAG, before)
                    elif not is_first(g):
                        add_x(g - 1, 1 - par, q - SUM_LAG + G4, before)
                    if not is_first(g):
                        if q == SUM_LAG - 1:
                            moments(g - 1)
                        if q == G4 - 1:
                            rows(g - 1, 1 - par)

            weights(0, 0)
            groups(dve, body)
            for q in range(G4 - SUM_LAG, G4):
                add_x(NG - 1, 1, q, None)
            moments(NG - 1)
            rows(NG - 1, 1)

        @block.scalar
        def _(act):
            def body(g, par, before):
                for q in range(G4):
                    b = G4 * g + q
                    act.wait_ge(g_ready, b + 1)
                    at_least(act, o_ready, b - 1)
                    act.activation(gw_t[:, q % 2, :], g_ps[q % 2][0:HS, 0:2 * T], ACT.Identity).then_inc(gw_t_done, 1)
                    act.wait_ge(y_ready, b + 1)
                    act.activation(y_n[:, q % 2, :], y_ps[q % 2][0:HS, :], ACT.Identity).then_inc(y_n_done, 1)

            groups(act, body)

        @block.tensor
        def _(pe):
            def turn(b, q):
                pe.wait_ge(gw_done, b + 1)
                at_least(pe, gw_t_done, b - 1)
                for s in range(2):
                    mm = pe.transpose(g_ps[q % 2][0:HS, s * T:(s + 1) * T], gw[:, q % 2, s * HS:(s + 1) * HS], ident[0:T, 0:T])
                mm.then_inc(g_ready, 1)
                pe.wait_ge(yb_done, b + 1)
                at_least(pe, y_n_done, b - 1)
                for s in range(2):
                    for k in range(KD):
                        mm = pe.transpose(y_ps[q % 2][0:HS, s * D + k * P:s * D + (k + 1) * P],
                                          yb[:, q, k, s * HS:(s + 1) * HS], ident[:, :])
                mm.then_inc(y_ready, 1)

            def bring_back(b, q):
                pe.wait_ge(gw_t_done, b + 1)
                pe.wait_ge(y_n_done, b + 1)
                at_least(pe, z_done, b - 1)
                for s in range(2):
                    mm = pe.matmul(o_ps[q % 2][0:T, 0:D], gw_t[:, q % 2, s * T:(s + 1) * T], y_n[:, q % 2, s * D:(s + 1) * D],
                                   start=(s == 0), stop=(s == 1))
                mm.then_inc(o_ready, 1)

            def body(g, par, before):
                for q in range(G4):
                    turn(G4 * g + q, q)
                    if not (is_first(g) and q == 0):
                        bring_back(G4 * g + q - 1, (q - 1) % G4)

            groups(pe, body)
            bring_back(B - 1, G4 - 1)

        @block.sync
        def _(sp):
            def body(g, par, before):
                sp.wait_ge(rows_done, g + 1)
                sp.dma_start(out[bass.ds(G4 * g, G4), :, :].rearrange("b t d -> t b d"), z[:, par, :, :]).then_inc(stored[par], 16)

            groups(sp, body)
            for par in range(2):
                sp.wait_ge(stored[par], 16 * NG // 2)


_INS = ['x', 'ctx_1024', 'mask_BxS2_bf1', 'L0_attn_wq', 'L0_attn_wk', 'L0_attn_wv', 'L0_attn_wo', 'L0_attn_proj',
        'L0_attn_w1', 'L0_attn_b1', 'L0_attn_w2', 'L0_attn_b2', 'L0_attn_g1', 'L0_attn_beta1', 'L0_attn_g2',
        'L0_attn_beta2', 'L0_xattn_norm_w', 'L0_xattn_norm_b', 'L0_xattn_ctx_norm_w', 'L0_xattn_ctx_norm_b',
        'L0_xattn_Wq', 'L0_xattn_Wkv', 'L0_xattn_Wo', 'L0_ffn_Wr', 'L0_ffn_br', 'L0_ffn_W1', 'L0_ffn_b1',
        'L0_ffn_W2', 'L0_ffn_b2']


def kernel(**inputs):
    import numpy as _np
    import concourse.bacc as _bacc
    from concourse.bass_utils import run_bass_kernel_spmd as _run

    nc = _bacc.Bacc("TRN2", target_bir_lowering=False, num_devices=1)
    arrays, args = {}, {}
    for name in _INS:
        a = _np.ascontiguousarray(inputs[name])
        if a.dtype == _np.bool_:
            a = a.view(_np.uint8)
        arrays[f"in_{name}_dram"] = a
        args[name] = nc.dram_tensor(f"in_{name}_dram", a.shape, mybir.dt.from_np(a.dtype), kind="ExternalInput").ap()
    out = nc.dram_tensor("out_dram", (B, T, D), F32, kind="ExternalOutput").ap()
    decoder_kernel(nc, args, out)
    r = _run(nc, [arrays], core_ids=[0])
    return r.results[0]["out_dram"]
```
